# Optimizing a Trainium2 kernel written in Bass

```python
import numpy as np
import jax
import jax.numpy as jnp

def _softmax(x, axis=-1):
    return jax.nn.softmax(x, axis=axis)

def _gelu(x):
    return jax.nn.gelu(x, approximate=True)

def _silu(x):
    return jax.nn.silu(x)

def _sigmoid(x):
    return jax.nn.sigmoid(x)

def _layernorm(x, axis=-1, eps=1e-05):
    m = jnp.mean(x, axis=axis, keepdims=True)
    v = jnp.var(x, axis=axis, keepdims=True)
    return (x - m) / jnp.sqrt(v + eps)

def _scatter_add(tgt, idx, src, axis=0):
    return tgt.at[idx].add(src)

def _segment_sum(src, seg, n):
    return jax.ops.segment_sum(src, seg, n)
kernel_name = 'mk_perceiver_d4_seqx_r4_4b2e55'

def setup_inputs(seed: int=0):
    np.random.seed(seed)
    _w = jnp.asarray

    def _rec_inputs():
        import jax
        import jax.numpy as jnp
        _rk = jax.random.key(seed)
        x = -0.0005146 + 1 * jax.random.normal(jax.random.fold_in(_rk, 1), (32, 32, 256), jnp.float32)
        _lenS = 32 - jax.random.randint(jax.random.fold_in(_rk, 7), (32,), 0, max(1, 32 // 4) + 1, jnp.int32)
        _lenS2 = 257 - jax.random.randint(jax.random.fold_in(_rk, 8), (32,), 0, max(1, 257 // 4) + 1, jnp.int32)
        _ctx_768P = jax.random.normal(jax.random.fold_in(_rk, 11), (32, 16, 192), jnp.float32)
        _ctx_768c = jax.random.dirichlet(jax.random.fold_in(_rk, 511), 0.3 * jnp.ones((16,), jnp.float32), (32, 257))
        _ctx_768t = jnp.einsum('bsk,bkd->bsd', _ctx_768c, _ctx_768P)
        _ctx_768t = _ctx_768t * jax.lax.rsqrt(jnp.mean(jnp.square(_ctx_768t)) + 1e-12) * 0.953939
        ctx_768 = -0.00040386 + 0.999972 * (_ctx_768t + 0.3 * jax.random.normal(jax.random.fold_in(_rk, 611), (32, 257, 192), jnp.float32))
        _validS = jnp.arange(32)[None, :] < _lenS[:, None]
        _validS2 = jnp.arange(257)[None, :] < _lenS2[:, None]
        _causal = jnp.tril(jnp.ones((32, 32), dtype=bool))
        mask_BxS2_bk0 = jnp.logical_not(jnp.broadcast_to(_validS2[:, :], (32, 257)))
        mask_BxS_bf1 = jnp.ones((32, 32), dtype=bool)
        mask_BxS2_bf1 = jnp.ones((32, 257), dtype=bool)
        return (x, ctx_768, mask_BxS2_bk0, mask_BxS_bf1, mask_BxS2_bf1)
    x, ctx_768, mask_BxS2_bk0, mask_BxS_bf1, mask_BxS2_bf1 = _rec_inputs()

    def _L0_xattn_setup():
        import jax, jax.numpy as jnp
        import numpy as np
        DIM_IN, DIM_LAT, DIM_HEAD = (192, 256, 64)
        INNER = max(DIM_LAT, DIM_IN)
        HEADS = INNER // DIM_HEAD
        SCALE = DIM_HEAD ** (-0.5)
        RMS_EPS = 1e-08
        LN_EPS = 1e-05

        def layernorm(x, g, b):
            mu = jnp.mean(x, axis=-1, keepdims=True)
            var = jnp.mean((x - mu) ** 2, axis=-1, keepdims=True)
            return (x - mu) * jax.lax.rsqrt(var + LN_EPS) * g + b

        def rmsnorm(x, gamma):
            norm = jnp.sqrt(jnp.sum(x * x, axis=-1, keepdims=True)) * x.shape[-1] ** (-0.5)
            return x / jnp.maximum(norm, RMS_EPS) * gamma
        key = jax.random.key(seed)
        ks = jax.random.split(key, 12)
        b, n, m = (4, 1024, 128)
        x = jax.random.normal(ks[0], (b, n, DIM_IN), jnp.float32)
        latents = jax.random.normal(ks[1], (b, m, DIM_LAT), jnp.float32)
        mask = jax.random.randint(ks[2], (b, n), 0, 2).astype(bool)
        s = lambda k, sh, fan: jax.random.normal(k, sh, jnp.float32) * fan ** (-0.5)
        return {'x': x, 'latents': latents, 'mask': mask, 'ln_x_g': jnp.ones((DIM_IN,), jnp.float32), 'ln_x_b': jnp.zeros((DIM_IN,), jnp.float32), 'ln_l_g': jnp.ones((DIM_LAT,), jnp.float32), 'ln_l_b': jnp.zeros((DIM_LAT,), jnp.float32), 'qn_g': jnp.ones((DIM_HEAD,), jnp.float32), 'kn_g': jnp.ones((DIM_HEAD,), jnp.float32), 'Wq': s(ks[3], (INNER, DIM_LAT), DIM_LAT), 'Wkv': s(ks[4], (2 * INNER, DIM_IN), DIM_IN), 'Wlkv': s(ks[5], (2 * INNER, DIM_LAT), DIM_LAT), 'Wo': s(ks[6], (DIM_LAT, INNER), INNER), 'bo': jnp.zeros((DIM_LAT,), jnp.float32)}
    _L0_xattn_all = _L0_xattn_setup()
    _L0_xattn_in = {k: v for k, v in _L0_xattn_all.items() if k in ('ln_x_g', 'ln_x_b', 'ln_l_g', 'ln_l_b', 'qn_g', 'kn_g', 'Wq', 'Wkv', 'Wlkv', 'Wo', 'bo')}
    del _L0_xattn_all

    def _L0_attn_setup():
        import jax, jax.numpy as jnp
        import numpy as np
        import math
        D_K = 64
        key = jax.random.key(seed)
        ks = jax.random.split(key, 5)
        b, m, d, h, dk, dv = (8, 256, 256, 16, 64, 64)
        return {'x': jax.random.normal(ks[0], (b, m, d), dtype=jnp.float32), 'P_q': jax.random.normal(ks[1], (h, d, dk), dtype=jnp.float32) * 0.02, 'P_k': jax.random.normal(ks[2], (h, d, dk), dtype=jnp.float32) * 0.02, 'P_v': jax.random.normal(ks[3], (h, d, dv), dtype=jnp.float32) * 0.02, 'P_o': jax.random.normal(ks[4], (h, d, dv), dtype=jnp.float32) * 0.02}
    _L0_attn_all = _L0_attn_setup()
    _L0_attn_in = {k: v for k, v in _L0_attn_all.items() if k in ('P_q', 'P_k', 'P_v', 'P_o')}
    del _L0_attn_all

    def _L0_ffn_setup():
        import jax, jax.numpy as jnp
        import numpy as np
        H = 256
        DFF = 1024
        E = 8
        B = 8
        S = 128
        INIT_LAMBDA = 0.2
        key = jax.random.key(seed)
        ks = jax.random.split(key, 9)
        hidden_states = jax.random.normal(ks[0], (S, B, H), dtype=jnp.float32)
        gW1 = 0.01 * jax.random.normal(ks[1], (H, H), dtype=jnp.float32)
        gb1 = jnp.zeros((H,), dtype=jnp.float32)
        gW2 = 0.01 * jax.random.normal(ks[2], (E, H), dtype=jnp.float32)
        gb2 = jnp.full((E,), INIT_LAMBDA, dtype=jnp.float32)
        sc1 = 1.0 / np.sqrt(H)
        sc2 = 1.0 / np.sqrt(DFF)
        eW1 = sc1 * jax.random.normal(ks[3], (E, DFF, H), dtype=jnp.float32)
        eb1 = sc1 * jax.random.normal(ks[4], (E, DFF), dtype=jnp.float32)
        eW2 = sc2 * jax.random.normal(ks[5], (E, H, DFF), dtype=jnp.float32)
        eb2 = sc2 * jax.random.normal(ks[6], (E, H), dtype=jnp.float32)
        return {'hidden_states': hidden_states, 'gW1': gW1, 'gb1': gb1, 'gW2': gW2, 'gb2': gb2, 'eW1': eW1, 'eb1': eb1, 'eW2': eW2, 'eb2': eb2}
    _L0_ffn_all = _L0_ffn_setup()
    _L0_ffn_in = {k: v for k, v in _L0_ffn_all.items() if k in ('gW1', 'gb1', 'gW2', 'gb2', 'eW1', 'eb1', 'eW2', 'eb2')}
    del _L0_ffn_all

    def _L1_xattn_setup():
        import jax, jax.numpy as jnp
        import numpy as np
        B, T, DT, G, DV = (16, 128, 256, 144, 192)
        H, DH = (4, 32)
        INNER = H * DH
        HID = 4 * DT
        N_STATE = 64
        K_TOP = 32

        def layernorm(x, g, b, eps=1e-05):
            m = x.mean(-1, keepdims=True)
            v = x.var(-1, keepdims=True)
            return (x - m) * jax.lax.rsqrt(v + eps) * g + b

        def s4d(x, log_dt, A_re, A_im, C_re, C_im, D_skip):
            Bb, L, D = x.shape
            dt = jnp.exp(log_dt)
            A = A_re + 1j * A_im
            C = C_re + 1j * C_im
            dtA = dt[:, None] * A
            dC = C * (jnp.exp(dtA) - 1.0) / A
            powers = jnp.exp(dtA[:, :, None] * jnp.arange(L))
            K = 2.0 * jnp.einsum('dn,dnl->dl', dC, powers).real
            n = 2 * L
            Kf = jnp.fft.rfft(K, n=n, axis=-1)
            xf = jnp.fft.rfft(x, n=n, axis=1)
            y = jnp.fft.irfft(xf * Kf.T[None], n=n, axis=1)[:, :L]
            return y + x * D_skip
        key = jax.random.key(seed)
        ks = jax.random.split(key, 16)
        s = 0.02
        inp = {'x_text': jax.random.normal(ks[0], (B, T, DT), jnp.float32), 'x_vision': jax.random.normal(ks[1], (B, G, DV), jnp.float32), 'text_mask': jnp.ones((B, T), bool), 'vision_mask': jnp.ones((B, G), bool), 'Wq': jax.random.normal(ks[2], (DT, INNER), jnp.float32) * s, 'Wk': jax.random.normal(ks[3], (DV, INNER), jnp.float32) * s, 'Wv': jax.random.normal(ks[4], (DV, DT), jnp.float32) * s, 'W_film_in': jax.random.normal(ks[5], (DT, 2 * DT), jnp.float32) * s, 'b_film_in': jnp.zeros((2 * DT,), jnp.float32), 'W_film_out': jax.random.normal(ks[6], (DT, 2 * DT), jnp.float32) * s, 'b_film_out': jnp.zeros((2 * DT,), jnp.float32), 'g_norm_in': jnp.ones((DT,), jnp.float32), 'b_norm_in': jnp.zeros((DT,), jnp.float32), 'g_norm_out': jnp.ones((DT,), jnp.float32), 'b_norm_out': jnp.zeros((DT,), jnp.float32), 'g_ffn': jnp.ones((DT,), jnp.float32), 'b_ffn': jnp.zeros((DT,), jnp.float32), 'W1': jax.random.normal(ks[7], (DT, HID), jnp.float32) * s, 'b1': jnp.zeros((HID,), jnp.float32), 'W2': jax.random.normal(ks[8], (HID, DT), jnp.float32) * s, 'b2': jnp.zeros((DT,), jnp.float32), 'log_dt': jnp.log(0.001) + jax.random.uniform(ks[9], (DT,), jnp.float32) * (jnp.log(0.1) - jnp.log(0.001)), 'A_re': -0.5 * jnp.ones((DT, N_STATE), jnp.float32), 'A_im': jnp.tile(jnp.pi * jnp.arange(N_STATE, dtype=jnp.float32), (DT, 1)), 'C_re': jax.random.normal(ks[10], (DT, N_STATE), jnp.float32) * 0.5 ** 0.5, 'C_im': jax.random.normal(ks[11], (DT, N_STATE), jnp.float32) * 0.5 ** 0.5, 'D_skip': jax.random.normal(ks[12], (DT,), jnp.float32), 'mod_gate': jnp.array(0.5, jnp.float32)}
        return inp
    _L1_xattn_all = _L1_xattn_setup()
    _L1_xattn_in = {k: v for k, v in _L1_xattn_all.items() if k in ('Wq', 'Wk', 'Wv', 'W_film_in', 'b_film_in', 'W_film_out', 'b_film_out', 'g_norm_in', 'b_norm_in', 'g_norm_out', 'b_norm_out', 'g_ffn', 'b_ffn', 'W1', 'b1', 'W2', 'b2', 'log_dt', 'A_re', 'A_im', 'C_re', 'C_im', 'D_skip', 'mod_gate')}
    del _L1_xattn_all

    def _L1_attn_setup():
        import jax, jax.numpy as jnp
        import numpy as np
        EPS = 1e-05

        def exp_map_at_origin(v, c):
            sqrt_c = jnp.sqrt(c)
            v_norm = jnp.maximum(jnp.linalg.norm(v, axis=-1, keepdims=True), EPS)
            return 1.0 / sqrt_c * jnp.tanh(sqrt_c * v_norm) * (v / v_norm)

        def log_map_at_origin(y, c):
            sqrt_c = jnp.sqrt(c)
            y_norm = jnp.maximum(jnp.linalg.norm(y, axis=-1, keepdims=True), EPS)
            y_norm_clamped = jnp.minimum(y_norm, 1.0 / sqrt_c - EPS)
            return 1.0 / sqrt_c * jnp.arctanh(sqrt_c * y_norm_clamped) * (y / y_norm)

        def poincare_distance(x, y, c):
            sqrt_c = jnp.sqrt(c)
            xns = jnp.sum(x * x, axis=-1, keepdims=True)
            yns = jnp.sum(y * y, axis=-1, keepdims=True)
            xy = jnp.einsum('bhsd,bhtd->bhst', x, y)
            xnsb = xns
            ynsb = jnp.swapaxes(yns, -2, -1)
            diff_norm_sq = xnsb - 2.0 * xy + ynsb
            denom = jnp.maximum((1.0 - c * xnsb) * (1.0 - c * ynsb), EPS)
            arg = jnp.maximum(1.0 + 2.0 * c * diff_norm_sq / denom, 1.0 + EPS)
            return 1.0 / sqrt_c * jnp.arccosh(arg)
        key = jax.random.key(seed)
        ks = jax.random.split(key, 5)
        B, S, D = (2, 256, 256)
        x = jax.random.normal(ks[0], (B, S, D), dtype=jnp.float32)
        scale = 0.02
        W_q = scale * jax.random.normal(ks[1], (D, D), dtype=jnp.float32)
        W_k = scale * jax.random.normal(ks[2], (D, D), dtype=jnp.float32)
        W_v = scale * jax.random.normal(ks[3], (D, D), dtype=jnp.float32)
        W_o = scale * jax.random.normal(ks[4], (D, D), dtype=jnp.float32)
        return {'x': x, 'W_q': W_q, 'W_k': W_k, 'W_v': W_v, 'W_o': W_o, 'log_c': jnp.zeros((), jnp.float32), 'beta': jnp.zeros((), jnp.float32), 'attention_bias': jnp.zeros((), jnp.float32)}
    _L1_attn_all = _L1_attn_setup()
    _L1_attn_in = {k: v for k, v in _L1_attn_all.items() if k in ('W_q', 'W_k', 'W_v', 'W_o', 'log_c', 'beta', 'attention_bias')}
    del _L1_attn_all

    def _L1_ffn_setup():
        import jax, jax.numpy as jnp
        import numpy as np
        D, F, E, K = (256, 688, 8, 2)
        key = jax.random.key(seed)
        k0, k1, k2, k3, k4 = jax.random.split(key, 5)
        s = 0.02
        x = jax.random.normal(k0, (2, 128, D), jnp.float32)
        Ws = jax.random.normal(k1, (D, E), jnp.float32) * s
        bs = jnp.zeros((E,), jnp.float32)
        Wg = jax.random.normal(k2, (E, D, F), jnp.float32) * s
        Wu = jax.random.normal(k3, (E, D, F), jnp.float32) * s
        Wd = jax.random.normal(k4, (E, F, D), jnp.float32) * s
        return {'x': x, 'Ws': Ws, 'bs': bs, 'Wg': Wg, 'Wu': Wu, 'Wd': Wd}
    _L1_ffn_all = _L1_ffn_setup()
    _L1_ffn_in = {k: v for k, v in _L1_ffn_all.items() if k in ('Ws', 'bs', 'Wg', 'Wu', 'Wd')}
    del _L1_ffn_all

    def _L2_xattn_setup():
        import jax, jax.numpy as jnp
        import numpy as np
        B, N, M = (8, 1024, 77)
        Q_DIM, CTX_DIM = (256, 192)
        H, D = (16, 64)
        INNER = H * D
        key = jax.random.key(seed)
        ks = jax.random.split(key, 7)
        x = jax.random.normal(ks[0], (B, N, Q_DIM), dtype=jnp.float32)
        context = jax.random.normal(ks[1], (B, M, CTX_DIM), dtype=jnp.float32)
        Wq = jax.random.normal(ks[2], (Q_DIM, INNER), dtype=jnp.float32) * Q_DIM ** (-0.5)
        Wk = jax.random.normal(ks[3], (CTX_DIM, INNER), dtype=jnp.float32) * CTX_DIM ** (-0.5)
        Wv = jax.random.normal(ks[4], (CTX_DIM, INNER), dtype=jnp.float32) * CTX_DIM ** (-0.5)
        Wo = jax.random.normal(ks[5], (INNER, Q_DIM), dtype=jnp.float32) * INNER ** (-0.5)
        bo = jax.random.normal(ks[6], (Q_DIM,), dtype=jnp.float32) * 0.01
        return {'x': x, 'context': context, 'Wq': Wq, 'Wk': Wk, 'Wv': Wv, 'Wo': Wo, 'bo': bo}
    _L2_xattn_all = _L2_xattn_setup()
    _L2_xattn_in = {k: v for k, v in _L2_xattn_all.items() if k in ('Wq', 'Wk', 'Wv', 'Wo', 'bo')}
    del _L2_xattn_all

    def _L2_attn_setup():
        import jax, jax.numpy as jnp
        import numpy as np
        import math
        B, S, D = (4, 2048, 256)
        CHUNK = 64

        def _forward(x, Wk, bk, Wv, bv, Wq, bq, Wkp, bkp, Wqp, bqp, phase_scale, ln_g, ln_b, Wo, bo):
            b, s, d = x.shape
            key = x @ Wk + bk
            value = x @ Wv + bv
            query = x @ Wq + bq
            key_phase = jnp.tanh(key @ Wkp + bkp) * phase_scale
            query_phase = jnp.tanh(query @ Wqp + bqp) * phase_scale
            bound_real = value * jnp.cos(key_phase)
            bound_imag = value * jnpp_sin((bound := None)) if False else value * jnp.sin(key_phase)
            pad = -s % CHUNK
            if pad:
                bound_real = jnp.pad(bound_real, ((0, 0), (0, pad), (0, 0)))
                bound_imag = jnp.pad(bound_imag, ((0, 0), (0, pad), (0, 0)))
                query_phase = jnp.pad(query_phase, ((0, 0), (0, pad), (0, 0)))
            nc = (s + pad) // CHUNK
            br = bound_real.reshape(b, nc, CHUNK, d)
            bi = bound_imag.reshape(b, nc, CHUNK, d)
            qp = query_phase.reshape(b, nc, CHUNK, d)
            mem_real = jnp.cumsum(br, axis=2)
            mem_imag = jnp.cumsum(bi, axis=2)
            retrieved = mem_real * jnp.cos(qp) + mem_imag * jnp.sin(qp)
            retrieved = retrieved.reshape(b, s + pad, d)[:, :s]
            retrieved = retrieved / math.sqrt(d)
            mu = jnp.mean(retrieved, axis=-1, keepdims=True)
            var = jnp.mean(jnp.square(retrieved - mu), axis=-1, keepdims=True)
            normed = (retrieved - mu) * jax.lax.rsqrt(var + 1e-05) * ln_g + ln_b
            out = normed @ Wo + bo
            return x + out
        key = jax.random.key(seed)
        ks = jax.random.split(key, 8)
        w = 0.02
        inp = {'x': jax.random.normal(ks[0], (B, S, D), jnp.float32), 'Wk': jax.random.normal(ks[1], (D, D), jnp.float32) * w, 'bk': jnp.zeros((D,), jnp.float32), 'Wv': jax.random.normal(ks[2], (D, D), jnp.float32) * w, 'bv': jnp.zeros((D,), jnp.float32), 'Wq': jax.random.normal(ks[3], (D, D), jnp.float32) * w, 'bq': jnp.zeros((D,), jnp.float32), 'Wkp': jax.random.normal(ks[4], (D, D), jnp.float32) * w, 'bkp': jnp.zeros((D,), jnp.float32), 'Wqp': jax.random.normal(ks[5], (D, D), jnp.float32) * w, 'bqp': jnp.zeros((D,), jnp.float32), 'phase_scale': jnp.ones((D,), jnp.float32) * math.pi, 'ln_g': jnp.ones((D,), jnp.float32), 'ln_b': jnp.zeros((D,), jnp.float32), 'Wo': jax.random.normal(ks[6], (D, D), jnp.float32) * w, 'bo': jnp.zeros((D,), jnp.float32)}
        return inp
    _L2_attn_all = _L2_attn_setup()
    _L2_attn_in = {k: v for k, v in _L2_attn_all.items() if k in ('Wk', 'bk', 'Wv', 'bv', 'Wq', 'bq', 'Wkp', 'bkp', 'Wqp', 'bqp', 'phase_scale', 'ln_g', 'ln_b', 'Wo', 'bo')}
    del _L2_attn_all

    def _L2_ffn_setup():
        import jax, jax.numpy as jnp
        import numpy as np
        FP8_MAX = 448.0

        def quant_fp8(x):
            amax = jnp.max(jnp.abs(x)).astype(jnp.float32)
            scale = jnp.minimum(FP8_MAX / jnp.maximum(amax, 1e-12), FP8_MAX)
            x_fp8 = jnp.clip(x * scale, -FP8_MAX, FP8_MAX).astype(jnp.float8_e4m3fn)
            return (x_fp8, 1.0 / scale)
        key = jax.random.key(seed)
        k1, k2, k3 = jax.random.split(key, 3)
        B, S, IN, OUT = (4, 2048, 256, 256)
        input = jax.random.normal(k1, (B, S, IN), dtype=jnp.float32)
        bound = 1.0 / np.sqrt(IN)
        weight = jax.random.uniform(k2, (OUT, IN), dtype=jnp.float32, minval=-bound, maxval=bound)
        bias = jax.random.uniform(k3, (OUT,), dtype=jnp.float32, minval=-bound, maxval=bound)
        return {'input': input, 'weight': weight, 'bias': bias}
    _L2_ffn_all = _L2_ffn_setup()
    _L2_ffn_in = {k: v for k, v in _L2_ffn_all.items() if k in ('weight', 'bias')}
    del _L2_ffn_all

    def _L3_xattn_setup():
        import jax, jax.numpy as jnp
        import numpy as np
        QUERY_DIM = 256
        KEY_DIM = 192
        NUM_HEADS = 16
        HEAD_DIM = QUERY_DIM // NUM_HEADS
        SCALE = HEAD_DIM ** (-0.5)
        key = jax.random.key(seed)
        ks = jax.random.split(key, 11)
        B, Nq, Nk = (4, 1024, 256)
        s_q = QUERY_DIM ** (-0.5)
        s_k = KEY_DIM ** (-0.5)
        return {'query': jax.random.normal(ks[0], (B, Nq, QUERY_DIM), jnp.float32), 'key': jax.random.normal(ks[1], (B, Nk, KEY_DIM), jnp.float32), 'value': jax.random.normal(ks[2], (B, Nk, KEY_DIM), jnp.float32), 'Wq': jax.random.normal(ks[3], (QUERY_DIM, QUERY_DIM), jnp.float32) * s_q, 'bq': jnp.zeros((QUERY_DIM,), jnp.float32), 'Wk': jax.random.normal(ks[4], (KEY_DIM, QUERY_DIM), jnp.float32) * s_k, 'bk': jnp.zeros((QUERY_DIM,), jnp.float32), 'Wv': jax.random.normal(ks[5], (KEY_DIM, QUERY_DIM), jnp.float32) * s_k, 'bv': jnp.zeros((QUERY_DIM,), jnp.float32), 'Wo': jax.random.normal(ks[6], (QUERY_DIM, QUERY_DIM), jnp.float32) * s_q, 'bo': jnp.zeros((QUERY_DIM,), jnp.float32)}
    _L3_xattn_all = _L3_xattn_setup()
    _L3_xattn_in = {k: v for k, v in _L3_xattn_all.items() if k in ('Wq', 'bq', 'Wk', 'bk', 'Wv', 'bv', 'Wo', 'bo')}
    del _L3_xattn_all

    def _L3_attn_setup():
        import jax, jax.numpy as jnp
        import numpy as np
        S, B, D, H, C = (256, 1, 256, 16, 64)
        DH = D // H

        def _xavier(key, shape):
            fan_in, fan_out = (shape[1], shape[0])
            a = float(np.sqrt(6.0 / (fan_in + fan_out)))
            return jax.random.uniform(key, shape, jnp.float32, -a, a)
        key = jax.random.key(seed)
        ks = jax.random.split(key, 7)
        x = jax.random.normal(ks[0], (S, B, D), jnp.float32)
        q_c = _xavier(ks[1], (C, D))
        beta = jnp.zeros((H,), jnp.float32)
        Wq = _xavier(ks[2], (D, D))
        bq = jnp.zeros((D,), jnp.float32)
        Wk = _xavier(ks[3], (D, D))
        bk = jnp.zeros((D,), jnp.float32)
        Wv = _xavier(ks[4], (D, D))
        bv = jnp.zeros((D,), jnp.float32)
        Wo = _xavier(ks[5], (D, D))
        bo = jnp.zeros((D,), jnp.float32)
        return {'x': x, 'q_c': q_c, 'beta': beta, 'Wq': Wq, 'bq': bq, 'Wk': Wk, 'bk': bk, 'Wv': Wv, 'bv': bv, 'Wo': Wo, 'bo': bo}
    _L3_attn_all = _L3_attn_setup()
    _L3_attn_in = {k: v for k, v in _L3_attn_all.items() if k in ('q_c', 'beta', 'Wq', 'bq', 'Wk', 'bk', 'Wv', 'bv', 'Wo', 'bo')}
    del _L3_attn_all

    def _L3_ffn_setup():
        import jax, jax.numpy as jnp
        import numpy as np
        BLOCK = 32
        W_BITS = 4
        ACT_BITS = 16

        def act_qdq(x):
            qmax = 2.0 ** (ACT_BITS - 1) - 1.0
            scale = jnp.maximum(jnp.max(jnp.abs(x)) / qmax, 1e-12)
            return jnp.clip(jnp.round(x / scale), -qmax - 1.0, qmax) * scale

        def fixed_qdq_u16(x):
            scale = 1.0 / 65536.0
            return jnp.clip(jnp.round(x / scale), 0.0, 65535.0) * scale

        def lpbq_dequant(w):
            O, I = w.shape
            qmax = 2.0 ** (W_BITS - 1) - 1.0
            wb = w.reshape(O, I // BLOCK, BLOCK)
            s = jnp.maximum(jnp.max(jnp.abs(wb), axis=-1, keepdims=True) / qmax, 1e-12)
            wq = jnp.clip(jnp.round(wb / s), -qmax - 1.0, qmax) * s
            return wq.reshape(O, I)
        key = jax.random.key(seed)
        k1, k2, k3, k4 = jax.random.split(key, 4)
        B, S, H, I = (2, 1024, 256, 768)
        x = jax.random.normal(k1, (B, S, H), jnp.float32)
        w_gate = jax.random.normal(k2, (I, H), jnp.float32) * 0.02
        w_up = jax.random.normal(k3, (I, H), jnp.float32) * 0.02
        w_down = jax.random.normal(k4, (H, I), jnp.float32) * 0.02
        return {'x': x, 'w_gate': w_gate, 'w_up': w_up, 'w_down': w_down}
    _L3_ffn_all = _L3_ffn_setup()
    _L3_ffn_in = {k: v for k, v in _L3_ffn_all.items() if k in ('w_gate', 'w_up', 'w_down')}
    del _L3_ffn_all
    return {'x': x, 'ctx_768': ctx_768, 'mask_BxS2_bk0': mask_BxS2_bk0, 'mask_BxS_bf1': mask_BxS_bf1, 'mask_BxS2_bf1': mask_BxS2_bf1, 'L0_xattn_ln_x_g': _L0_xattn_in['ln_x_g'], 'L0_xattn_ln_x_b': _L0_xattn_in['ln_x_b'], 'L0_xattn_ln_l_g': _L0_xattn_in['ln_l_g'], 'L0_xattn_ln_l_b': _L0_xattn_in['ln_l_b'], 'L0_xattn_qn_g': _L0_xattn_in['qn_g'], 'L0_xattn_kn_g': _L0_xattn_in['kn_g'], 'L0_xattn_Wq': _L0_xattn_in['Wq'], 'L0_xattn_Wkv': _L0_xattn_in['Wkv'], 'L0_xattn_Wlkv': _L0_xattn_in['Wlkv'], 'L0_xattn_Wo': _L0_xattn_in['Wo'], 'L0_xattn_bo': _L0_xattn_in['bo'], 'L0_attn_P_q': _L0_attn_in['P_q'], 'L0_attn_P_k': _L0_attn_in['P_k'], 'L0_attn_P_v': _L0_attn_in['P_v'], 'L0_attn_P_o': _L0_attn_in['P_o'], 'L0_ffn_gW1': _L0_ffn_in['gW1'], 'L0_ffn_gb1': _L0_ffn_in['gb1'], 'L0_ffn_gW2': _L0_ffn_in['gW2'], 'L0_ffn_gb2': _L0_ffn_in['gb2'], 'L0_ffn_eW1': _L0_ffn_in['eW1'], 'L0_ffn_eb1': _L0_ffn_in['eb1'], 'L0_ffn_eW2': _L0_ffn_in['eW2'], 'L0_ffn_eb2': _L0_ffn_in['eb2'], 'L1_xattn_Wq': _L1_xattn_in['Wq'], 'L1_xattn_Wk': _L1_xattn_in['Wk'], 'L1_xattn_Wv': _L1_xattn_in['Wv'], 'L1_xattn_W_film_in': _L1_xattn_in['W_film_in'], 'L1_xattn_b_film_in': _L1_xattn_in['b_film_in'], 'L1_xattn_W_film_out': _L1_xattn_in['W_film_out'], 'L1_xattn_b_film_out': _L1_xattn_in['b_film_out'], 'L1_xattn_g_norm_in': _L1_xattn_in['g_norm_in'], 'L1_xattn_b_norm_in': _L1_xattn_in['b_norm_in'], 'L1_xattn_g_norm_out': _L1_xattn_in['g_norm_out'], 'L1_xattn_b_norm_out': _L1_xattn_in['b_norm_out'], 'L1_xattn_g_ffn': _L1_xattn_in['g_ffn'], 'L1_xattn_b_ffn': _L1_xattn_in['b_ffn'], 'L1_xattn_W1': _L1_xattn_in['W1'], 'L1_xattn_b1': _L1_xattn_in['b1'], 'L1_xattn_W2': _L1_xattn_in['W2'], 'L1_xattn_b2': _L1_xattn_in['b2'], 'L1_xattn_log_dt': _L1_xattn_in['log_dt'], 'L1_xattn_A_re': _L1_xattn_in['A_re'], 'L1_xattn_A_im': _L1_xattn_in['A_im'], 'L1_xattn_C_re': _L1_xattn_in['C_re'], 'L1_xattn_C_im': _L1_xattn_in['C_im'], 'L1_xattn_D_skip': _L1_xattn_in['D_skip'], 'L1_xattn_mod_gate': _L1_xattn_in['mod_gate'], 'L1_attn_W_q': _L1_attn_in['W_q'], 'L1_attn_W_k': _L1_attn_in['W_k'], 'L1_attn_W_v': _L1_attn_in['W_v'], 'L1_attn_W_o': _L1_attn_in['W_o'], 'L1_attn_log_c': _L1_attn_in['log_c'], 'L1_attn_beta': _L1_attn_in['beta'], 'L1_attn_attention_bias': _L1_attn_in['attention_bias'], 'L1_ffn_Ws': _L1_ffn_in['Ws'], 'L1_ffn_bs': _L1_ffn_in['bs'], 'L1_ffn_Wg': _L1_ffn_in['Wg'], 'L1_ffn_Wu': _L1_ffn_in['Wu'], 'L1_ffn_Wd': _L1_ffn_in['Wd'], 'L2_xattn_Wq': _L2_xattn_in['Wq'], 'L2_xattn_Wk': _L2_xattn_in['Wk'], 'L2_xattn_Wv': _L2_xattn_in['Wv'], 'L2_xattn_Wo': _L2_xattn_in['Wo'], 'L2_xattn_bo': _L2_xattn_in['bo'], 'L2_attn_Wk': _L2_attn_in['Wk'], 'L2_attn_bk': _L2_attn_in['bk'], 'L2_attn_Wv': _L2_attn_in['Wv'], 'L2_attn_bv': _L2_attn_in['bv'], 'L2_attn_Wq': _L2_attn_in['Wq'], 'L2_attn_bq': _L2_attn_in['bq'], 'L2_attn_Wkp': _L2_attn_in['Wkp'], 'L2_attn_bkp': _L2_attn_in['bkp'], 'L2_attn_Wqp': _L2_attn_in['Wqp'], 'L2_attn_bqp': _L2_attn_in['bqp'], 'L2_attn_phase_scale': _L2_attn_in['phase_scale'], 'L2_attn_ln_g': _L2_attn_in['ln_g'], 'L2_attn_ln_b': _L2_attn_in['ln_b'], 'L2_attn_Wo': _L2_attn_in['Wo'], 'L2_attn_bo': _L2_attn_in['bo'], 'L2_ffn_weight': _L2_ffn_in['weight'], 'L2_ffn_bias': _L2_ffn_in['bias'], 'L3_xattn_Wq': _L3_xattn_in['Wq'], 'L3_xattn_bq': _L3_xattn_in['bq'], 'L3_xattn_Wk': _L3_xattn_in['Wk'], 'L3_xattn_bk': _L3_xattn_in['bk'], 'L3_xattn_Wv': _L3_xattn_in['Wv'], 'L3_xattn_bv': _L3_xattn_in['bv'], 'L3_xattn_Wo': _L3_xattn_in['Wo'], 'L3_xattn_bo': _L3_xattn_in['bo'], 'L3_attn_q_c': _L3_attn_in['q_c'], 'L3_attn_beta': _L3_attn_in['beta'], 'L3_attn_Wq': _L3_attn_in['Wq'], 'L3_attn_bq': _L3_attn_in['bq'], 'L3_attn_Wk': _L3_attn_in['Wk'], 'L3_attn_bk': _L3_attn_in['bk'], 'L3_attn_Wv': _L3_attn_in['Wv'], 'L3_attn_bv': _L3_attn_in['bv'], 'L3_attn_Wo': _L3_attn_in['Wo'], 'L3_attn_bo': _L3_attn_in['bo'], 'L3_ffn_w_gate': _L3_ffn_in['w_gate'], 'L3_ffn_w_up': _L3_ffn_in['w_up'], 'L3_ffn_w_down': _L3_ffn_in['w_down']}

def reference(x, ctx_768, mask_BxS2_bk0, mask_BxS_bf1, mask_BxS2_bf1, L0_xattn_ln_x_g, L0_xattn_ln_x_b, L0_xattn_ln_l_g, L0_xattn_ln_l_b, L0_xattn_qn_g, L0_xattn_kn_g, L0_xattn_Wq, L0_xattn_Wkv, L0_xattn_Wlkv, L0_xattn_Wo, L0_xattn_bo, L0_attn_P_q, L0_attn_P_k, L0_attn_P_v, L0_attn_P_o, L0_ffn_gW1, L0_ffn_gb1, L0_ffn_gW2, L0_ffn_gb2, L0_ffn_eW1, L0_ffn_eb1, L0_ffn_eW2, L0_ffn_eb2, L1_xattn_Wq, L1_xattn_Wk, L1_xattn_Wv, L1_xattn_W_film_in, L1_xattn_b_film_in, L1_xattn_W_film_out, L1_xattn_b_film_out, L1_xattn_g_norm_in, L1_xattn_b_norm_in, L1_xattn_g_norm_out, L1_xattn_b_norm_out, L1_xattn_g_ffn, L1_xattn_b_ffn, L1_xattn_W1, L1_xattn_b1, L1_xattn_W2, L1_xattn_b2, L1_xattn_log_dt, L1_xattn_A_re, L1_xattn_A_im, L1_xattn_C_re, L1_xattn_C_im, L1_xattn_D_skip, L1_xattn_mod_gate, L1_attn_W_q, L1_attn_W_k, L1_attn_W_v, L1_attn_W_o, L1_attn_log_c, L1_attn_beta, L1_attn_attention_bias, L1_ffn_Ws, L1_ffn_bs, L1_ffn_Wg, L1_ffn_Wu, L1_ffn_Wd, L2_xattn_Wq, L2_xattn_Wk, L2_xattn_Wv, L2_xattn_Wo, L2_xattn_bo, L2_attn_Wk, L2_attn_bk, L2_attn_Wv, L2_attn_bv, L2_attn_Wq, L2_attn_bq, L2_attn_Wkp, L2_attn_bkp, L2_attn_Wqp, L2_attn_bqp, L2_attn_phase_scale, L2_attn_ln_g, L2_attn_ln_b, L2_attn_Wo, L2_attn_bo, L2_ffn_weight, L2_ffn_bias, L3_xattn_Wq, L3_xattn_bq, L3_xattn_Wk, L3_xattn_bk, L3_xattn_Wv, L3_xattn_bv, L3_xattn_Wo, L3_xattn_bo, L3_attn_q_c, L3_attn_beta, L3_attn_Wq, L3_attn_bq, L3_attn_Wk, L3_attn_bk, L3_attn_Wv, L3_attn_bv, L3_attn_Wo, L3_attn_bo, L3_ffn_w_gate, L3_ffn_w_up, L3_ffn_w_down):
    import jax
    import jax.numpy as jnp

    def _L0_xattn_ref(x, latents, mask, ln_x_g, ln_x_b, ln_l_g, ln_l_b, qn_g, kn_g, Wq, Wkv, Wlkv, Wo, bo):
        import jax, jax.numpy as jnp
        import numpy as np
        DIM_IN, DIM_LAT, DIM_HEAD = (192, 256, 64)
        INNER = max(DIM_LAT, DIM_IN)
        HEADS = INNER // DIM_HEAD
        SCALE = DIM_HEAD ** (-0.5)
        RMS_EPS = 1e-08
        LN_EPS = 1e-05

        def layernorm(x, g, b):
            mu = jnp.mean(x, axis=-1, keepdims=True)
            var = jnp.mean((x - mu) ** 2, axis=-1, keepdims=True)
            return (x - mu) * jax.lax.rsqrt(var + LN_EPS) * g + b

        def rmsnorm(x, gamma):
            norm = jnp.sqrt(jnp.sum(x * x, axis=-1, keepdims=True)) * x.shape[-1] ** (-0.5)
            return x / jnp.maximum(norm, RMS_EPS) * gamma
        b, n, _ = x.shape
        m = latents.shape[1]
        xn = layernorm(x, ln_x_g, ln_x_b)
        ln = layernorm(latents, ln_l_g, ln_l_b)
        q = ln @ Wq.T
        kv = jnp.concatenate([xn @ Wkv.T, ln @ Wlkv.T], axis=1)
        k, v = (kv[..., :INNER], kv[..., INNER:])
        split_heads = lambda t: t.reshape(t.shape[0], t.shape[1], HEADS, DIM_HEAD).transpose(0, 2, 1, 3)
        q, k, v = (split_heads(q), split_heads(k), split_heads(v))
        qn = rmsnorm(q, qn_g) * SCALE
        kn = rmsnorm(k, kn_g)
        attn = jnp.einsum('bhid,bhjd->bhij', qn, kn)
        full_mask = jnp.pad(mask, ((0, 0), (0, m)), constant_values=True)
        attn = jnp.where(full_mask[:, None, None, :], attn, -jnp.finfo(attn.dtype).max)
        attn = jax.nn.softmax(attn, axis=-1)
        out = jnp.einsum('bhij,bhjd->bhid', attn, v)
        out = out.transpose(0, 2, 1, 3).reshape(b, m, INNER)
        return out @ Wo.T + bo

    def _L0_attn_ref(x, P_q, P_k, P_v, P_o):
        import jax, jax.numpy as jnp
        import numpy as np
        import math
        D_K = 64
        m = x.shape[1]
        Q = jnp.einsum('bmd,hdk->bhmk', x, P_q)
        K = jnp.einsum('bmd,hdk->bhmk', x, P_k)
        V = jnp.einsum('bmd,hdv->bhmv', x, P_v)
        logits = jnp.einsum('bhmk,bhnk->bhmn', Q, K) * math.sqrt(D_K)
        causal = jnp.tril(jnp.ones((m, m), dtype=bool))
        logits = jnp.where(causal[None, None], logits, -jnp.inf)
        key_weights = jax.nn.softmax(logits, axis=-1)
        o = jnp.einsum('bhmm,bhmv->bhmv', key_weights, V)
        y = jnp.einsum('bhmv,hdv->bmd', o, P_o)
        return y

    def _L0_ffn_ref(hidden_states, gW1, gb1, gW2, gb2, eW1, eb1, eW2, eb2):
        import jax, jax.numpy as jnp
        import numpy as np
        H = 256
        DFF = 1024
        E = 8
        B = 8
        S = 128
        INIT_LAMBDA = 0.2
        x = jnp.transpose(hidden_states, (1, 0, 2))
        h = jax.nn.relu(jnp.einsum('bsh,oh->bso', x, gW1) + gb1)
        gate = jnp.einsum('bsh,eh->bse', h, gW2) + gb2
        g = gate.mean(axis=1)
        W1 = jnp.einsum('be,eoi->boi', g, eW1)
        b1 = g @ eb1
        W2 = jnp.einsum('be,eoi->boi', g, eW2)
        b2 = g @ eb2
        y = jax.nn.relu(jnp.einsum('bsi,boi->bso', x, W1) + b1[:, None, :])
        y = jnp.einsum('bsi,boi->bso', y, W2) + b2[:, None, :]
        return jnp.transpose(y, (1, 0, 2))

    def _L1_xattn_ref(x_text, x_vision, text_mask, vision_mask, Wq, Wk, Wv, W_film_in, b_film_in, W_film_out, b_film_out, g_norm_in, b_norm_in, g_norm_out, b_norm_out, g_ffn, b_ffn, W1, b1, W2, b2, log_dt, A_re, A_im, C_re, C_im, D_skip, mod_gate):
        import jax, jax.numpy as jnp
        import numpy as np
        B, T, DT, G, DV = (16, 128, 256, 144, 192)
        H, DH = (4, 32)
        INNER = H * DH
        HID = 4 * DT
        N_STATE = 64
        K_TOP = 32

        def layernorm(x, g, b, eps=1e-05):
            m = x.mean(-1, keepdims=True)
            v = x.var(-1, keepdims=True)
            return (x - m) * jax.lax.rsqrt(v + eps) * g + b

        def s4d(x, log_dt, A_re, A_im, C_re, C_im, D_skip):
            Bb, L, D = x.shape
            dt = jnp.exp(log_dt)
            A = A_re + 1j * A_im
            C = C_re + 1j * C_im
            dtA = dt[:, None] * A
            dC = C * (jnp.exp(dtA) - 1.0) / A
            powers = jnp.exp(dtA[:, :, None] * jnp.arange(L))
            K = 2.0 * jnp.einsum('dn,dnl->dl', dC, powers).real
            n = 2 * L
            Kf = jnp.fft.rfft(K, n=n, axis=-1)
            xf = jnp.fft.rfft(x, n=n, axis=1)
            y = jnp.fft.irfft(xf * Kf.T[None], n=n, axis=1)[:, :L]
            return y + x * D_skip
        Bb, Tt, D = x_text.shape
        Gg = x_vision.shape[1]
        Q = (x_text @ Wq).reshape(Bb, Tt, H, DH)
        K = (x_vision @ Wk).reshape(Bb, Gg, H, DH)
        scores = jnp.einsum('bthd,bghd->bhtg', Q, K) / np.sqrt(DH).astype(np.float32)
        scores = jnp.where(vision_mask[:, None, None, :], scores, -jnp.inf)
        topv, topi = jax.lax.top_k(scores, K_TOP)
        probs = jax.nn.softmax(topv, axis=-1)
        bi = jnp.arange(Bb)[:, None, None, None]
        hi = jnp.arange(H)[None, :, None, None]
        ti = jnp.arange(Tt)[None, None, :, None]
        attn = jnp.zeros_like(scores).at[bi, hi, ti, topi].set(probs)
        attn_mean = attn.mean(axis=1)
        V = x_vision @ Wv
        c_t = jnp.einsum('btg,bgd->btd', attn_mean, V)
        c_t = c_t * text_mask[..., None]
        x = layernorm(x_text, g_norm_in, b_norm_in)
        scale_in, shift_in = jnp.split(c_t @ W_film_in + b_film_in, 2, axis=-1)
        x = x * (1.0 + mod_gate * scale_in) + mod_gate * shift_in
        y = s4d(x, log_dt, A_re, A_im, C_re, C_im, D_skip)
        scale_out, shift_out = jnp.split(c_t @ W_film_out + b_film_out, 2, axis=-1)
        y = y * (1.0 + mod_gate * scale_out) + mod_gate * shift_out
        xt = x_text + y
        h = layernorm(xt, g_ffn, b_ffn)
        h = jax.nn.gelu(h @ W1 + b1, approximate=False) @ W2 + b2
        xt = xt + h
        return layernorm(xt, g_norm_out, b_norm_out)

    def _L1_attn_ref(x, W_q, W_k, W_v, W_o, log_c, beta, attention_bias):
        import jax, jax.numpy as jnp
        import numpy as np
        EPS = 1e-05

        def exp_map_at_origin(v, c):
            sqrt_c = jnp.sqrt(c)
            v_norm = jnp.maximum(jnp.linalg.norm(v, axis=-1, keepdims=True), EPS)
            return 1.0 / sqrt_c * jnp.tanh(sqrt_c * v_norm) * (v / v_norm)

        def log_map_at_origin(y, c):
            sqrt_c = jnp.sqrt(c)
            y_norm = jnp.maximum(jnp.linalg.norm(y, axis=-1, keepdims=True), EPS)
            y_norm_clamped = jnp.minimum(y_norm, 1.0 / sqrt_c - EPS)
            return 1.0 / sqrt_c * jnp.arctanh(sqrt_c * y_norm_clamped) * (y / y_norm)

        def poincare_distance(x, y, c):
            sqrt_c = jnp.sqrt(c)
            xns = jnp.sum(x * x, axis=-1, keepdims=True)
            yns = jnp.sum(y * y, axis=-1, keepdims=True)
            xy = jnp.einsum('bhsd,bhtd->bhst', x, y)
            xnsb = xns
            ynsb = jnp.swapaxes(yns, -2, -1)
            diff_norm_sq = xnsb - 2.0 * xy + ynsb
            denom = jnp.maximum((1.0 - c * xnsb) * (1.0 - c * ynsb), EPS)
            arg = jnp.maximum(1.0 + 2.0 * c * diff_norm_sq / denom, 1.0 + EPS)
            return 1.0 / sqrt_c * jnp.arccosh(arg)
        B, S, D = x.shape
        H = 16
        dh = D // H
        c = jax.nn.softplus(log_c)
        beta_pos = jax.nn.softplus(beta)

        def split_heads(t):
            return jnp.transpose(t.reshape(B, S, H, dh), (0, 2, 1, 3))
        q_t = split_heads(x @ W_q.T)
        k_t = split_heads(x @ W_k.T)
        v_t = split_heads(x @ W_v.T)
        q_h = exp_map_at_origin(q_t, c)
        k_h = exp_map_at_origin(k_t, c)
        v_h = exp_map_at_origin(v_t, c)
        dist = poincare_distance(q_h, k_h, c)
        scores = -beta_pos * dist - attention_bias
        weights = jax.nn.softmax(scores, axis=-1)
        v_tan = log_map_at_origin(v_h, c)
        out_tan = jnp.einsum('bhst,bhtd->bhsd', weights, v_tan)
        out_hyp = exp_map_at_origin(out_tan, c)
        out_heads_tan = log_map_at_origin(out_hyp, c)
        concat = jnp.transpose(out_heads_tan, (0, 2, 1, 3)).reshape(B, S, D)
        return concat @ W_o.T

    def _L1_ffn_ref(x, Ws, bs, Wg, Wu, Wd):
        import jax, jax.numpy as jnp
        import numpy as np
        D, F, E, K = (256, 688, 8, 2)
        b, n, d = x.shape
        xt = x.reshape(-1, d)
        logits = xt @ Ws + bs
        topk_w, topk_idx = jax.lax.top_k(logits, K)
        topk_w = jax.nn.softmax(topk_w, axis=-1)
        combine = jnp.sum(jax.nn.one_hot(topk_idx, E, dtype=xt.dtype) * topk_w[..., None], axis=1)
        g = jnp.einsum('td,edf->tef', xt, Wg)
        u = jnp.einsum('td,edf->tef', xt, Wu)
        h = jax.nn.silu(g) * u
        y = jnp.einsum('tef,efd->ted', h, Wd)
        out = jnp.einsum('ted,te->td', y, combine)
        return out.reshape(b, n, d)

    def _L2_xattn_ref(x, context, Wq, Wk, Wv, Wo, bo):
        import jax, jax.numpy as jnp
        import numpy as np
        B, N, M = (8, 1024, 77)
        Q_DIM, CTX_DIM = (256, 192)
        H, D = (16, 64)
        INNER = H * D
        scale = D ** (-0.5)

        def heads(t):
            b, s, _ = t.shape
            return t.reshape(b, s, H, D).transpose(0, 2, 1, 3)
        q = heads(x @ Wq)
        k = heads(context @ Wk)
        v = heads(context @ Wv)
        scores = jnp.einsum('bhid,bhjd->bhij', q, k) * scale
        attn = jax.nn.softmax(scores, axis=-1)
        out = jnp.einsum('bhij,bhjd->bhid', attn, v)
        out = out.transpose(0, 2, 1, 3).reshape(x.shape[0], x.shape[1], INNER)
        return out @ Wo + bo

    def _L2_attn_ref(x, Wk, bk, Wv, bv, Wq, bq, Wkp, bkp, Wqp, bqp, phase_scale, ln_g, ln_b, Wo, bo):
        import jax, jax.numpy as jnp
        import numpy as np
        import math
        B, S, D = (4, 2048, 256)
        CHUNK = 64

        def _forward(x, Wk, bk, Wv, bv, Wq, bq, Wkp, bkp, Wqp, bqp, phase_scale, ln_g, ln_b, Wo, bo):
            b, s, d = x.shape
            key = x @ Wk + bk
            value = x @ Wv + bv
            query = x @ Wq + bq
            key_phase = jnp.tanh(key @ Wkp + bkp) * phase_scale
            query_phase = jnp.tanh(query @ Wqp + bqp) * phase_scale
            bound_real = value * jnp.cos(key_phase)
            bound_imag = value * jnpp_sin((bound := None)) if False else value * jnp.sin(key_phase)
            pad = -s % CHUNK
            if pad:
                bound_real = jnp.pad(bound_real, ((0, 0), (0, pad), (0, 0)))
                bound_imag = jnp.pad(bound_imag, ((0, 0), (0, pad), (0, 0)))
                query_phase = jnp.pad(query_phase, ((0, 0), (0, pad), (0, 0)))
            nc = (s + pad) // CHUNK
            br = bound_real.reshape(b, nc, CHUNK, d)
            bi = bound_imag.reshape(b, nc, CHUNK, d)
            qp = query_phase.reshape(b, nc, CHUNK, d)
            mem_real = jnp.cumsum(br, axis=2)
            mem_imag = jnp.cumsum(bi, axis=2)
            retrieved = mem_real * jnp.cos(qp) + mem_imag * jnp.sin(qp)
            retrieved = retrieved.reshape(b, s + pad, d)[:, :s]
            retrieved = retrieved / math.sqrt(d)
            mu = jnp.mean(retrieved, axis=-1, keepdims=True)
            var = jnp.mean(jnp.square(retrieved - mu), axis=-1, keepdims=True)
            normed = (retrieved - mu) * jax.lax.rsqrt(var + 1e-05) * ln_g + ln_b
            out = normed @ Wo + bo
            return x + out
        return _forward(x, Wk, bk, Wv, bv, Wq, bq, Wkp, bkp, Wqp, bqp, phase_scale, ln_g, ln_b, Wo, bo)

    def _L2_ffn_ref(input, weight, bias):
        import jax, jax.numpy as jnp
        import numpy as np
        FP8_MAX = 448.0

        def quant_fp8(x):
            amax = jnp.max(jnp.abs(x)).astype(jnp.float32)
            scale = jnp.minimum(FP8_MAX / jnp.maximum(amax, 1e-12), FP8_MAX)
            x_fp8 = jnp.clip(x * scale, -FP8_MAX, FP8_MAX).astype(jnp.float8_e4m3fn)
            return (x_fp8, 1.0 / scale)
        prev_shape = input.shape
        x2d = input.reshape(-1, weight.shape[1])
        w_fp8, w_scale = quant_fp8(weight)
        x_fp8, x_scale = quant_fp8(x2d)
        acc = jnp.matmul(x_fp8.astype(jnp.float32), w_fp8.astype(jnp.float32).T)
        out2d = (acc * (x_scale * w_scale) + bias).astype(jnp.bfloat16)
        out = out2d.reshape(*prev_shape[:-1], weight.shape[0]).astype(input.dtype)
        return out

    def _L3_xattn_ref(query, key, value, Wq, bq, Wk, bk, Wv, bv, Wo, bo):
        import jax, jax.numpy as jnp
        import numpy as np
        QUERY_DIM = 256
        KEY_DIM = 192
        NUM_HEADS = 16
        HEAD_DIM = QUERY_DIM // NUM_HEADS
        SCALE = HEAD_DIM ** (-0.5)
        B, Nq, _ = query.shape
        Nk = key.shape[1]
        q = (query @ Wq + bq).reshape(B, Nq, NUM_HEADS, HEAD_DIM).transpose(0, 2, 1, 3)
        k = (key @ Wk + bk).reshape(B, Nk, NUM_HEADS, HEAD_DIM).transpose(0, 2, 1, 3)
        v = (value @ Wv + bv).reshape(B, Nk, NUM_HEADS, HEAD_DIM).transpose(0, 2, 1, 3)
        attn = jnp.einsum('bhqd,bhkd->bhqk', q, k) * SCALE
        attn = jax.nn.softmax(attn, axis=-1)
        out = jnp.einsum('bhqk,bhkd->bhqd', attn, v)
        out = out.transpose(0, 2, 1, 3).reshape(B, Nq, QUERY_DIM)
        return out @ Wo + bo

    def _L3_attn_ref(x, q_c, beta, Wq, bq, Wk, bk, Wv, bv, Wo, bo):
        import jax, jax.numpy as jnp
        import numpy as np
        S, B, D, H, C = (256, 1, 256, 16, 64)
        DH = D // H

        def _xavier(key, shape):
            fan_in, fan_out = (shape[1], shape[0])
            a = float(np.sqrt(6.0 / (fan_in + fan_out)))
            return jax.random.uniform(key, shape, jnp.float32, -a, a)
        s_len, bsz, d_model = x.shape
        h, dh = (H, DH)
        c_len = q_c.shape[0]

        def proj(W, b):
            return (x @ W.T + b).reshape(s_len, bsz, h, dh).transpose(1, 2, 0, 3)
        q = proj(Wq, bq)
        k = proj(Wk, bk)
        v = proj(Wv, bv)
        qc = q_c.reshape(c_len, h, dh).transpose(1, 0, 2)
        cw = jnp.einsum('hcd,bhsd->bhcs', qc, k)
        cw = jnp.exp(cw - jnp.max(cw, axis=-1, keepdims=True))
        norm = jnp.cumsum(cw, axis=-1)
        kv = jnp.concatenate([k, v], axis=-1)
        kv_c = jnp.cumsum(cw[..., None] * kv[:, :, None, :, :], axis=3) / norm[..., None]
        k_c, v_c = (kv_c[..., :dh], kv_c[..., dh:])
        q = q / (jnp.sqrt(jnp.float32(dh)) * jnp.exp(beta)[None, :, None, None])
        sw = jax.nn.softmax(jnp.einsum('bhsd,bhcsd->bhsc', q, k_c), axis=-1)
        o = jnp.einsum('bhsc,bhcsd->bhsd', sw, v_c)
        o = o.transpose(2, 0, 1, 3).reshape(s_len, bsz, d_model)
        return o @ Wo.T + bo

    def _L3_ffn_ref(x, w_gate, w_up, w_down):
        import jax, jax.numpy as jnp
        import numpy as np
        BLOCK = 32
        W_BITS = 4
        ACT_BITS = 16

        def act_qdq(x):
            qmax = 2.0 ** (ACT_BITS - 1) - 1.0
            scale = jnp.maximum(jnp.max(jnp.abs(x)) / qmax, 1e-12)
            return jnp.clip(jnp.round(x / scale), -qmax - 1.0, qmax) * scale

        def fixed_qdq_u16(x):
            scale = 1.0 / 65536.0
            return jnp.clip(jnp.round(x / scale), 0.0, 65535.0) * scale

        def lpbq_dequant(w):
            O, I = w.shape
            qmax = 2.0 ** (W_BITS - 1) - 1.0
            wb = w.reshape(O, I // BLOCK, BLOCK)
            s = jnp.maximum(jnp.max(jnp.abs(wb), axis=-1, keepdims=True) / qmax, 1e-12)
            wq = jnp.clip(jnp.round(wb / s), -qmax - 1.0, qmax) * s
            return wq.reshape(O, I)
        x = act_qdq(x)
        up = act_qdq(x @ lpbq_dequant(w_up).T)
        gate = act_qdq(x @ lpbq_dequant(w_gate).T)
        sig = fixed_qdq_u16(jax.nn.sigmoid(gate))
        gate = act_qdq(gate * sig)
        o = act_qdq(gate * up)
        return o @ lpbq_dequant(w_down).T
    x = x + _L0_xattn_ref(ctx_768, _layernorm(x, axis=-1), mask_BxS2_bk0, L0_xattn_ln_x_g, L0_xattn_ln_x_b, L0_xattn_ln_l_g, L0_xattn_ln_l_b, L0_xattn_qn_g, L0_xattn_kn_g, L0_xattn_Wq, L0_xattn_Wkv, L0_xattn_Wlkv, L0_xattn_Wo, L0_xattn_bo)
    x = x + _L0_attn_ref(_layernorm(x, axis=-1), L0_attn_P_q, L0_attn_P_k, L0_attn_P_v, L0_attn_P_o)
    x = x + _L0_ffn_ref(_layernorm(x, axis=-1), L0_ffn_gW1, L0_ffn_gb1, L0_ffn_gW2, L0_ffn_gb2, L0_ffn_eW1, L0_ffn_eb1, L0_ffn_eW2, L0_ffn_eb2)
    x = x + _L1_xattn_ref(_layernorm(x, axis=-1), ctx_768, mask_BxS_bf1, mask_BxS2_bf1, L1_xattn_Wq, L1_xattn_Wk, L1_xattn_Wv, L1_xattn_W_film_in, L1_xattn_b_film_in, L1_xattn_W_film_out, L1_xattn_b_film_out, L1_xattn_g_norm_in, L1_xattn_b_norm_in, L1_xattn_g_norm_out, L1_xattn_b_norm_out, L1_xattn_g_ffn, L1_xattn_b_ffn, L1_xattn_W1, L1_xattn_b1, L1_xattn_W2, L1_xattn_b2, L1_xattn_log_dt, L1_xattn_A_re, L1_xattn_A_im, L1_xattn_C_re, L1_xattn_C_im, L1_xattn_D_skip, L1_xattn_mod_gate)
    x = x + _L1_attn_ref(_layernorm(x, axis=-1), L1_attn_W_q, L1_attn_W_k, L1_attn_W_v, L1_attn_W_o, L1_attn_log_c, L1_attn_beta, L1_attn_attention_bias)
    x = x + _L1_ffn_ref(_layernorm(x, axis=-1), L1_ffn_Ws, L1_ffn_bs, L1_ffn_Wg, L1_ffn_Wu, L1_ffn_Wd)
    x = x + _L2_xattn_ref(_layernorm(x, axis=-1), ctx_768, L2_xattn_Wq, L2_xattn_Wk, L2_xattn_Wv, L2_xattn_Wo, L2_xattn_bo)
    x = x + _L2_attn_ref(_layernorm(x, axis=-1), L2_attn_Wk, L2_attn_bk, L2_attn_Wv, L2_attn_bv, L2_attn_Wq, L2_attn_bq, L2_attn_Wkp, L2_attn_bkp, L2_attn_Wqp, L2_attn_bqp, L2_attn_phase_scale, L2_attn_ln_g, L2_attn_ln_b, L2_attn_Wo, L2_attn_bo)
    x = x + _L2_ffn_ref(_layernorm(x, axis=-1), L2_ffn_weight, L2_ffn_bias)
    x = x + _L3_xattn_ref(_layernorm(x, axis=-1), ctx_768, ctx_768, L3_xattn_Wq, L3_xattn_bq, L3_xattn_Wk, L3_xattn_bk, L3_xattn_Wv, L3_xattn_bv, L3_xattn_Wo, L3_xattn_bo)
    x = x + _L3_attn_ref(_layernorm(x, axis=-1), L3_attn_q_c, L3_attn_beta, L3_attn_Wq, L3_attn_bq, L3_attn_Wk, L3_attn_bk, L3_attn_Wv, L3_attn_bv, L3_attn_Wo, L3_attn_bo)
    x = x + _L3_ffn_ref(_layernorm(x, axis=-1), L3_ffn_w_gate, L3_ffn_w_up, L3_ffn_w_down)
    return x

_drawn_inputs = setup_inputs


def setup_inputs(seed=0):
    import zlib

    import numpy as np

    out = dict(_drawn_inputs(seed))
    spreads = {'L0_xattn_ln_x_g': (1.0, 0.2),
     'L0_xattn_ln_x_b': (0.0, 0.1),
     'L0_xattn_ln_l_g': (1.0, 0.2),
     'L0_xattn_ln_l_b': (0.0, 0.1),
     'L0_xattn_qn_g': (1.0, 0.2),
     'L0_xattn_kn_g': (1.0, 0.2),
     'L0_xattn_bo': (0.0, 0.1),
     'L0_ffn_gb1': (0.0, 0.1),
     'L0_ffn_gb2': (0.20000000298023224, 0.2),
     'L1_xattn_b_film_in': (0.0, 0.1),
     'L1_xattn_b_film_out': (0.0, 0.1),
     'L1_xattn_g_norm_in': (1.0, 0.2),
     'L1_xattn_b_norm_in': (0.0, 0.1),
     'L1_xattn_g_norm_out': (1.0, 0.2),
     'L1_xattn_b_norm_out': (0.0, 0.1),
     'L1_xattn_g_ffn': (1.0, 0.2),
     'L1_xattn_b_ffn': (0.0, 0.1),
     'L1_xattn_b1': (0.0, 0.1),
     'L1_xattn_b2': (0.0, 0.1),
     'L1_xattn_A_re': (-0.5, 0.2),
     'L1_ffn_bs': (0.0, 0.1),
     'L2_attn_bk': (0.0, 0.1),
     'L2_attn_bv': (0.0, 0.1),
     'L2_attn_bq': (0.0, 0.1),
     'L2_attn_bkp': (0.0, 0.1),
     'L2_attn_bqp': (0.0, 0.1),
     'L2_attn_phase_scale': (3.1415927410125732, 0.2),
     'L2_attn_ln_g': (1.0, 0.2),
     'L2_attn_ln_b': (0.0, 0.1),
     'L2_attn_bo': (0.0, 0.1),
     'L3_xattn_bq': (0.0, 0.1),
     'L3_xattn_bk': (0.0, 0.1),
     'L3_xattn_bv': (0.0, 0.1),
     'L3_xattn_bo': (0.0, 0.1),
     'L3_attn_beta': (0.0, 0.1),
     'L3_attn_bq': (0.0, 0.1),
     'L3_attn_bk': (0.0, 0.1),
     'L3_attn_bv': (0.0, 0.1),
     'L3_attn_bo': (0.0, 0.1)}
    factors = {}
    for name, (base, spread) in spreads.items():
        noise = np.random.default_rng([zlib.crc32(name.encode()), seed]).standard_normal(out[name].shape)
        drawn = base * np.exp(spread * noise) if base else spread * noise
        out[name] = jnp.asarray(drawn.astype(out[name].dtype))
    for name, factor in factors.items():
        out[name] = (out[name] * factor).astype(out[name].dtype)
    return out
```

```python
from contextlib import ExitStack

import numpy as np

import concourse.bass as bass
from concourse import mybir

F32 = mybir.dt.float32
BF16 = mybir.dt.bfloat16
U8 = mybir.dt.uint8
U32 = mybir.dt.uint32
I32 = mybir.dt.int32
ALU = mybir.AluOpType
ACT = mybir.ActivationFunctionType
AX = mybir.AxisListType.X

P = 128
NB, NS, D = 32, 32, 256
NT = NB * NS
TILES = NT // P
BT = P // NS
DC = D // P
G, DV = 257, 192
V1 = DV - P
CT0, CT1, CK = 0, G, 2 * G
NEG = -1.0e30
HALF = 512
LN_EPS = 1e-5
ROUND = 12582912.0
TWO_PI_HI, TWO_PI_LO = 6.28125, 0.0019353071795864769
PI_CLAMP = 3.1415925


class Queue:

    def __init__(self, name):
        self.name, self.ops, self.sem, self.n, self.seen = name, [], None, 0, {}

    def wait(self, *tickets):
        for t in tickets:
            if t is None:
                continue
            if isinstance(t, list):
                self.wait(*t)
                continue
            s, v = t
            if self.seen.get(id(s), 0) < v:
                self.seen[id(s)] = v
                self.ops.append(lambda e, s=s, v=v: e.wait_ge(s, v))

    def __call__(self, fn, *tickets):
        self.wait(*tickets)
        self.n += 1
        self.ops.append(lambda e, s=self.sem: fn(e).then_inc(s, 1))
        return (self.sem, self.n)

    def silent(self, fn, *tickets):
        self.wait(*tickets)
        self.ops.append(fn)

    def now(self):
        return (self.sem, self.n) if self.n else None


class Slot:

    def __init__(self, t, sem=None):
        self.t, self.free, self.sem, self.n = t, [], sem, 0


class Ring:
    def __init__(self, slots):
        self.slots, self.i = slots, 0

    def next(self):
        self.i += 1
        return self.slots[(self.i - 1) % len(self.slots)]



def chunks(w, rows=P):
    k = -(-w.shape[0] // rows)
    out = np.zeros((k * rows, w.shape[1]), w.dtype)
    out[:w.shape[0]] = w
    return out.reshape(k, rows, w.shape[1]).transpose(1, 0, 2).reshape(rows, -1)


def col(b):
    return chunks(b.reshape(-1, 1))


def row(b):
    return b.reshape(1, -1)


def wide(b):
    return np.broadcast_to(b.reshape(1, -1), (P, b.size))


def layout(pieces):
    at, n = {}, 0
    for name, a in pieces.items():
        at[name] = (a.shape[0], n, n + a.shape[1])
        n += a.shape[1]
    out = np.zeros((P, n), np.float32)
    for name, a in pieces.items():
        r, c0, c1 = at[name]
        out[:r, c0:c1] = a
    return at, out


def words(mask):
    pad = -mask.shape[1] % 4
    return np.ascontiguousarray(np.pad(mask, ((0, 0), (0, pad)))).view(np.uint32)


def head_pad_k(wk, dh, aug):
    h = wk.shape[1] // dh
    out = np.zeros((P, h, aug), np.float32)
    for i in range(h):
        f = i * dh % P
        out[f:f + dh, i, :] = wk[:, i * dh:(i + 1) * dh].T
    return out.reshape(P, -1)


def head_pad_v(wv, dh):
    h = wv.shape[1] // dh
    out = np.zeros((wv.shape[0], h, P), np.float32)
    for i in range(h):
        f = i * dh % P
        out[:, i, f:f + dh] = wv[:, i * dh:(i + 1) * dh]
    return out.reshape(wv.shape[0], -1)


def host_layout(a):
    p, s = {}, {}
    eye = np.eye(P, dtype=np.float32)
    tok = np.arange(P)
    same = (tok[:, None] // NS == tok[None, :] // NS)
    causal = same & (tok[:, None] % NS <= tok[None, :] % NS)
    head16 = (np.arange(P)[:, None] // 16 == np.arange(8)[None, :]).astype(np.float32)
    p["const"] = {
        "eye": eye, "ones": np.ones((P, HALF), np.float32), "causal": causal.astype(np.float32),
        "head16": head16, "iota8": wide(np.arange(8, dtype=np.float32)),
        "causal_neg": np.tile(np.where(np.arange(NS)[None, :] <= np.arange(NS)[:, None], 0.0, NEG)
                              .astype(np.float32), (BT, 1)),
        "diag32": np.tile(np.eye(NS, dtype=np.float32), (BT, 1)),
        "pos": wide(np.arange(NS, dtype=np.float32)),
        "not_first": wide((np.arange(NT) % NS != 0).astype(np.float32)),
    }
    L = lambda b, n: np.asarray(a[f"{b}_{n}"])
    b = "L0_xattn"
    p[b] = {"wq": chunks(L(b, "Wq").T), "wkv0": L(b, "Wkv").T[:P], "wkv1": L(b, "Wkv").T[P:],
            "wlkv": chunks(L(b, "Wlkv").T), "wo": chunks(L(b, "Wo").T), "bo": row(L(b, "bo")),
            "gx0": col(L(b, "ln_x_g")[:P]), "gx1": L(b, "ln_x_g")[P:, None],
            "bx0": col(L(b, "ln_x_b")[:P]), "bx1": L(b, "ln_x_b")[P:, None],
            "gl": col(L(b, "ln_l_g")), "bl": col(L(b, "ln_l_b")),
            "qn": wide(L(b, "qn_g")), "kn": wide(L(b, "kn_g"))}
    b = "L0_attn"
    flat = lambda w: w.transpose(1, 0, 2).reshape(D, -1)
    p[b] = {"wq": chunks(flat(L(b, "P_q"))), "wk": chunks(flat(L(b, "P_k"))),
            "wv": chunks(flat(L(b, "P_v")))}
    p[b] |= {"wo": chunks(L(b, "P_o").transpose(0, 2, 1).reshape(-1, D))}
    b = "L0_ffn"
    p[b] = {"gw1": chunks(L(b, "gW1").T), "gb1": col(L(b, "gb1")), "gw2": chunks(L(b, "gW2").T),
            "gw2b": chunks(np.repeat(L(b, "gW2").T[:, :, None], P, 2).reshape(D, -1)),
            "gb2w": wide(L(b, "gb2")), "gb2": L(b, "gb2")[:, None],
            "eb1": L(b, "eb1"), "eb2": L(b, "eb2")}
    s["eW1"] = np.ascontiguousarray(L(b, "eW1").reshape(8, 8, P, DC, P).transpose(1, 4, 0, 3, 2)
                                    .reshape(8, P, 8 * DC * P))
    s["eW2"] = np.ascontiguousarray(L(b, "eW2").reshape(4, 2, D, 8, P).transpose(0, 4, 3, 1, 2)
                                    .reshape(4, P, 8 * 2 * D))
    b = "L1_xattn"
    wk = L(b, "Wk")
    p[b] = {"wq": chunks(L(b, "Wq")), "wk0": head_pad_k(wk, 32, DV),
            "wv0": L(b, "Wv")[:P], "wv1": L(b, "Wv")[P:],
            "fi": chunks(L(b, "W_film_in")), "bfi": col(L(b, "b_film_in")),
            "fo": chunks(L(b, "W_film_out")), "bfo": col(L(b, "b_film_out")),
            "gi": col(L(b, "g_norm_in")), "bi": col(L(b, "b_norm_in")),
            "gf": col(L(b, "g_ffn")), "bf": col(L(b, "b_ffn")),
            "go": wide(L(b, "g_norm_out")), "bo": wide(L(b, "b_norm_out")),
            "b1": col(L(b, "b1")), "b2": row(L(b, "b2")), "logdt": col(L(b, "log_dt")),
            "are": chunks(L(b, "A_re")), "aim": chunks(L(b, "A_im")),
            "cre": chunks(L(b, "C_re")), "cim": chunks(L(b, "C_im")),
            "dskip": col(L(b, "D_skip")), "mg": wide(L(b, "mod_gate"))}
    p[b] |= {"w1": chunks(L(b, "W1")), "w2": chunks(L(b, "W2"))}
    b = "L1_attn"
    p[b] = {"wq": chunks(L(b, "W_q").T), "wk": chunks(L(b, "W_k").T), "wv": chunks(L(b, "W_v").T),
            "wo": chunks(L(b, "W_o").T), "logc": wide(L(b, "log_c")), "beta": wide(L(b, "beta")),
            "ab": wide(L(b, "attention_bias"))}
    b = "L1_ffn"
    p[b] = {"ws": chunks(L(b, "Ws")), "bs": row(L(b, "bs"))}
    s["Wgu"] = np.stack([np.concatenate([chunks(L(b, "Wg")[e]), chunks(L(b, "Wu")[e]),
                                         chunks(L(b, "Wd")[e])], 1) for e in range(8)])
    b = "L2_xattn"
    p[b] = {"wq": chunks(L(b, "Wq")),
            "wk": L(b, "Wk").T.reshape(8, P, DV).transpose(1, 0, 2).reshape(P, -1),
            "bo": row(L(b, "bo"))}
    p[b] |= {"wv0": L(b, "Wv")[:P], "wv1": L(b, "Wv")[P:], "wo": chunks(L(b, "Wo"))}
    b = "L2_attn"
    p[b] = {n.lower(): chunks(L(b, n)) for n in ("Wk", "Wv", "Wq", "Wkp", "Wqp", "Wo")}
    p[b] |= {n: col(L(b, n)) for n in ("bk", "bv", "bq", "bkp", "bqp", "phase_scale", "ln_g", "ln_b")}
    p[b] |= {"bo": row(L(b, "bo"))}
    b = "L2_ffn"
    p[b] = {"w": chunks(L(b, "weight").T), "bias": wide(L(b, "bias"))}
    b = "L3_xattn"
    wka = np.concatenate([L(b, "Wk"), L(b, "bk")[None]], 0)
    wva = np.concatenate([L(b, "Wv"), L(b, "bv")[None]], 0)
    p[b] = {"wq": chunks(L(b, "Wq")), "bq": col(L(b, "bq")), "wk": head_pad_k(wka, 16, DV + 1),
            "wv0": head_pad_v(wva[:P], 16), "wv1": head_pad_v(wva[P:], 16),
            "wo": chunks(L(b, "Wo")), "bo": row(L(b, "bo"))}
    b = "L3_attn"
    qc = np.zeros((DC, P, 4, 2, 64), np.float32)
    for h in range(16):
        qc[h // 8, h % 8 * 16:h % 8 * 16 + 16, h % 8 // 2, h % 2] = L(b, "q_c")[:, h * 16:h * 16 + 16].T
    p[b] = {n.lower(): chunks(L(b, n).T) for n in ("Wq", "Wk", "Wv", "Wo")}
    p[b] |= {"bq": col(L(b, "bq")), "bk": col(L(b, "bk")), "bv": row(L(b, "bv")), "bo": row(L(b, "bo")),
             "qc": qc.transpose(1, 0, 2, 3, 4).reshape(P, -1), "beta": col(np.repeat(L(b, "beta"), 16))}
    b = "L3_ffn"
    p[b] = {"gate": chunks(L(b, "w_gate")), "up": chunks(L(b, "w_up")), "down": chunks(L(b, "w_down"))}
    at, arrays = {}, {}
    for name, pieces in p.items():
        at[name], arrays[f"w_{name}"] = layout(pieces)
    for name, x in s.items():
        arrays[f"s_{name}"] = x
    arrays["x"] = np.ascontiguousarray(np.asarray(a["x"]).reshape(TILES, P, D).transpose(1, 0, 2))
    ctx = np.asarray(a["ctx_768"])
    aug = np.concatenate([ctx, np.ones((NB, G, 1), np.float32)], 2)
    pack = np.zeros((NB, P, 2 * G + 3 * (DV + 1)), np.float32)
    tr = aug.transpose(0, 2, 1)
    pack[:, :, CT0:CT0 + G], pack[:, :V1 + 1, CT1:CT1 + G] = tr[:, :P], tr[:, P:]
    for i in range(3):
        part = aug[:, i * P:(i + 1) * P]
        pack[:, :part.shape[1], CK + i * (DV + 1):CK + (i + 1) * (DV + 1)] = part
    arrays["ctx"] = pack
    arrays["ctx_last"] = np.ascontiguousarray(ctx[:, G - 1])
    arrays["keep0"] = words(np.asarray(a["mask_BxS2_bk0"]))
    arrays["keep1"] = words(np.asarray(a["mask_BxS2_bf1"]))
    arrays["qmask"] = words(np.tile(np.asarray(a["mask_BxS_bf1"]).T, (4, 1)))
    return at, arrays


class Core:

    WEIGHTS = 9500
    SCRATCH = 25400

    def __init__(self, nc, ctx, dram, at):
        self.nc, self.ctx, self.dram, self.at = nc, ctx, dram, at
        self.pe, self.dve, self.act, self.pool, self.sp = (Queue(n) for n in ("pe", "dve", "act", "pool", "sp"))
        self.X = self.sb("X", TILES * D).rearrange("p (t d) -> p t d", t=TILES)
        self.XN = self.sb("XN", TILES * D).rearrange("p (t d) -> p t d", t=TILES)
        self.XT = self.sb("XT", DC * NT).rearrange("p (c n) -> p c n", c=DC)
        self.consts = self.sb("consts", max(c1 for _, _, c1 in at["const"].values()))
        self.stats = self.sb("stats", TILES * 6).rearrange("p (t k) -> p t k", t=TILES)
        self.meanvar = self.sb("meanvar", TILES * 2).rearrange("p (t k) -> p t k", t=TILES)
        self.rstd = self.sb("rstd", TILES)
        self.areas = [self.sb(f"weights{i}", self.WEIGHTS) for i in range(2)]
        self.scratch = self.sb("scratch", self.SCRATCH)
        self.banks = Ring([Slot(ctx.enter_context(nc.psum_tensor(f"bank{i}", [P, HALF], F32))[:, :])
                           for i in range(8)])
        self.weight_sem = [self.new_sem(f"weights{i}_loaded") for i in range(2)]
        self.block_no = 0
        self.prefetched = None
        self.ends = []

    def sb(self, name, cols):
        return self.ctx.enter_context(self.nc.sbuf_tensor(name, [P, cols], F32))[:, :]

    def new_sem(self, name):
        return self.ctx.enter_context(self.nc.semaphore(name))

    def const(self, name):
        r, c0, c1 = self.at["const"][name]
        return self.consts[:r, c0:c1]

    def load_weights(self, name, area):
        cols = self.dram[f"w_{name}"].shape[1]
        assert cols <= self.WEIGHTS, (name, cols)
        sem, n = self.weight_sem[area], 16 * (self.loads.get(area, 0) + 1)
        self.loads[area] = self.loads.get(area, 0) + 1
        if len(self.ends) >= 1:
            self.sp.wait(self.ends[-1])
        self.sp.silent(lambda e: e.dma_start(self.areas[area][:, :cols], self.dram[f"w_{name}"]).then_inc(sem, 16))
        return (sem, n)

    loads = {}

    def begin(self, name, nxt):
        for q in (self.pe, self.dve, self.act, self.pool):
            q.sem, q.n = self.new_sem(f"{name}_{q.name}"), 0
            if self.ends:
                q.wait(self.ends[-1])
        area = self.block_no % 2
        self.w_ready = self.prefetched or self.load_weights(name, area)
        self.prefetched = self.load_weights(nxt, 1 - area) if nxt else None
        for q in (self.pe, self.dve, self.act, self.pool):
            q.wait(self.w_ready)
        self.area, self.name, self.used = self.areas[area], name, 0
        self.block_no += 1
        for b in self.banks.slots:
            b.free = []

    def fence(self):
        now = [q.now() for q in (self.pe, self.dve, self.act, self.pool)]
        for q in (self.pe, self.dve, self.act, self.pool, self.sp):
            q.wait(now)

    def end(self):
        self.ends.append([q.now() for q in (self.pe, self.dve, self.act, self.pool)])

    def w(self, piece):
        r, c0, c1 = self.at[self.name][piece]
        return self.area[:r, c0:c1]

    def wc(self, piece, k):
        return self.w(piece).rearrange("p (k n) -> p k n", k=k)

    def tmp(self, cols, rows=P):
        a = self.scratch[:rows, self.used:self.used + cols]
        self.used += cols
        assert self.used <= self.SCRATCH, (self.name, self.used)
        return a

    def mm(self, out, terms, *tickets):
        self.pe.wait(*tickets)
        for i, (l, r) in enumerate(terms):
            last = i == len(terms) - 1
            f = lambda e, l=l, r=r, i=i, last=last: e.matmul(out, lhsT=l, rhs=r, start=i == 0, stop=last)
            t = self.pe(f) if last else self.pe.silent(f)
        return t

    def transpose(self, out, in_, *tickets):
        k = in_.shape[0]
        return self.pe(lambda e: e.transpose(out, in_, self.const("eye")[:k, :k]), *tickets)

    def copy(self, q, out, in_, *tickets):
        if q is self.act:
            return q(lambda e: e.activation(out, in_, ACT.Copy), *tickets)
        return q(lambda e: e.tensor_copy(out, in_), *tickets)

    def tt(self, out, a, b, op, *tickets, q=None):
        return (q or self.dve)(lambda e: e.tensor_tensor(out, a, b, op), *tickets)

    def ts(self, out, a, s1, s2, op0, op1, *tickets, q=None):
        if op1 is None:
            return (q or self.dve)(lambda e: e.tensor_scalar(out, a, s1, None, op0), *tickets)
        return (q or self.dve)(lambda e: e.tensor_scalar(out, a, s1, s2, op0, op1), *tickets)

    def stt(self, out, a, s, b, op0, op1, *tickets):
        return self.dve(lambda e: e.scalar_tensor_tensor(out=out, in0=a, scalar=s, in1=b, op0=op0, op1=op1),
                        *tickets)

    def recip(self, x, *tickets, out=None):
        out = x if out is None else out
        return self.dve(lambda e: e.reciprocal(out, x), *tickets)

    def reduce(self, out, in_, op, *tickets):
        return self.dve(lambda e: e.tensor_reduce(out, in_, AX.X, op), *tickets)

    def af(self, out, in_, func, *tickets, bias=0.0, scale=1.0, accum=None):
        if accum is None:
            return self.act(lambda e: e.activation(out, in_, func, bias=bias, scale=scale), *tickets)
        return self.act(lambda e: e.activation(out, in_, func, bias=bias, scale=scale, accum_out=accum), *tickets)


    def normalise(self, src, dst, *tickets):
        for t in range(TILES):
            st = self.dve(lambda e, t=t: e.bn_stats(self.stats[:, t, :], src[:, t, :]), *tickets)
        for t in range(TILES):
            st = self.dve(lambda e, t=t: e.bn_aggr(self.meanvar[:, t, :], self.stats[:, t, :]), st)
        r = self.ts(self.rstd, self.meanvar[:, :, 1], LN_EPS, None, ALU.add, None, st)
        r = self.recip(self.rstd, self.af(self.rstd, self.rstd, ACT.Sqrt, r))
        return [self.ts(dst[:, t, :], src[:, t, :], self.meanvar[:, t, 0:1], self.rstd[:, t:t + 1],
                        ALU.subtract, ALU.mult, r) for t in range(TILES)]

    def to_features(self, src, dst, src_ready, gain=None, shift=None, *tickets):
        done = []
        for c in range(DC):
            for h in range(2):
                b = self.banks.next()
                for j in range(4):
                    t = 4 * h + j
                    tr = self.transpose(b.t[:, j * P:(j + 1) * P], src[:, t, c * P:(c + 1) * P],
                                        b.free, src_ready[t], *tickets)
                o = dst[:, c, h * HALF:(h + 1) * HALF]
                if gain is not None:
                    d = self.ts(o, b.t, gain[:, c:c + 1], shift[:, c:c + 1], ALU.mult, ALU.add, tr)
                else:
                    d = self.copy(self.act if h else self.dve, o, b.t, tr)
                b.free = [d]
                done.append(d)
        return done

    def enter(self):
        ready = self.normalise(self.X, self.XN)
        return ready, self.to_features(self.XN, self.XT, ready)

    def project(self, dst, w, k, src, outs, ready, bias=None, scale=None, func=None):
        done = []
        for o in range(outs):
            for h in range(2):
                b = self.banks.next()
                cols = slice(h * HALF, (h + 1) * HALF)
                m = self.mm(b.t, [(w[:, c, o * P:(o + 1) * P], src[:, c, cols]) for c in range(k)],
                            b.free, ready, self.w_ready)
                bb = 0.0 if bias is None else bias[:, o:o + 1]
                if func is not None:
                    d = self.af(dst[:, o, cols], b.t, func, m, bias=bb)
                elif bias is None:
                    d = self.copy(self.act if (o + h) % 2 else self.dve, dst[:, o, cols], b.t, m)
                else:
                    d = self.ts(dst[:, o, cols], b.t, bb, None, ALU.add, None, m)
                b.free = [d]
                done.append(d)
        return done

    def add_output(self, src, w, k, ready, bias=None, tiles=range(TILES), cols=None):
        done = []
        for t in tiles:
            b = self.banks.next()
            o = b.t[:, :D]
            sel = cols if cols is not None else slice(t * P, (t + 1) * P)
            terms = [(src[:, c, sel], w[:, c, :]) for c in range(k)]
            if bias is not None:
                terms.append((self.const("ones")[0:1, :P], bias))
            m = self.mm(o, terms, b.free, ready, self.w_ready)
            d = self.tt(self.X[:, t, :], o, self.X[:, t, :], ALU.add, m)
            b.free = [d]
            done.append(d)
        return done


def l1_ffn(c):
    E, F = 8, 688
    FC = -(-F // P)
    sizes = [min(P, F - P * f) for f in range(FC)]
    stream = [Slot(c.tmp(2 * DC * F + FC * D), c.new_sem(f"expert_weights{i}")) for i in range(2)]
    loaded = []

    def load(e):
        s = stream[e % 2]
        c.sp.wait(s.free)
        c.sp.silent(lambda q: q.dma_start(s.t, c.dram["s_Wgu"][e]).then_inc(s.sem, 16))
        s.n += 16
        loaded.append((s.sem, s.n))

    c.sp.wait(c.ends[-1] if c.ends else None)
    load(0)
    load(1)
    ready, xt = c.enter()
    logit = c.tmp(TILES * E).rearrange("p (t e) -> p t e", t=TILES)
    top = c.tmp(TILES * 8).rearrange("p (t e) -> p t e", t=TILES)
    idx = c.tmp(TILES * 8).bitcast(U32).rearrange("p (t e) -> p t e", t=TILES)
    idf = c.tmp(TILES * 8).rearrange("p (t e) -> p t e", t=TILES)
    comb = c.tmp(TILES * E).rearrange("p (t e) -> p t e", t=TILES)
    hot = c.tmp(TILES * E).rearrange("p (t e) -> p t e", t=TILES)
    wt = c.tmp(TILES * 2).rearrange("p (t k) -> p t k", t=TILES)
    b = c.banks.next()
    for t in range(TILES):
        m = c.mm(b.t[:, t * E:(t + 1) * E],
                 [(c.XT[:, k, t * P:(t + 1) * P], c.wc("ws", DC)[:, k, :]) for k in range(DC)]
                 + [(c.const("ones")[0:1, :P], c.w("bs"))], b.free, xt, c.w_ready)
    cp = c.copy(c.dve, logit, b.t[:, :TILES * E], m)
    b.free = [cp]
    for t in range(TILES):
        mx = c.dve(lambda e, t=t: e.max(top[:, t, :], logit[:, t, :]), cp)
        mi = c.dve(lambda e, t=t: e.max_index(idx[:, t, :], top[:, t, :], logit[:, t, :]), mx)
    ix = c.copy(c.dve, idf, idx, mi)
    d1 = c.tt(wt[:, :, 1], top[:, :, 1], top[:, :, 0], ALU.subtract, mx)
    ex = c.af(wt[:, :, 1], wt[:, :, 1], ACT.Exp, d1)
    s1 = c.ts(wt[:, :, 0], wt[:, :, 1], 1.0, None, ALU.add, None, ex)
    s2 = c.dve(lambda e: e.reciprocal(wt[:, :, 0], wt[:, :, 0]), s1)
    s3 = c.tt(wt[:, :, 1], wt[:, :, 1], wt[:, :, 0], ALU.mult, s2)
    for t in range(TILES):
        h1 = c.ts(comb[:, t, :], c.const("iota8"), idf[:, t, 0:1], wt[:, t, 0:1], ALU.is_equal, ALU.mult, ix, s3)
        h2 = c.ts(hot[:, t, :], c.const("iota8"), idf[:, t, 1:2], wt[:, t, 1:2], ALU.is_equal, ALU.mult, ix, s3)
    comb_ready = c.tt(comb, comb, hot, ALU.add, h1, h2)
    hid = c.tmp(FC * NT).rearrange("p (f n) -> p f n", f=FC)
    gact = Ring([Slot(c.tmp(HALF)) for _ in range(4)])
    hid_free = [[], []]
    for e_ in range(E):
        s = stream[e_ % 2]
        wg = s.t[:, :DC * F].rearrange("p (k f) -> p k f", k=DC)
        wu = s.t[:, DC * F:2 * DC * F].rearrange("p (k f) -> p k f", k=DC)
        wd = s.t[:, 2 * DC * F:].rearrange("p (k d) -> p k d", k=FC)
        hid_done = [[], []]
        for h in range(2):
            cols = slice(h * HALF, (h + 1) * HALF)
            for f in range(FC):
                n = sizes[f]
                bg, bu = c.banks.next(), c.banks.next()
                mg = c.mm(bg.t[:n], [(wg[:, k, f * P:f * P + n], c.XT[:, k, cols]) for k in range(DC)],
                          bg.free, xt, loaded[e_])
                mu = c.mm(bu.t[:n], [(wu[:, k, f * P:f * P + n], c.XT[:, k, cols]) for k in range(DC)],
                          bu.free)
                g = gact.next()
                a = c.af(g.t[:n], bg.t[:n], ACT.Silu, mg, g.free)
                bg.free = [a]
                v = c.tt(hid[:n, f, cols], g.t[:n], bu.t[:n], ALU.mult, a, mu, hid_free[h])
                g.free = bu.free = [v]
                hid_done[h].append(v)
        for h in range(2):
            for t in range(4 * h, 4 * h + 4):
                b = c.banks.next()
                m = c.mm(b.t[:, :D], [(hid[:sizes[f], f, t * P:(t + 1) * P], wd[:sizes[f], f, :])
                                      for f in range(FC)], b.free, hid_done[h])
                v = c.stt(c.X[:, t, :], b.t[:, :D], comb[:, t, e_:e_ + 1], c.X[:, t, :],
                          ALU.mult, ALU.add, m, comb_ready, ready, last_x[t] if e_ else None)
                if t == 0:
                    nxt = []
                nxt.append(v)
                b.free = [v]
            hid_free[h] = [m]
        last_x = nxt
        s.free = [m]
        if e_ + 2 < E:
            load(e_ + 2)


def phase_sin(c, out, y, tmp, shift, ready):
    a = c.ts(out, y, 1.0, shift, ALU.mult, ALU.add, ready)
    n = c.ts(tmp, out, 1.0 / (2.0 * np.pi), ROUND, ALU.mult, ALU.add, a)
    n = c.ts(tmp, tmp, ROUND, None, ALU.subtract, None, n)
    r = c.stt(out, tmp, -TWO_PI_HI, out, ALU.mult, ALU.add, n)
    r = c.stt(out, tmp, -TWO_PI_LO, out, ALU.mult, ALU.add, r)
    r = c.ts(out, out, PI_CLAMP, -PI_CLAMP, ALU.min, ALU.max, r)
    return c.af(out, out, ACT.Sin, r)


def l2_attn(c):
    big = lambda: c.tmp(DC * NT).rearrange("p (k n) -> p k n", k=DC)
    flat = lambda a: a.rearrange("p k n -> p (k n)")
    ready, xt = c.enter()
    key, val, qry, kp, qp, cs, tmp = (big() for _ in range(7))
    k = c.project(key, c.wc("wk", DC), DC, c.XT, DC, xt, bias=c.w("bk"))
    v = c.project(val, c.wc("wv", DC), DC, c.XT, DC, xt, bias=c.w("bv"))
    q = c.project(qry, c.wc("wq", DC), DC, c.XT, DC, xt, bias=c.w("bq"))
    kt = c.project(kp, c.wc("wkp", DC), DC, key, DC, k, bias=c.w("bkp"), func=ACT.Tanh)
    qt = c.project(qp, c.wc("wqp", DC), DC, qry, DC, q, bias=c.w("bqp"), func=ACT.Tanh)
    for i in range(DC):
        kt.append(c.ts(kp[:, i], kp[:, i], c.w("phase_scale")[:, i:i + 1], None, ALU.mult, None, kt))
        qt.append(c.ts(qp[:, i], qp[:, i], c.w("phase_scale")[:, i:i + 1], None, ALU.mult, None, qt))
    last = [kt, qt]
    for phase, shift, mem in ((kp, np.pi / 2, key), (kp, 0.0, qry)):
        s = phase_sin(c, flat(cs), flat(phase), flat(tmp), shift, last)
        m = c.tt(flat(cs), flat(cs), flat(val), ALU.mult, s, v)
        last = []
        for i in range(DC):
            last.append(c.dve(lambda e, i=i, mem=mem: e.tensor_tensor_scan(
                mem[:, i], c.const("not_first"), cs[:, i], 0.0, ALU.mult, ALU.add), m))
    s = phase_sin(c, flat(cs), flat(qp), flat(tmp), np.pi / 2, last)
    m = c.tt(flat(key), flat(key), flat(cs), ALU.mult, s)
    s = phase_sin(c, flat(cs), flat(qp), flat(tmp), 0.0, m)
    m = c.tt(flat(qry), flat(qry), flat(cs), ALU.mult, s)
    m = c.tt(flat(key), flat(key), flat(qry), ALU.add, m)
    r = c.ts(flat(key), flat(key), 1.0 / np.sqrt(D), None, ALU.mult, None, m)
    tm = val.rearrange("p k n -> p (k n)").rearrange("p (t d) -> p t d", t=TILES)
    back = to_tokens(c, key, tm, [r] * DC)
    tm2 = kp.rearrange("p k n -> p (k n)").rearrange("p (t d) -> p t d", t=TILES)
    n = c.normalise(tm, tm2, back)
    f = c.to_features(tm2, qp, n, c.w("ln_g"), c.w("ln_b"), s)
    c.add_output(qp, c.wc("wo", DC), DC, [f, ready], c.w("bo"))
    for t in range(TILES):
        c.tt(c.X[:, t, :], c.X[:, t, :], c.XN[:, t, :], ALU.add, c.dve.now())


def to_tokens(c, src, dst, ready):
    done = []
    for t in range(0, TILES, 2):
        b = c.banks.next()
        for j in range(2):
            for k in range(DC):
                tr = c.transpose(b.t[:, j * D + k * P:j * D + (k + 1) * P],
                                 src[:, k, (t + j) * P:(t + j + 1) * P], b.free, ready[k])
        d = c.copy(c.act if t % 4 else c.dve, dst[:, t:t + 2, :], b.t, tr)
        b.free = [d]
        done.append(d)
    return done


def global_max(c, parts, ready):
    one, allp = c.tmp(1), c.tmp(1)
    line = c.tmp(P, 1)
    m = c.reduce(one, parts, ALU.max, ready)
    b = c.banks.next()
    t = c.transpose(b.t[0:1, :P], one, b.free, m)
    m = c.reduce(line[:, 0:1], b.t[0:1, :P], ALU.max, t)
    t = c.mm(b.t[:, 256:257], [(c.const("ones")[0:1, :P], line[:, 0:1])], m)
    m = c.copy(c.dve, allp, b.t[:, 256:257], t)
    b.free = [m]
    return allp, m


def absmax(c, out, in_, ready):
    return c.dve(lambda e: e.tensor_reduce(out, in_, AX.X, ALU.max, apply_absolute_value=True), ready)


def l2_ffn(c):
    FP8_MAX = 448.0
    ready, xt = c.enter()

    def quantise(x, n, ready):
        q, step = c.tmp(n), c.tmp(n)
        out = c.tmp(n // 2).bitcast(BF16)
        part, sc, inv = c.tmp(1), c.tmp(1), c.tmp(1)
        a = absmax(c, part, x, ready)
        big, a = global_max(c, part, a)
        a = c.ts(sc, big, 1e-12, None, ALU.max, None, a)
        a = c.recip(sc, a)
        a = c.ts(sc, sc, FP8_MAX, FP8_MAX, ALU.mult, ALU.min, a)
        i = c.recip(sc, a, out=inv)
        a = c.ts(q, x, sc, FP8_MAX, ALU.mult, ALU.min, a)
        a = c.ts(q, q, -FP8_MAX, None, ALU.max, None, a)
        b = c.dve(lambda e: e.tensor_scalar(step.bitcast(U32), q.bitcast(U32), 0x7F800000, None,
                                            ALU.bitwise_and), a)
        b = c.ts(step, step, 2.0 ** -6, 1.5 * 2.0 ** 20, ALU.max, ALU.mult, b)
        b = c.tt(q, q, step, ALU.add, b)
        b = c.tt(out, q, step, ALU.subtract, b)
        return out, inv, [b, i]

    wq, w_inv, wr = quantise(c.w("w"), DC * D, c.w_ready)
    xq, x_inv, xr = quantise(c.XT.rearrange("p c n -> p (c n)"), DC * NT, xt)
    wq = wq.rearrange("p (c n) -> p c n", c=DC)
    xq = xq.rearrange("p (c n) -> p c n", c=DC)
    sc = c.tmp(1)
    s = c.tt(sc, w_inv, x_inv, ALU.mult, wr, xr)
    res = Ring([Slot((c.tmp(D), c.tmp(D // 2).bitcast(BF16))) for _ in range(2)])
    for t in range(TILES):
        b = c.banks.next()
        m = c.mm(b.t[:, :D], [(xq[:, k, t * P:(t + 1) * P], wq[:, k, :]) for k in range(DC)], b.free, wr, xr)
        r = res.next()
        y, yb = r.t
        d = c.stt(y, b.t[:, :D], sc, c.w("bias"), ALU.mult, ALU.add, m, s, r.free)
        b.free = [d]
        d = c.copy(c.dve, yb, y, d)
        r.free = [c.tt(c.X[:, t, :], yb, c.X[:, t, :], ALU.add, d)]


def l3_ffn(c):
    H, HC, BLK = 768, 6, 32
    QMAX = 32767.0
    ready, xt = c.enter()
    one = c.const("ones")[:, 0:1]

    def dequant(w, cols, ready):
        nb = cols // BLK
        s, inv = c.tmp(nb), c.tmp(nb)
        sb, ib = (v.rearrange("p (b o) -> p b o", o=1).to_broadcast([P, nb, BLK]) for v in (s, inv))
        wv = w.rearrange("p (b k) -> p b k", k=BLK)
        a = absmax(c, s, wv, ready)
        a = c.ts(s, s, 1.0 / 7.0, 1e-12, ALU.mult, ALU.max, a)
        a = c.recip(s, a, out=inv)
        a = c.tt(wv, wv, ib, ALU.mult, a)
        a = c.ts(w, w, ROUND, None, ALU.add, None, a)
        a = c.ts(w, w, ROUND, None, ALU.subtract, None, a)
        a = c.ts(w, w, 7.0, -8.0, ALU.min, ALU.max, a)
        return c.tt(wv, wv, sb, ALU.mult, a)

    def flip(w, rows, cols, ready):
        rc, cc = rows // P, cols // P
        src = w.rearrange("p (r n) -> p r n", r=rc)
        dst = c.tmp(rows * cc).rearrange("p (k r) -> p k r", k=cc)
        done = []
        for k in range(cc):
            for r0 in range(0, rc, 4):
                b = c.banks.next()
                n = min(4, rc - r0)
                for r in range(n):
                    tr = c.transpose(b.t[:, r * P:(r + 1) * P], src[:, r0 + r, k * P:(k + 1) * P], b.free, ready)
                d = c.copy(c.act, dst[:, k, r0 * P:(r0 + n) * P], b.t[:, :n * P], tr)
                b.free = [d]
                done.append(d)
        return dst, done

    def act_scale(parts, ready):
        big, a = global_max(c, parts, ready)
        sc = c.tmp(1)
        a = c.ts(sc, big, 1.0 / QMAX, 1e-12, ALU.mult, ALU.max, a)
        inv = c.tmp(1)
        return (sc, inv), c.recip(sc, a, out=inv)

    def qdq(x, sc, ready):
        scale, inv = sc
        a = c.ts(x, x, inv, ROUND, ALU.mult, ALU.add, ready)
        a = c.ts(x, x, ROUND, QMAX, ALU.subtract, ALU.min, a)
        return c.ts(x, x, -QMAX - 1.0, scale, ALU.max, ALU.mult, a)

    wg, gr = flip(c.w("gate"), H, D, dequant(c.w("gate"), HC * D, c.w_ready))
    wu, ur = flip(c.w("up"), H, D, dequant(c.w("up"), HC * D, c.w_ready))
    wd, dr = flip(c.w("down"), D, H, dequant(c.w("down"), DC * H, c.w_ready))
    part = c.tmp(1)
    x = c.XT.rearrange("p c n -> p (c n)")
    sc, a = act_scale(part, absmax(c, part, x, xt))
    xq = qdq(x, sc, a)
    up = c.tmp(HC * NT).rearrange("p (f n) -> p f n", f=HC)
    gate = c.tmp(HC * NT).rearrange("p (f n) -> p f n", f=HC)
    parts = c.tmp(HC), c.tmp(HC)

    def branch(y, w, part, wr):
        d = c.project(y, w, DC, c.XT, HC, [xq, wr])
        m = [absmax(c, part[:, f:f + 1], y[:, f], d) for f in range(HC)]
        sc, a = act_scale(part, m)
        return [qdq(y[:, f], sc, a) for f in range(HC)]

    g = branch(gate, wg, parts[0], gr)
    u = branch(up, wu, parts[1], ur)
    sig = Ring([Slot(c.tmp(NT)) for _ in range(1)])
    m = []
    for f in range(HC):
        s = sig.next()
        a = c.af(s.t, gate[:, f], ACT.Sigmoid, g[f], s.free)
        a = c.ts(s.t, s.t, 65536.0, ROUND, ALU.mult, ALU.add, a)
        a = c.ts(s.t, s.t, ROUND, 65535.0, ALU.subtract, ALU.min, a)
        a = c.ts(s.t, s.t, 0.0, 1.0 / 65536.0, ALU.max, ALU.mult, a)
        a = c.tt(gate[:, f], gate[:, f], s.t, ALU.mult, a)
        s.free = [a]
        m.append(absmax(c, parts[0][:, f:f + 1], gate[:, f], a))
    sc, a = act_scale(parts[0], m)
    m = []
    for f in range(HC):
        b = qdq(gate[:, f], sc, a)
        b = c.tt(gate[:, f], gate[:, f], up[:, f], ALU.mult, b, u)
        m.append(absmax(c, parts[1][:, f:f + 1], gate[:, f], b))
    sc, a = act_scale(parts[1], m)
    o = [qdq(gate[:, f], sc, a) for f in range(HC)]
    c.add_output(gate, wd, HC, [o, dr])



def each(a, n):
    m = a.shape[1]
    return a.rearrange("p (m o) -> p m o", o=1).to_broadcast([P, m, n])


def rows_of(a, m):
    n = a.shape[1]
    return a.rearrange("p (o n) -> p o n", o=1).to_broadcast([P, m, n])


def softmax_rows(c, s3, n, ready, normalise=True):
    m = s3.shape[1]
    mx, sm = c.tmp(m), c.tmp(m)
    a = c.reduce(mx, s3, ALU.max, ready)
    a = c.tt(s3, s3, each(mx, n), ALU.subtract, a)
    a = c.af(s3, s3, ACT.Exp, a)
    a = c.reduce(sm, s3, ALU.add, a)
    a = c.recip(sm, a)
    if normalise:
        a = c.tt(s3, s3, each(sm, n), ALU.mult, a)
    return a, sm


def l0_attn(c):
    H, DK = 16, 64
    HC = H * DK // P
    ready, xt = c.enter()
    q3 = c.tmp(HC * NT).rearrange("p (k n) -> p k n", k=HC)
    k3 = c.tmp(HC * NT).rearrange("p (k n) -> p k n", k=HC)
    q = c.project(q3, c.wc("wq", DC), DC, c.XT, HC, xt)
    k = c.project(k3, c.wc("wk", DC), DC, c.XT, HC, xt)
    wv = c.wc("wv", DC)
    slots = Ring([Slot((c.tmp(H * NS), c.tmp(H), c.tmp(H), c.tmp(H))) for _ in range(2)])
    vals = Ring([Slot(c.tmp(H * DK)) for _ in range(2)])
    outs = Ring([Slot(c.tmp(HC * P)) for _ in range(2)])
    own_buf = Slot(c.tmp(H * NS))
    for t in range(TILES):
        sl = slots.next()
        sc, mx, sm, own = sl.t
        s3 = sc.rearrange("p (h n) -> p h n", h=H)
        a = []
        for odd in range(2):
            b = c.banks.next()
            r = slice(odd * DK, odd * DK + DK)
            for s in range(BT):
                cols = slice(t * P + s * NS, t * P + (s + 1) * NS)
                for i in range(H // 2):
                    m = c.mm(b.t[s * NS:(s + 1) * NS, i * NS:(i + 1) * NS],
                             [(q3[r, i, cols], k3[r, i, cols])], b.free, q, k)
            d = c.stt(s3[:, odd::2], b.t[:, :H // 2 * NS].rearrange("p (h n) -> p h n", n=NS), float(np.sqrt(DK)),
                      rows_of(c.const("causal_neg"), H // 2), ALU.mult, ALU.add, m, sl.free)
            b.free = [d]
            a.append(d)
        a = c.reduce(mx, s3, ALU.max, a)
        a = c.tt(s3, s3, each(mx, NS), ALU.subtract, a)
        a = c.af(s3, s3, ACT.Exp, a)
        a1 = c.reduce(sm, s3, ALU.add, a)
        a1 = c.recip(sm, a1)
        o3 = own_buf.t.rearrange("p (h n) -> p h n", h=H)
        a2 = c.tt(o3, s3, rows_of(c.const("diag32"), H), ALU.mult, a, own_buf.free)
        a2 = c.reduce(own, o3, ALU.add, a2)
        own_buf.free = [a2]
        a = c.tt(own, own, sm, ALU.mult, a1, a2)
        v = vals.next()
        vd = []
        for half in range(2):
            b = c.banks.next()
            m = c.mm(b.t, [(c.XT[:, i, t * P:(t + 1) * P], wv[:, i, half * HALF:(half + 1) * HALF])
                           for i in range(DC)], b.free, xt)
            n = HALF // DK
            d = c.tt(v.t[:, half * HALF:(half + 1) * HALF].rearrange("p (h d) -> p h d", h=n),
                     b.t.rearrange("p (h d) -> p h d", h=n), each(own[:, half * n:(half + 1) * n], DK),
                     ALU.mult, m, a, v.free)
            b.free = [d]
            vd.append(d)
        sl.free = [d]
        o = outs.next()
        od = []
        for half in range(2):
            b = c.banks.next()
            for i in range(4):
                m = c.transpose(b.t[:, i * P:(i + 1) * P], v.t[:, half * HALF + i * P:half * HALF + (i + 1) * P],
                                b.free, vd[half])
            d = c.copy(c.act, o.t[:, half * HALF:(half + 1) * HALF], b.t, m, o.free)
            b.free = [d]
            od.append(d)
        v.free = [m]
        c.add_output(o.t.rearrange("p (k n) -> p k n", k=HC), c.wc("wo", HC), HC, od, tiles=[t], cols=slice(0, P))
        o.free = [c.pe.now()]


def l0_ffn(c):
    E, HC = 8, 8
    w1_ring = Ring([Slot(c.tmp(E * DC * P), c.new_sem(f"hidden_weights{i}")) for i in range(2)])
    c.sp.wait(c.ends[-1] if c.ends else None)

    def load(ring, src):
        s = ring.next()
        c.sp.wait(s.free)
        c.sp.silent(lambda q: q.dma_start(s.t, src).then_inc(s.sem, 16))
        s.n += 16
        return s, (s.sem, s.n)

    first = [load(w1_ring, c.dram["s_eW1"][i]) for i in range(2)]
    ready, xt = c.enter()
    hid = c.tmp(HC * NT).rearrange("p (k n) -> p k n", k=HC)
    h = hid[:, 0:DC]
    d = c.project(h, c.wc("gw1", DC), DC, c.XT, DC, xt, bias=c.w("gb1"), func=ACT.Relu)
    mean = c.tmp(DC * NB).rearrange("p (k b) -> p k b", k=DC)
    for k in range(DC):
        a = c.reduce(mean[:, k], h[:, k].rearrange("p (s b) -> p b s", b=NB), ALU.add, d)
    a = c.ts(mean, mean, 1.0 / NS, None, ALU.mult, None, a)
    rep = c.tmp(DC * P).rearrange("p (k s b) -> p k s b", k=DC, s=BT)
    for k in range(DC):
        r = c.copy(c.dve, rep[:, k], rows_of(mean[:, k], BT), a)
    gate_tok, gate_row = c.tmp(E), c.tmp(E * NB)
    gate_col = c.tmp(HALF, E)
    b = c.banks.next()
    rep2 = rep.rearrange("p k s b -> p k (s b)")
    c.mm(b.t[:, 0:E], [(rep2[:, k], c.wc("gw2", DC)[:, k]) for k in range(DC)], b.free, r)
    c.mm(b.t[0:E, 32:32 + NB], [(c.wc("gw2", DC)[:, k], mean[:, k]) for k in range(DC)])
    gw = c.w("gw2b").rearrange("p (k e m) -> p k e m", k=DC, e=E)
    for e in range(E):
        m3 = c.mm(b.t[:, 64 + e * NB:64 + (e + 1) * NB], [(gw[:, k, e], mean[:, k]) for k in range(DC)])
    g1 = c.tt(gate_tok, b.t[:, 0:E], c.w("gb2w"), ALU.add, m3)
    g2 = c.ts(gate_col.rearrange("p (s b) -> p s b", b=NB),
              b.t[0:E, 32:32 + NB].rearrange("p (o b) -> p o b", o=1).to_broadcast([E, HALF // NB, NB]),
              c.w("gb2"), None, ALU.add, None, m3)
    gr3 = gate_row.rearrange("p (e b) -> p e b", e=E)
    g3 = c.tt(gr3, b.t[:, 64:64 + E * NB].rearrange("p (e b) -> p e b", e=E), each(c.w("gb2w"), NB), ALU.add, m3)
    b.free = [g1, g2, g3]
    xs = c.tmp(E * DC * HALF)
    xs4 = xs.rearrange("p (e k n) -> p e k n", e=E, k=DC)
    xs_free, hid_done = [], []
    for half in range(2):
        cols = slice(half * HALF, (half + 1) * HALF)
        sd = []
        for e in range(E):
            for k in range(DC):
                sd.append(c.tt(xs4[:, e, k].rearrange("p (s b) -> p s b", b=NB),
                               c.XT[:, k, cols].rearrange("p (s b) -> p s b", b=NB),
                               rows_of(gr3[:, e], HALF // NB), ALU.mult, g3, xt, xs_free,
                               q=c.pool if k else c.dve))
        for f in range(HC):
            s, got = first.pop(0)
            w = s.t.rearrange("p (e k n) -> p e k n", e=E, k=DC)
            b = c.banks.next()
            m = c.mm(b.t, [(w[:, e, k], xs4[:, e, k]) for e in range(E) for k in range(DC)]
                     + [(c.w("eb1")[:, f * P:(f + 1) * P], gate_col)], b.free, sd, got, g2)
            d = c.af(hid[:, f, cols], b.t, ACT.Relu, m)
            b.free = [d]
            hid_done.append(d)
            s.free = [m]
            if half * HC + f + 2 < 2 * HC:
                first.append(load(w1_ring, c.dram["s_eW1"][(f + 2) % HC]))
        xs_free = [m]
    w2_ring = Ring([Slot(xs[:, i * HC * HALF:(i + 1) * HC * HALF], c.new_sem(f"output_weights{i}")) for i in range(2)])
    for s in w2_ring.slots:
        s.free = [m]
    nxt = [load(w2_ring, c.dram["s_eW2"][i]) for i in range(2)]
    x_done = [[] for _ in range(TILES)]
    for t in range(TILES):
        b = c.banks.next()
        m = c.mm(b.t[:, :D], [(gate_col[:, :P], c.w("eb2"))], b.free, g2)
        x_done[t] = b.free = [c.tt(c.X[:, t], b.t[:, :D], c.X[:, t], ALU.add, m, ready)]
    for p_ in range(E // 2):
        s, got = nxt.pop(0)
        w = s.t.rearrange("p (k n) -> p k n", k=HC)
        for t in range(TILES):
            b = c.banks.next()
            m = c.mm(b.t, [(hid[:, k, t * P:(t + 1) * P], w[:, k]) for k in range(HC)], b.free, hid_done, got)
            for i in range(2):
                e = 2 * p_ + i
                x_done[t] = c.stt(c.X[:, t], b.t[:, i * D:(i + 1) * D], gate_tok[:, e:e + 1], c.X[:, t],
                                  ALU.mult, ALU.add, m, g1, x_done[t])
            b.free = [x_done[t]]
        s.free = [m]
        if p_ + 2 < E // 2:
            nxt.append(load(w2_ring, c.dram["s_eW2"][p_ + 2]))


def l1_attn(c):
    H, DH, EPS = 16, 16, 1e-5
    NH = TILES * H
    ready, xt = c.enter()

    def softplus(x):
        y, z = c.tmp(1), c.tmp(1)
        a = c.ts(y, x, -1.0, None, ALU.mult, None, c.w_ready)
        a = c.tt(y, y, x, ALU.min, a)
        a = c.af(y, y, ACT.Exp, a)
        a = c.af(y, y, ACT.Ln, a, bias=1.0)
        a2 = c.ts(z, x, 0.0, None, ALU.max, None, c.w_ready)
        return z, c.tt(z, z, y, ALU.add, a, a2)

    cc, a0 = softplus(c.w("logc"))
    bp, a1 = softplus(c.w("beta"))
    rc, irc, edge, negc, twoc, slope, negab = (c.tmp(1) for _ in range(7))
    a = c.af(rc, cc, ACT.Sqrt, a0)
    a = c.recip(rc, a, out=irc)
    consts = [c.ts(edge, irc, EPS, None, ALU.subtract, None, a),
              c.ts(negc, cc, -1.0, None, ALU.mult, None, a0),
              c.ts(twoc, cc, 2.0, None, ALU.mult, None, a0),
              c.ts(slope, bp, irc, -1.0, ALU.mult, ALU.mult, a, a1),
              c.ts(negab, c.w("ab"), -1.0, None, ALU.mult, None, c.w_ready)]

    tok = lambda a: a.rearrange("p (t d) -> p t d", t=TILES)
    heads = lambda a: a.rearrange("p t (h d) -> p (t h) d", h=H)
    qkv, done = [], []
    for n in ("wq", "wk", "wv"):
        dst = tok(c.tmp(TILES * D))
        dd = []
        for t in range(0, TILES, 2):
            b = c.banks.next()
            for j in range(2):
                m = c.mm(b.t[:, j * D:(j + 1) * D],
                         [(c.XT[:, k, (t + j) * P:(t + j + 1) * P], c.wc(n, DC)[:, k]) for k in range(DC)],
                         b.free, xt)
            d = c.copy(c.act if t % 4 else c.dve, dst[:, t:t + 2], b.t, m)
            b.free = [d]
            dd.append(d)
        qkv.append(dst)
        done.append(dd)
    sq = tok(c.tmp(TILES * D))

    def norm2(v, ready):
        n2 = c.tmp(NH)
        a = c.tt(sq, v, v, ALU.mult, ready, c.dve.now())
        return n2, c.reduce(n2, heads(sq), ALU.add, a)

    def exp_factor(n2, ready):
        vn, f = c.tmp(NH), c.tmp(NH)
        a = c.af(vn, n2, ACT.Sqrt, ready)
        a = c.ts(vn, vn, EPS, rc, ALU.max, ALU.mult, a, consts)
        a = c.af(f, vn, ACT.Tanh, a)
        a = c.recip(vn, a)
        return f, c.tt(f, f, vn, ALU.mult, a)

    def log_factor(n2, ready):
        y, z, g = c.tmp(NH), c.tmp(NH), c.tmp(NH)
        a = c.af(y, n2, ACT.Sqrt, ready)
        a = c.ts(y, y, EPS, None, ALU.max, None, a)
        b = c.ts(z, y, edge, rc, ALU.min, ALU.mult, a, consts)
        a = c.ts(y, y, rc, 2.0, ALU.mult, ALU.mult, b)
        a = c.recip(y, a)
        b = c.ts(g, z, -1.0, 1.0, ALU.mult, ALU.add, b)
        b = c.recip(g, b)
        b = c.stt(g, z, 1.0, g, ALU.add, ALU.mult, b)
        b = c.af(g, g, ACT.Ln, b)
        return g, c.tt(g, g, y, ALU.mult, a, b)

    def times(v, f, ready):
        return c.tt(heads(v), heads(v), each(f, DH), ALU.mult, ready)

    def to_ball_and_back(v, ready):
        n2, a = norm2(v, ready)
        f, b = exp_factor(n2, a)
        a = times(v, f, b)
        n2, a = norm2(v, a)
        f, b = log_factor(n2, a)
        return times(v, f, b)

    q, k, v = qkv
    sides = []
    for x, d in ((q, done[0]), (k, done[1])):
        n2, a = norm2(x, d)
        f, a = exp_factor(n2, a)
        a = times(x, f, a)
        n2, b = norm2(x, a)
        sides.append((n2, b, a))
    vdone = to_ball_and_back(v, done[2])
    (xns, xns_ok, q_ok), (_, kb, k_ok) = sides
    onemc = c.tmp(NH)
    om = c.ts(onemc, xns, negc, 1.0, ALU.mult, ALU.add, xns_ok, consts)
    qT = c.XT
    kT = c.XN.rearrange("p t d -> p (t d)").rearrange("p (k n) -> p k n", k=DC)
    qd = c.to_features(q, qT, [[q_ok, m]] * TILES)
    kd = c.to_features(k, kT, [[k_ok, xt]] * TILES)
    work = q.rearrange("p t d -> p (t d)"), k.rearrange("p t d -> p (t d)")
    kbd = Slot(work[0].rearrange("p (k h n) -> p k h n", k=DC, h=8))
    kbd.free = [qd]
    k2 = Slot(work[1].rearrange("p (k h n) -> p k h n", k=DC, h=8))
    k2.free = [kd]
    dist = c.tmp(TILES * H * NS).rearrange("p (t n) -> p t n", t=TILES)
    yns = Slot(c.tmp(H * NS))
    dd = []
    for t in range(TILES):
        for i in range(DC):
            e1 = c.tt(kbd.t[:, i], rows_of(kT[:, i, t * P:(t + 1) * P], 8), each(c.const("head16"), P),
                      ALU.mult, kd, kbd.free)
        e2 = c.tt(k2.t, kbd.t, kbd.t, ALU.mult, e1, k2.free)
        bxy, by = c.banks.next(), c.banks.next()
        for s in range(BT):
            r = slice(s * NS, (s + 1) * NS)
            for i in range(DC):
                m1 = c.mm(bxy.t[r, i * D:(i + 1) * D],
                          [(qT[:, i, t * P + s * NS:t * P + (s + 1) * NS], kbd.t[:, i, :, r])], bxy.free, qd, e1)
                m2 = c.mm(by.t[r, i * D:(i + 1) * D], [(c.const("ones")[:, :NS], k2.t[:, i, :, r])], by.free, e2)
        kbd.free, k2.free = [m1, e2], [m2]
        hs = slice(t * H, (t + 1) * H)
        y3 = yns.t.rearrange("p (h n) -> p h n", h=H)
        d3 = dist[:, t].rearrange("p (h n) -> p h n", h=H)
        a = c.copy(c.act, yns.t, by.t, m2, yns.free)
        by.free = [a]
        b = c.stt(dist[:, t], bxy.t, -2.0, yns.t, ALU.mult, ALU.add, m1, a)
        bxy.free = [b]
        b = c.tt(d3, d3, each(xns[:, hs], NS), ALU.add, b)
        a = c.ts(yns.t, yns.t, negc, 1.0, ALU.mult, ALU.add, b)
        a = c.tt(y3, y3, each(onemc[:, hs], NS), ALU.mult, a, om)
        a = c.ts(yns.t, yns.t, EPS, None, ALU.max, None, a)
        a = c.recip(yns.t, a)
        b = c.tt(dist[:, t], dist[:, t], yns.t, ALU.mult, a)
        yns.free = [b]
        dd.append(b)
    u = dist.rearrange("p t n -> p (t n)")
    r2 = c.tmp(TILES * H * NS)
    a = c.ts(u, u, twoc, EPS, ALU.mult, ALU.max, dd)
    a = c.stt(r2, u, 2.0, u, ALU.add, ALU.mult, a)
    a = c.af(r2, r2, ACT.Sqrt, a)
    a = c.tt(u, u, r2, ALU.add, a)
    a = c.af(u, u, ACT.Ln, a, bias=1.0)
    a = c.ts(u, u, slope, negab, ALU.mult, ALU.add, a)
    u3 = u.rearrange("p (m n) -> p m n", n=NS)
    a, _ = softmax_rows(c, u3, NS, a)
    wt = r2
    z = c.pool(lambda e: e.memset(q.rearrange("p t d -> p (t d)"), 0.0), kbd.free)
    bd = Slot(q.rearrange("p t d -> p (t d)").rearrange("p (h m) -> p h m", h=H))
    out = sq
    od = []
    for t in range(TILES):
        w = wt[:, t * H * NS:(t + 1) * H * NS]
        x = c.dve(lambda e, t=t, w=w: e.transpose(w, dist[:, t]), a)
        w3 = w.rearrange("p (h m) -> p h m", h=H)
        for s in range(BT):
            r = slice(s * NS, (s + 1) * NS)
            x2 = c.copy(c.dve, bd.t[r, :, r], w3[r], x, bd.free, z)
        b = c.banks.next()
        for h in range(H):
            m = c.mm(b.t[:, h * DH:(h + 1) * DH], [(bd.t[:, h], v[:, t, h * DH:(h + 1) * DH])], b.free, x2, vdone)
        bd.free = [m]
        d = c.copy(c.act, out[:, t], b.t[:, :D], m)
        b.free = [d]
        od.append(d)
    sq = tok(r2[:, :TILES * D])
    a = to_ball_and_back(out, [od, c.dve.now(), m])
    oT = c.XT
    f = c.to_features(out, oT, [a] * TILES)
    c.add_output(oT, c.wc("wo", DC), DC, f)


def l3_attn(c):
    H, DH, C = 16, 16, 64
    HP = H // 2
    ready, xt = c.enter()
    big = lambda: c.tmp(DC * NT).rearrange("p (k n) -> p k n", k=DC)
    xs = c.XN.rearrange("p t d -> p (t d)").rearrange("p (k n) -> p k n", k=DC)
    perm = [c.copy(q, xs[:, k].rearrange("p (b s) -> p b s", b=NB), c.XT[:, k].rearrange("p (s b) -> p b s", b=NB), xt)
            for k, q in ((0, c.dve), (1, c.pool))]
    q3, k3 = big(), big()
    kd = c.project(k3, c.wc("wk", DC), DC, xs, DC, perm, bias=c.w("bk"))
    qd = c.project(q3, c.wc("wq", DC), DC, xs, DC, perm, bias=c.w("bq"))
    temp = c.tmp(DC)
    a = c.af(temp, c.w("beta"), ACT.Exp, c.w_ready, scale=-1.0)
    qd = [c.ts(q3[:, k], q3[:, k], temp[:, k:k + 1], 1.0 / np.sqrt(DH), ALU.mult, ALU.mult, a, qd) for k in range(DC)]
    v3 = c.tmp(TILES * D).rearrange("p (t d) -> p t d", t=TILES)
    vd = []
    for t in range(TILES):
        b = c.banks.next()
        m = c.mm(b.t[:, :D], [(xs[:, k, t * P:(t + 1) * P], c.wc("wv", DC)[:, k]) for k in range(DC)]
                 + [(c.const("ones")[0:1, :P], c.w("bv"))], b.free, perm)
        d = c.copy(c.act, v3[:, t], b.t[:, :D], m)
        b.free = [d]
        vd.append(d)
    cw = c.tmp(HP * NT).rearrange("p (g n) -> p g n", g=HP)
    mx = Ring([Slot(c.tmp(NB // 2)) for _ in range(4)])
    qc = c.w("qc").rearrange("p (k g m) -> p k g m", k=DC, g=HP // DC)
    cd = [[], []]
    for half in range(2):
        for g in range(HP):
            cols = slice(half * HALF, (half + 1) * HALF)
            b = c.banks.next()
            k = g * DC // HP
            m = c.mm(b.t, [(qc[:, k, g % (HP // DC)], k3[:, k, cols])], b.free, kd)
            x = mx.next()
            b3 = b.t.rearrange("p (b s) -> p b s", s=NS)
            a = c.reduce(x.t, b3, ALU.max, m, x.free)
            a = c.tt(cw[:, g, cols].rearrange("p (b s) -> p b s", s=NS), b3, each(x.t, NS), ALU.subtract, a)
            b.free = x.free = [a]
            cd[half].append(c.af(cw[:, g, cols], cw[:, g, cols], ACT.Exp, a))
    cwT, rn, s_, wT = (Slot(c.tmp(H * C)) for _ in range(4))
    qbd, am, bm = (Slot(c.tmp(H * P)) for _ in range(3))
    o_ = Slot(c.tmp(D))
    mxs, sms = c.tmp(H), c.tmp(H)
    oT = c.XT
    outd = []
    for t in range(TILES):
        cols = slice(t * P, (t + 1) * P)
        ctd = []
        for half in range(2):
            b = c.banks.next()
            for g in range(4):
                m = c.transpose(b.t[:, g * P:(g + 1) * P], cw[:, 4 * half + g, cols], b.free, cd[t // 4])
            d = c.copy(c.act, cwT.t[:, half * HALF:(half + 1) * HALF], b.t, m, cwT.free)
            b.free = [d]
            ctd.append(d)
        nd = []
        for half in range(2):
            b = c.banks.next()
            hc = slice(half * HALF, (half + 1) * HALF)
            m = c.mm(b.t, [(c.const("causal"), cwT.t[:, hc])], b.free, ctd)
            d = c.dve(lambda e, b=b, hc=hc: e.reciprocal(rn.t[:, hc], b.t), m, rn.free)
            b.free = [d]
            nd.append(d)
        q4 = qbd.t.rearrange("p (k h n) -> p k h n", k=DC, h=8)
        qb = [c.tt(q4[:, k], rows_of(q3[:, k, cols], 8), each(c.const("head16"), P), ALU.mult, qd, qbd.free, q=c.pool)
              for k in range(DC)]
        a3 = am.t.rearrange("p (h n) -> p h n", h=H)
        ad = []
        for g in range(4):
            b = c.banks.next()
            m = c.mm(b.t, [(k3[:, g // 2, cols], q4[:, g // 2, g % 2 * 4:g % 2 * 4 + 4])], b.free, kd, qb)
            d = c.tt(a3[:, 4 * g:4 * g + 4], b.t.rearrange("p (h n) -> p h n", h=4), rows_of(c.const("causal"), 4),
                     ALU.mult, m, am.free)
            b.free = [d]
            ad.append(d)
        qbd.free = [m]
        sd = []
        for half in range(2):
            b = c.banks.next()
            for h in range(8):
                hh = 8 * half + h
                m = c.mm(b.t[:, h * C:(h + 1) * C], [(a3[:, hh], cwT.t[:, hh * C:(hh + 1) * C])], b.free, ad, ctd)
            hc = slice(half * HALF, (half + 1) * HALF)
            d = c.tt(s_.t[:, hc], b.t, rn.t[:, hc], ALU.mult, m, nd, s_.free)
            b.free = [d]
            sd.append(d)
        cwT.free = am.free = [m]
        s3 = s_.t.rearrange("p (h n) -> p h n", h=H)
        a = c.reduce(mxs, s3, ALU.max, sd)
        a = c.tt(s3, s3, each(mxs, C), ALU.subtract, a)
        a = c.af(s3, s3, ACT.Exp, a)
        a1 = c.reduce(sms, s3, ALU.add, a)
        a1 = c.recip(sms, a1)
        a2 = c.tt(s_.t, s_.t, rn.t, ALU.mult, a, a1)
        rn.free = [a2]
        a = c.tt(s3, s3, each(sms, C), ALU.mult, a1, a2)
        wd = []
        for half in range(2):
            b = c.banks.next()
            for g in range(4):
                m = c.transpose(b.t[:, g * P:(g + 1) * P], s_.t[:, half * HALF + g * P:half * HALF + (g + 1) * P], b.free, a)
            d = c.copy(c.act, wT.t[:, half * HALF:(half + 1) * HALF], b.t, m, wT.free)
            b.free = [d]
            wd.append(d)
        s_.free = [m]
        b3 = bm.t.rearrange("p (h n) -> p h n", h=H)
        bd = []
        for g in range(4):
            b = c.banks.next()
            for j in range(4):
                h = 8 * (g // 2) + 2 * j + g % 2
                r = slice(h % 2 * C, h % 2 * C + C)
                m = c.mm(b.t[:, j * P:(j + 1) * P],
                         [(cw[r, h // 2, cols], wT.t[r, h // 2 * P:(h // 2 + 1) * P])], b.free, wd)
            h0 = 8 * (g // 2) + g % 2
            d = c.tt(b3[:, h0:h0 + 7:2], b.t.rearrange("p (h n) -> p h n", h=4), rows_of(c.const("causal"), 4),
                     ALU.mult, m, bm.free)
            b.free = [d]
            bd.append(d)
        wT.free = [m]
        b = c.banks.next()
        for h in range(H):
            m = c.mm(b.t[:, h * DH:(h + 1) * DH], [(b3[:, h], v3[:, t, h * DH:(h + 1) * DH])], b.free, bd, vd)
        bm.free = [m]
        d = c.copy(c.act, o_.t, b.t[:, :D], m, o_.free)
        b.free = [d]
        b = c.banks.next()
        for k in range(DC):
            m = c.transpose(b.t[:, k * P:(k + 1) * P], o_.t[:, k * P:(k + 1) * P], b.free, d)
        o_.free = [m]
        for k in range(DC):
            d = c.copy(c.dve, oT[:, k].rearrange("p (s b) -> p b s", b=NB)[:, t * BT:(t + 1) * BT],
                       b.t[:, k * P:(k + 1) * P].rearrange("p (b s) -> p b s", b=BT), m, perm)
            outd.append(d)
        b.free = [d]
    c.add_output(oT, c.wc("wo", DC), DC, [outd, ready], c.w("bo"))



class Context:

    def __init__(self, c, slots):
        self.c = c
        self.cols = 2 * G + 3 * (DV + 1)
        self.ring = Ring([Slot(c.tmp(self.cols), c.new_sem(f"{c.name}_context{i}")) for i in range(slots)])
        c.sp.wait(c.ends[-1] if c.ends else None)
        self.queue, self.asked = [], 0
        for _ in range(slots):
            self.ask()

    def ask(self):
        if self.asked < NB:
            s, b = self.ring.next(), self.asked
            self.c.sp.wait(s.free)
            self.c.sp.silent(lambda q: q.dma_start(s.t, self.c.dram["ctx"][b]).then_inc(s.sem, 16))
            s.n += 16
            self.queue.append((s, (s.sem, s.n)))
            self.asked += 1

    def next(self):
        return self.queue.pop(0)


def head_queries(c, wk, heads, aug, src, q_tile, scale, ready, slot):
    qa, qb = slot.t
    done = []
    for part, rows, c0 in ((qa, P, 0), (qb, aug - P, P)):
        for g in range(0, heads, 4):
            b = c.banks.next()
            for j in range(4):
                m = c.mm(b.t[:rows, j * P:(j + 1) * P], [(wk(g + j)[:, c0:c0 + rows], src(g + j)[:, q_tile])],
                         b.free, ready, slot.free)
            done.append(c.copy(c.act if c0 else c.dve, part[:rows, :, g:g + 4, :].rearrange("p s h q -> p h s q"),
                               b.t[:rows].rearrange("p (h s q) -> p h s q", h=4, s=BT), m, slot.free))
            b.free = done[-1:]
    return done


def softmax_keys(c, bank, n, p_slot, stat, m, scale_after=None):
    nmax, total = stat.t
    a = c.dve(lambda e: e.tensor_reduce(nmax, bank.t[:, :n], AX.X, ALU.max, negate=True), m, stat.free)
    a = c.af(p_slot.t[:, :n], bank.t[:, :n], ACT.Exp, a, p_slot.free, bias=nmax, accum=total)
    bank.free = [a]
    a = c.recip(total, a)
    a = c.ts(p_slot.t[:, :n], p_slot.t[:, :n], total, None, ALU.mult, None, a, q=c.pool)
    stat.free = [a]
    return a


def raw_attention(c, heads, aug_k, aug_v, queries, finish):
    R = heads // 4
    ctx = Context(c, 3)
    qslots = Ring([Slot((c.tmp(BT * heads * NS).rearrange("p (s h q) -> p s h q", s=BT, h=heads),
                         c.tmp(BT * heads * NS).rearrange("p (s h q) -> p s h q", s=BT, h=heads)))
                   for _ in range(2)])
    probs = Ring([Slot(c.tmp(G)) for _ in range(2 * R)])
    stats = Ring([Slot((c.tmp(1), c.tmp(1))) for _ in range(2 * R)])
    pts = Ring([Slot((c.tmp(R * P), c.tmp(R * P), c.tmp(R * P))) for _ in range(2)])
    pc = Slot((c.tmp(heads * P).rearrange("p (h n) -> p h n", h=heads),
               c.tmp(heads * P).rearrange("p (h n) -> p h n", h=heads)))
    state = {}

    def scores(s):
        t, i = divmod(s, BT)
        if i == 0:
            slot = qslots.next()
            state["q"] = slot, queries(t, slot)
        slot, qd = state["q"]
        qa, qb = slot.t
        cx, got = ctx.next()
        out = []
        for r in range(R):
            b, p, st = c.banks.next(), probs.next(), stats.next()
            m = c.mm(b.t[:, :G], [(qa[:, i, 4 * r:4 * r + 4].rearrange("p h q -> p (h q)"), cx.t[:, CT0:CT0 + G]),
                                  (qb[:aug_k - P, i, 4 * r:4 * r + 4].rearrange("p h q -> p (h q)"),
                                   cx.t[:aug_k - P, CT1:CT1 + G])], b.free, qd, got)
            out.append((p, softmax_keys(c, b, G, p, st, m)))
        slot.free = [m]
        return cx, out

    def products(s, cx, out):
        t, i = divmod(s, BT)
        pt = pts.next()
        done = []
        for k, (k0, n) in enumerate(((0, P), (P, P), (2 * P, 1))):
            b = c.banks.next()
            for r, (p, ready) in enumerate(out):
                m = c.transpose(b.t[:n, r * P:(r + 1) * P], p.t[:, k0:k0 + n], b.free, ready)
            d = c.copy((c.act, c.dve, c.dve)[k], pt.t[k][:n], b.t[:n, :R * P], m, pt.free)
            b.free = [d]
            done.append(d)
        for p, _ in out:
            p.free = [m]
        for part, rows, f0 in ((pc.t[0], P, 0), (pc.t[1], aug_v - P, P)):
            b = c.banks.next()
            m = c.mm(b.t[:rows, :R * P],
                     [(cx.t[:n, CK + k * (DV + 1) + f0:CK + k * (DV + 1) + f0 + rows], pt.t[k][:n])
                      for k, n in enumerate((P, P, 1))], b.free, done)
            d = c.copy(c.dve if f0 else c.act, part[:rows, :, i * NS:(i + 1) * NS],
                       b.t[:rows, :R * P].rearrange("p (h q) -> p h q", h=heads), m, pc.free)
            b.free = [d]
            state.setdefault("pc", []).append(d)
        pt.free = [m]
        cx.free = [m]
        ctx.ask()
        if i == BT - 1:
            finish(t, pc.t[0], pc.t[1], state.pop("pc"))
            pc.free = [c.pe.now()]

    last = None
    for s in range(NB + 1):
        cur = scores(s) if s < NB else None
        if last:
            products(s - 1, *last)
        last = cur


def l2_xattn(c):
    H, DK = 16, 64
    ready, xt = c.enter()
    HC = H * DK // P
    qt = Slot(c.tmp(HC * P).rearrange("p (k n) -> p k n", k=HC))
    ot = Slot(c.tmp(HC * P).rearrange("p (k n) -> p k n", k=HC))
    wk = c.w("wk").rearrange("p (k f) -> p k f", k=HC)

    def queries(t, slot):
        d = []
        for g in range(0, HC, 4):
            b = c.banks.next()
            for j in range(4):
                m = c.mm(b.t[:, j * P:(j + 1) * P],
                         [(c.wc("wq", DC)[:, k, (g + j) * P:(g + j + 1) * P], c.XT[:, k, t * P:(t + 1) * P])
                          for k in range(DC)], b.free, xt)
            d.append(c.dve(lambda e, b=b, g=g: e.tensor_scalar(qt.t[:, g:g + 4].rearrange("p k n -> p (k n)"), b.t,
                                                              DK ** -0.5, None, ALU.mult), m, qt.free))
            b.free = [d[-1]]
        qa, qb = slot.t
        done = []
        for odd in range(2):
            r = slice(odd * DK, odd * DK + DK)
            for part, rows, c0 in ((qa, P, 0), (qb, V1, P)):
                for g in range(0, HC, 4):
                    b = c.banks.next()
                    for j in range(4):
                        m = c.mm(b.t[:rows, j * P:(j + 1) * P], [(wk[r, g + j, c0:c0 + rows], qt.t[r, g + j])],
                                 b.free, d)
                    done.append(c.copy(c.act if c0 else c.dve,
                                       part[:rows, :, 2 * g + odd:2 * g + odd + 7:2, :].rearrange("p s h q -> p h s q"),
                                       b.t[:rows].rearrange("p (h s q) -> p h s q", h=4, s=BT), m, slot.free))
                    b.free = done[-1:]
        qt.free = [m]
        return done

    def finish(t, pa, pb, pr):
        d = []
        for g in range(0, HC, 4):
            b = c.banks.next()
            for j in range(4):
                for odd in range(2):
                    h = 2 * (g + j) + odd
                    hc = slice(h * DK, (h + 1) * DK)
                    m = c.mm(b.t[odd * DK:(odd + 1) * DK, j * P:(j + 1) * P],
                             [(c.w("wv0")[:, hc], pa[:, h]), (c.w("wv1")[:, hc], pb[:V1, h])], b.free, pr)
            d.append(c.copy(c.act, ot.t[:, g:g + 4].rearrange("p k n -> p (k n)"), b.t, m, ot.free))
            b.free = [d[-1]]
        c.add_output(ot.t, c.wc("wo", HC), HC, [d, ready], c.w("bo"), tiles=[t], cols=slice(0, P))
        ot.free = [c.pe.now()]

    raw_attention(c, H, DV, DV, queries, finish)


def l3_xattn(c):
    H, DK = 16, 16
    ready, xt = c.enter()
    q3 = c.tmp(DC * NT).rearrange("p (k n) -> p k n", k=DC)
    ot = Slot(c.tmp(DC * P).rearrange("p (k n) -> p k n", k=DC))
    qd = c.project(q3, c.wc("wq", DC), DC, c.XT, DC, xt, bias=c.w("bq"))
    qd = [c.ts(q3[:, k], q3[:, k], DK ** -0.5, None, ALU.mult, None, qd) for k in range(DC)]
    wk = c.w("wk").rearrange("p (h f) -> p h f", h=H)
    wv = [c.w(n).rearrange("p (h f) -> p h f", h=H) for n in ("wv0", "wv1")]

    def queries(t, slot):
        return head_queries(c, lambda h: wk[:, h], H, DV + 1, lambda h: q3[:, h // 8], slice(t * P, (t + 1) * P),
                            None, qd, slot)

    def finish(t, pa, pb, pr):
        b = c.banks.next()
        for k in range(DC):
            m = c.mm(b.t[:, k * P:(k + 1) * P],
                     [x for h in range(8 * k, 8 * k + 8)
                      for x in ((wv[0][:, h], pa[:, h]), (wv[1][:, h], pb[:V1 + 1, h]))], b.free, pr)
        d = c.copy(c.act, ot.t.rearrange("p k n -> p (k n)"), b.t[:, :DC * P], m, ot.free)
        b.free = [d]
        c.add_output(ot.t, c.wc("wo", DC), DC, [d, ready], c.w("bo"), tiles=[t], cols=slice(0, P))
        ot.free = [c.pe.now()]

    raw_attention(c, H, DV + 1, DV + 1, queries, finish)


def mask_rows(c, src, cols, first, last, name):
    sem = c.new_sem(name)
    packed = c.tmp(-(-G // 4), NB).bitcast(U32)
    raw = packed.bitcast(U8)[:, :G]
    out = c.tmp(cols, NB)
    c.sp.wait(c.ends[-1] if c.ends else None)
    c.sp.silent(lambda q: q.dma_start(packed, c.dram[src]).then_inc(sem, 16))
    z = c.dve(lambda e: e.memset(out, 0.0))
    a = c.copy(c.dve, out[:, first:first + G - 1], raw[:, :G - 1], z, (sem, 16))
    a = c.copy(c.dve, out[:, last:last + 1], raw[:, G - 1:G], a)
    for x in (out[:, first:first + G - 1], out[:, last:last + 1]):
        a = c.ts(x, x, -NEG, NEG, ALU.mult, ALU.add, a)
    return out, a


def pick(c, b):
    return c.const("eye")[:NB, b:b + 1].to_broadcast([NB, P])


def l0_xattn(c):
    H, DK, RMS_EPS = 4, 64, 1e-8
    KEYS = G + NS
    L3 = NS + 1
    ctx = Context(c, 3)
    mask, mask_ok = mask_rows(c, "keep0", KEYS, 0, KEYS - 1, "keep0_loaded")
    ready = c.normalise(c.X, c.XN)
    tmp = c.tmp(TILES * D).rearrange("p (t d) -> p t d", t=TILES)
    n2 = c.normalise(c.XN, tmp, ready)
    lt = c.to_features(tmp, c.XT, n2, c.w("gl"), c.w("bl"))
    lnT = c.XT
    gq = c.tmp(DK)
    g = c.stt(gq, c.w("qn"), DK ** -0.5, c.w("kn"), ALU.mult, ALU.mult)
    q = tmp
    qd = []
    for t in range(0, TILES, 2):
        b = c.banks.next()
        for j in range(2):
            m = c.mm(b.t[:, j * D:(j + 1) * D],
                     [(lnT[:, k, (t + j) * P:(t + j + 1) * P], c.wc("wq", DC)[:, k]) for k in range(DC)], b.free, lt)
        d = c.copy(c.act if t % 4 else c.dve, q[:, t:t + 2], b.t, m)
        b.free = [d]
        qd.append(d)
    NH = TILES * H
    heads = lambda a: a.rearrange("p t (h d) -> p (t h) d", h=H)
    nrm = c.tmp(NH)
    qbd = c.tmp(DC * NB * P)

    def rms(n2, ready):
        a = c.af(n2, n2, ACT.Sqrt, ready, scale=1.0 / DK)
        a = c.ts(n2, n2, RMS_EPS, None, ALU.max, None, a)
        return c.recip(n2, a)

    a = c.tt(c.XN, q, q, ALU.mult, qd)
    a = c.reduce(nrm, heads(c.XN), ALU.add, a)
    a = rms(nrm, a)
    a = c.tt(heads(q), heads(q), each(nrm, DK), ALU.mult, a)
    a = c.tt(heads(q), heads(q), rows_of(gq, NH), ALU.mult, a, g)
    qT = c.XN.rearrange("p t d -> p (t d)").rearrange("p (k n) -> p k n", k=DC)
    qd = c.to_features(q, qT, [a] * TILES)
    z = c.pool(lambda e: e.memset(qbd, 0.0))
    q5 = qbd.rearrange("p (k b h q) -> p k b h q", k=DC, b=NB, h=H)
    bd = []
    for k in range(DC):
        for odd in range(2):
            r = slice(odd * DK, odd * DK + DK)
            bd.append(c.copy(c.dve if odd else c.act, q5[r, k, :, 2 * k + odd],
                             qT[r, k].rearrange("p (b q) -> p b q", b=NB), qd, z))
    sem = c.new_sem("last_rows_loaded")
    last = c.tmp(DV, NB)
    lT = [c.tmp(NB), c.tmp(NB, V1)]
    st = c.tmp(12)
    c.sp.silent(lambda e: e.dma_start(last, c.dram["ctx_last"]).then_inc(sem, 16))
    a = c.dve(lambda e: e.bn_stats(st[:NB, 0:6], last), (sem, 16))
    a = c.dve(lambda e: e.bn_aggr(st[:NB, 6:8], st[:NB, 0:6]), a)
    a = c.ts(st[:NB, 8:9], st[:NB, 7:8], LN_EPS, None, ALU.add, None, a)
    a = c.af(st[:NB, 8:9], st[:NB, 8:9], ACT.Sqrt, a)
    a = c.recip(st[:NB, 8:9], a)
    a = c.ts(last, last, st[:NB, 6:7], st[:NB, 8:9], ALU.subtract, ALU.mult, a)
    b = c.banks.next()
    c.transpose(b.t[:, 0:NB], last[:, 0:P], b.free, a)
    m = c.transpose(b.t[:V1, 64:64 + NB], last[:, P:DV])
    l1 = c.ts(lT[0], b.t[:, 0:NB], c.w("gx0"), c.w("bx0"), ALU.mult, ALU.add, m)
    l2 = c.ts(lT[1], b.t[:V1, 64:64 + NB], c.w("gx1"), c.w("bx1"), ALU.mult, ALU.add, m)
    b.free = [l1, l2]
    xn = Ring([Slot((c.tmp(2 * DV).rearrange("p (k d) -> p k d", k=2), c.tmp(24))) for _ in range(2)])
    xnT = Ring([Slot((c.tmp(2 * P), c.tmp(2 * P))) for _ in range(2)])
    k3 = Ring([Slot(c.tmp(3 * D)) for _ in range(2)])
    v3 = Ring([Slot(c.tmp(3 * D)) for _ in range(2)])
    sq = Slot((c.tmp(3 * D), c.tmp(3 * H)))
    kT = Ring([Slot(c.tmp(DC * KEYS).rearrange("p (k n) -> p k n", k=DC)) for _ in range(2)])
    probs = Ring([Slot(c.tmp(KEYS)) for _ in range(2)])
    stats = Ring([Slot((c.tmp(1), c.tmp(1))) for _ in range(2)])
    pts = Ring([Slot(c.tmp(3 * P)) for _ in range(2)])
    ot = Slot(c.tmp(DC * P).rearrange("p (k n) -> p k n", k=DC))
    for s in k3.slots:
        s.free = [c.pool(lambda e, s=s: e.memset(s.t, 0.0))]

    def keys_values(s):
        cx, got = ctx.next()
        xs = xn.next()
        x, st = xs.t
        for i in range(2):
            src = cx.t[:, CK + i * (DV + 1):CK + i * (DV + 1) + DV]
            a = c.dve(lambda e, src=src, i=i: e.bn_stats(st[:, 6 * i:6 * i + 6], src), got, xs.free)
        for i in range(2):
            a = c.dve(lambda e, i=i: e.bn_aggr(st[:, 12 + 2 * i:14 + 2 * i], st[:, 6 * i:6 * i + 6]), a)
        rs = st[:, 16:18]
        a = c.ts(rs, st[:, 12:16].rearrange("p (k v) -> p k v", k=2)[:, :, 1], LN_EPS, None, ALU.add, None, a)
        a = c.af(rs, rs, ACT.Sqrt, a)
        a = c.recip(rs, a)
        for i in range(2):
            src = cx.t[:, CK + i * (DV + 1):CK + i * (DV + 1) + DV]
            nd = c.ts(x[:, i], src, st[:, 12 + 2 * i:13 + 2 * i], rs[:, i:i + 1], ALU.subtract, ALU.mult, a)
        cx.free = [nd]
        ctx.ask()
        b = c.banks.next()
        for i in range(2):
            c.transpose(b.t[:, i * P:(i + 1) * P], x[:, i, 0:P], b.free, nd)
            m = c.transpose(b.t[:V1, 256 + i * P:256 + (i + 1) * P], x[:, i, P:DV])
        xs.free = [m]
        xt = xnT.next()
        d1 = c.ts(xt.t[0], b.t[:, :256], c.w("gx0"), c.w("bx0"), ALU.mult, ALU.add, m, xt.free)
        d2 = c.ts(xt.t[1][:V1], b.t[:V1, 256:], c.w("gx1"), c.w("bx1"), ALU.mult, ALU.add, m, xt.free)
        b.free = [d1, d2]
        ks, vs = k3.next(), v3.next()
        kd, vd = [], []
        for i in range(3):
            b = c.banks.next()
            if i < 2:
                n = P
                m = c.mm(b.t, [(xt.t[0][:, i * P:(i + 1) * P], c.w("wkv0")),
                               (xt.t[1][:V1, i * P:(i + 1) * P], c.w("wkv1"))], b.free, d1, d2)
            else:
                n = L3
                c.mm(b.t[:NS], [(lnT[:, k, s * NS:(s + 1) * NS], c.wc("wlkv", DC)[:, k]) for k in range(DC)],
                     b.free, lt)
                m = c.mm(b.t[NS:L3], [(lT[0][:, s:s + 1], c.w("wkv0")), (lT[1][:, s:s + 1], c.w("wkv1"))], l1, l2)
            e = c.dve if i == 1 else c.act
            kd.append(c.copy(e, ks.t[:n, i * D:(i + 1) * D], b.t[:n, :D], m, ks.free))
            vd.append(c.copy(e, vs.t[:n, i * D:(i + 1) * D], b.t[:n, D:], m, vs.free))
            b.free = [kd[-1], vd[-1]]
        xt.free = [m]
        s2, nr = sq.t
        a = c.tt(s2, ks.t, ks.t, ALU.mult, kd, sq.free, q=c.pool)
        a = c.reduce(nr, s2.rearrange("p (m d) -> p m d", d=DK), ALU.add, a)
        a = rms(nr, a)
        k4 = ks.t.rearrange("p (m d) -> p m d", d=DK)
        a = c.tt(k4, k4, each(nr, DK), ALU.mult, a)
        sq.free = [a]
        kt = kT.next()
        td = []
        for k in range(DC):
            b = c.banks.next()
            for i, n in enumerate((P, P, L3)):
                m = c.transpose(b.t[:, i * P:i * P + n], ks.t[:n, i * D + k * P:i * D + (k + 1) * P], b.free, a)
            d = c.copy((c.act, c.dve)[k], kt.t[:, k], b.t[:, :KEYS], m, kt.free)
            b.free = [d]
            td.append(d)
        ks.free = [m]
        return kt, td, vs, vd

    def scores(s, kt, td):
        b, p, st = c.banks.next(), probs.next(), stats.next()
        q4 = qbd.rearrange("p (k b m) -> p k b m", k=DC, b=NB)
        m = c.mm(b.t[:, :KEYS], [(pick(c, s), mask)] + [(q4[:, k, s], kt.t[:, k]) for k in range(DC)],
                 b.free, bd, td, mask_ok)
        kt.free = [m]
        return p, softmax_keys(c, b, KEYS, p, st, m)

    every, sums = c.banks, c.banks.slots[6:]
    c.banks = Ring(every.slots[:6])

    def products(s, p, pd, vs, vd):
        t, i = divmod(s, BT)
        pt = pts.next()
        b = c.banks.next()
        for k, n in enumerate((P, P, L3)):
            m = c.transpose(b.t[:n, k * P:(k + 1) * P], p.t[:, k * P:k * P + n], b.free, pd)
        p.free = [m]
        d1 = c.copy(c.act, pt.t[:, :2 * P], b.t[:, :2 * P], m, pt.free)
        d2 = c.copy(c.act, pt.t[:L3, 2 * P:], b.t[:L3, 2 * P:3 * P], m, pt.free)
        b.free = [d1, d2]
        for k in range(DC):
            ob = sums[k]
            m = c.mm(ob.t[:, i * 2 * NS:(i + 1) * 2 * NS],
                     [(vs.t[:n, j * D + k * P:j * D + (k + 1) * P],
                       pt.t[:n, j * P + k * 2 * NS:j * P + (k + 1) * 2 * NS]) for j, n in enumerate((P, P, L3))],
                     ob.free, d1, d2, vd)
        vs.free = pt.free = [m]
        if i == BT - 1:
            od = []
            for k in range(DC):
                ob = sums[k]
                for odd in range(2):
                    r = slice(odd * DK, odd * DK + DK)
                    od.append(c.copy(c.dve, ot.t[r, k].rearrange("p (s q) -> p s q", s=BT),
                                     ob.t[r, :BT * 2 * NS].rearrange("p (s h q) -> p h s q", s=BT, h=2)[:, odd],
                                     m, ot.free))
                ob.free = od[-2:]
            c.add_output(ot.t, c.wc("wo", DC), DC, od, c.w("bo"), tiles=[t], cols=slice(0, P))
            ot.free = [c.pe.now()]

    kv = keys_values(0)
    prev = None
    for s in range(NB + 1):
        if s < NB:
            sc = scores(s, kv[0], kv[1])
            cur = (s, *sc, kv[2], kv[3])
        if s + 1 < NB:
            kv = keys_values(s + 1)
        if s < NB:
            products(*cur)
    c.banks = every


def l1_xattn(c):
    H, DH, TOP = 4, 32, 32
    TAKEN = -3.0e38
    ready, xt = c.enter()
    ct3 = c.tmp(DC * NT).rearrange("p (k n) -> p k n", k=DC)
    kern = c.tmp(DC * NS).rearrange("p (k l) -> p k l", k=DC)
    mark = c.used
    mask, mask_ok = mask_rows(c, "keep1", G, 0, G - 1, "keep1_loaded")
    sem = c.new_sem("query_mask_loaded")
    packed = c.tmp(NB // 4).bitcast(U32)
    qraw = packed.bitcast(U8)
    qmask = c.tmp(NB)
    c.sp.silent(lambda e: e.dma_start(packed, c.dram["qmask"]).then_inc(sem, 16))
    qm = c.copy(c.dve, qmask, qraw, (sem, 16))
    q3 = c.tmp(NT)
    qd = []
    for h in range(2):
        b = c.banks.next()
        m = c.mm(b.t, [(c.wc("wq", DC)[:, k], c.XT[:, k, h * HALF:(h + 1) * HALF]) for k in range(DC)], b.free, xt)
        d = c.ts(q3[:, h * HALF:(h + 1) * HALF], b.t, DH ** -0.5, None, ALU.mult, None, m)
        b.free = [d]
        qd.append(d)
    wk = c.w("wk0").rearrange("p (h f) -> p h f", h=H)
    ctx = Context(c, 3)
    qslots = Ring([Slot((c.tmp(BT * P).rearrange("p (s h q) -> p s h q", s=BT, h=H),
                         c.tmp(BT * P).rearrange("p (s h q) -> p s h q", s=BT, h=H))) for _ in range(2)])
    works = Ring([Slot((c.tmp(G), c.tmp(8), c.tmp(1), c.tmp(1))) for _ in range(3)])
    probs = Ring([Slot(c.tmp(G)) for _ in range(3)])
    pts = Ring([Slot(c.tmp(3 * P)) for _ in range(2)])
    pc = Slot((c.tmp(H * P).rearrange("p (h n) -> p h n", h=H), c.tmp(H * P).rearrange("p (h n) -> p h n", h=H)))
    state = {}
    ctd = []

    def scores(s):
        t, i = divmod(s, BT)
        if i == 0:
            slot = qslots.next()
            state["q"] = slot, head_queries(c, lambda h: wk[:, h], H, DV, lambda h: q3, slice(t * P, (t + 1) * P),
                                            None, qd, slot)
        slot, hd = state["q"]
        qa, qb = slot.t
        cx, got = ctx.next()
        b, w, p = c.banks.next(), works.next(), probs.next()
        work, top, nmax, total = w.t
        m = c.mm(b.t[:, :G], [(pick(c, s), mask), (qa[:, i].rearrange("p h q -> p (h q)"), cx.t[:, CT0:CT0 + G]),
                              (qb[:V1, i].rearrange("p h q -> p (h q)"), cx.t[:V1, CT1:CT1 + G])],
                 b.free, hd, got, mask_ok)
        slot.free = [m]
        a = c.copy(c.act, work, b.t[:, :G], m, w.free)
        for r in range(TOP // 8):
            x = c.dve(lambda e: e.max(top, work), a)
            if r == 0:
                n = c.ts(nmax, top[:, 0:1], -1.0, None, ALU.mult, None, x)
            a = c.dve(lambda e: e.match_replace(work, top, work, TAKEN), x, n)
        x = c.af(p.t, b.t[:, :G], ACT.Exp, n, p.free, bias=nmax)
        b.free = [x]
        a = c.dve(lambda e: e.scalar_tensor_tensor(out=p.t, in0=work, scalar=TAKEN, in1=p.t, op0=ALU.is_equal,
                                                   op1=ALU.mult, accum_out=total), a, x)
        a = c.recip(total, a)
        a = c.tt(total, total, qmask[:, s:s + 1], ALU.mult, a, qm)
        a = c.ts(p.t, p.t, total, None, ALU.mult, None, a, q=c.pool)
        w.free = [a]
        return cx, p, a

    def products(s, cx, p, pd):
        t, i = divmod(s, BT)
        pt = pts.next()
        b = c.banks.next()
        for k, n in enumerate((P, P, 1)):
            m = c.transpose(b.t[:n, k * P:(k + 1) * P], p.t[:, k * P:k * P + n], b.free, pd)
        p.free = [m]
        d1 = c.copy(c.act, pt.t[:, :2 * P], b.t[:, :2 * P], m, pt.free)
        d2 = c.copy(c.act, pt.t[:1, 2 * P:], b.t[:1, 2 * P:3 * P], m, pt.free)
        b.free = [d1, d2]
        b = c.banks.next()
        for j, rows, f0 in ((0, P, 0), (1, V1, P)):
            m = c.mm(b.t[:rows, j * P:(j + 1) * P],
                     [(cx.t[:n, CK + k * (DV + 1) + f0:CK + k * (DV + 1) + f0 + rows], pt.t[:n, k * P:(k + 1) * P])
                      for k, n in enumerate((P, P, 1))], b.free, d1, d2)
        for j, rows in ((0, P), (1, V1)):
            d = c.copy(c.act, pc.t[j][:rows, :, i * NS:(i + 1) * NS],
                       b.t[:rows, j * P:(j + 1) * P].rearrange("p (h q) -> p h q", h=H), m, pc.free)
            state.setdefault("pc", []).append(d)
        b.free = [d]
        pt.free = cx.free = [m]
        ctx.ask()
        if i == BT - 1:
            pr = state.pop("pc")
            b = c.banks.next()
            for o in range(DC):
                oc = slice(o * P, (o + 1) * P)
                m = c.mm(b.t[:, oc], [x for h in range(H) for x in ((c.w("wv0")[:, oc], pc.t[0][:, h]),
                                                                  (c.w("wv1")[:, oc], pc.t[1][:V1, h]))], b.free, pr)
            pc.free = [m]
            d = c.af(ct3[:, :, t * P:(t + 1) * P], b.t[:, :D].rearrange("p (k n) -> p k n", k=DC), ACT.Copy, m,
                     scale=1.0 / H)
            b.free = [d]
            ctd.append(d)

    last = None
    for s in range(NB + 1):
        cur = scores(s) if s < NB else None
        if last:
            products(s - 1, *last)
        last = cur

    c.fence()
    c.used = mark
    s4d_kernel(c, kern)
    kern_ok = c.dve.now()
    c.fence()
    c.used = mark
    mg = c.w("mg")
    flat = lambda a: a.rearrange("p k n -> p (k n)")
    film = c.tmp(2 * DC * NT).rearrange("p (k n) -> p k n", k=2 * DC)
    x3, y3 = (c.tmp(DC * NT).rearrange("p (k n) -> p k n", k=DC) for _ in range(2))
    tok = c.tmp(TILES * D).rearrange("p (t d) -> p t d", t=TILES)

    def modulate(v, w, bias, ready, free):
        f = c.project(film, c.wc(w, DC), DC, ct3, 2 * DC, [ctd, free], bias=c.w(bias))
        a = c.ts(flat(film[:, :DC]), flat(film[:, :DC]), mg, 1.0, ALU.mult, ALU.add, f)
        b = c.ts(flat(film[:, DC:]), flat(film[:, DC:]), mg, None, ALU.mult, None, f, q=c.pool)
        a = c.tt(flat(v), flat(v), flat(film[:, :DC]), ALU.mult, a, ready)
        return c.tt(flat(v), flat(v), flat(film[:, DC:]), ALU.add, a, b)

    n = c.normalise(c.XN, tok, ready)
    f = c.to_features(tok, x3, n, c.w("gi"), c.w("bi"))
    a = modulate(x3, "fi", "bfi", f, None)
    first = c.tmp(DC)
    k0 = c.tt(first, kern[:, :, 0], c.w("dskip"), ALU.add, kern_ok)
    yd = []
    for k in range(DC):
        d = c.ts(y3[:, k], x3[:, k], first[:, k:k + 1], None, ALU.mult, None, k0, a)
        for j in range(1, NS):
            src = x3[:, k].rearrange("p (b s) -> p b s", s=NS)[:, :, :NS - j]
            dst = y3[:, k].rearrange("p (b s) -> p b s", s=NS)[:, :, j:]
            d = c.stt(dst, src, kern[:, k, j:j + 1], dst, ALU.mult, ALU.add, d)
        yd.append(d)
    a = modulate(y3, "fo", "bfo", yd, yd)
    back = to_tokens(c, y3, tok, [a] * DC)
    r = [c.tt(tok[:, t], tok[:, t], c.XN[:, t], ALU.add, back) for t in range(TILES)]
    hn = c.normalise(tok, c.XN, [r, n])
    h3 = c.XT
    f = c.to_features(c.XN, h3, hn, c.w("gf"), c.w("bf"))
    c.fence()
    c.used = mark
    tok2 = tok
    HC = 8
    hid = c.tmp(HC * NT).rearrange("p (k n) -> p k n", k=HC)
    hd = c.project(hid, c.wc("w1", DC), DC, h3, HC, f, bias=c.w("b1"), func=ACT.Gelu)
    od = []
    for t in range(TILES):
        b = c.banks.next()
        m = c.mm(b.t[:, :D], [(hid[:, k, t * P:(t + 1) * P], c.wc("w2", HC)[:, k]) for k in range(HC)]
                 + [(c.const("ones")[0:1, :P], c.w("b2"))], b.free, hd)
        d = c.tt(tok2[:, t], b.t[:, :D], tok2[:, t], ALU.add, m)
        b.free = [d]
        od.append(d)
    n = c.normalise(tok2, c.XN, od)
    for t in range(TILES):
        a = c.tt(c.XN[:, t], c.XN[:, t], c.w("go"), ALU.mult, n[t])
        a = c.tt(c.XN[:, t], c.XN[:, t], c.w("bo"), ALU.add, a)
        c.tt(c.X[:, t], c.X[:, t], c.XN[:, t], ALU.add, a)


def s4d_kernel(c, kern):
    N = 64
    n2 = lambda: c.tmp(DC * N)
    dt = c.tmp(DC)
    a0 = c.af(dt, c.w("logdt"), ACT.Exp)
    a, w = n2(), n2()
    k3 = lambda x: x.rearrange("p (k n) -> p k n", k=DC)
    r1 = c.tt(k3(a), k3(c.w("are")), each(dt, N), ALU.mult, a0)
    r2 = c.tt(k3(w), k3(c.w("aim")), each(dt, N), ALU.mult, a0)
    th, em1, ea, sw, cw, sh, t1 = (n2() for _ in range(7))
    r = c.af(th, a, ACT.Tanh, r1, scale=0.5)
    x = c.ts(t1, th, -1.0, 1.0, ALU.mult, ALU.add, r)
    x = c.recip(t1, x)
    x = c.stt(em1, th, 2.0, t1, ALU.mult, ALU.mult, x)
    e = c.ts(ea, em1, 1.0, None, ALU.add, None, x)
    s = phase_sin(c, sw, w, t1, 0.0, [x, e, r2])
    s = phase_sin(c, cw, w, t1, np.pi / 2, s)
    h = c.ts(th, w, 0.5, None, ALU.mult, None, s)
    s = phase_sin(c, sh, th, t1, 0.0, h)
    x = c.tt(em1, em1, cw, ALU.mult, s)
    y = c.tt(sh, sh, sh, ALU.mult, x)
    x = c.stt(em1, sh, -2.0, em1, ALU.mult, ALU.add, y)
    y = c.tt(sw, sw, ea, ALU.mult, x)
    cr, ci, ar, ai = c.w("cre"), c.w("cim"), c.w("are"), c.w("aim")
    nr, ni, dr, di, den = th, ea, cw, sh, n2()
    x = c.tt(nr, em1, cr, ALU.mult, y)
    y = c.tt(t1, sw, ci, ALU.mult, y)
    x = c.tt(nr, nr, t1, ALU.subtract, x, y)
    y = c.tt(ni, em1, ci, ALU.mult, x)
    z = c.tt(t1, sw, cr, ALU.mult, x)
    y = c.tt(ni, ni, t1, ALU.add, y, z)
    x = c.tt(den, ar, ar, ALU.mult, y)
    z = c.tt(t1, ai, ai, ALU.mult, y)
    x = c.tt(den, den, t1, ALU.add, x, z)
    x = c.recip(den, x)
    x = c.ts(den, den, 2.0, None, ALU.mult, None, x)
    x = c.tt(dr, nr, ar, ALU.mult, x)
    z = c.tt(t1, ni, ai, ALU.mult, x)
    x = c.tt(dr, dr, t1, ALU.add, z)
    x = c.tt(di, ni, ar, ALU.mult, x)
    z = c.tt(t1, nr, ai, ALU.mult, x)
    x = c.tt(di, di, t1, ALU.subtract, z)
    x = c.tt(dr, dr, den, ALU.mult, x)
    x = c.tt(di, di, den, ALU.mult, x)
    mag, s_, t_, u_, wl = (c.tmp(N * NS) for _ in range(5))
    v = lambda q: q.rearrange("p (n l) -> p n l", n=N)
    for k in range(DC):
        ak, wk, drk, dik = (q[:, k * N:(k + 1) * N] for q in (a, w, dr, di))
        y = c.tt(v(mag), each(ak, NS), rows_of(c.const("pos"), N), ALU.mult, x)
        y = c.af(mag, mag, ACT.Exp, y)
        z = c.tt(v(wl), each(wk, NS), rows_of(c.const("pos"), N), ALU.mult, x)
        z = phase_sin(c, s_, wl, t_, np.pi / 2, z)
        z = c.tt(v(s_), v(s_), each(drk, NS), ALU.mult, z)
        z2 = phase_sin(c, t_, wl, u_, 0.0, z)
        z2 = c.tt(v(t_), v(t_), each(dik, NS), ALU.mult, z2)
        z = c.tt(s_, s_, t_, ALU.subtract, z2)
        z = c.tt(s_, s_, mag, ALU.mult, z, y)
        x = c.reduce(kern[:, k], s_.rearrange("p (n l) -> p l n", n=N), ALU.add, z)



BLOCKS = [("L0_xattn", l0_xattn), ("L0_attn", l0_attn), ("L0_ffn", l0_ffn), ("L1_xattn", l1_xattn),
          ("L1_attn", l1_attn), ("L1_ffn", l1_ffn), ("L2_xattn", l2_xattn), ("L2_attn", l2_attn),
          ("L2_ffn", l2_ffn), ("L3_xattn", l3_xattn), ("L3_attn", l3_attn), ("L3_ffn", l3_ffn)]


def build(nc, dram, out, at, only=None):
    todo = [BLOCKS[i] for i in only] if only is not None else BLOCKS
    with ExitStack() as ctx:
        c = Core(nc, ctx, dram, at)
        x_in, x_out = c.new_sem("x_and_consts_loaded"), c.new_sem("x_stored")
        c.sp.silent(lambda e: e.dma_start(c.X, dram["x"]).then_inc(x_in, 16))
        c.sp.silent(lambda e: e.dma_start(c.consts, dram["w_const"]).then_inc(x_in, 16))
        for q in (c.pe, c.dve, c.act, c.pool):
            q.wait((x_in, 32))
        for i, (name, body) in enumerate(todo):
            c.begin(name, todo[i + 1][0] if i + 1 < len(todo) else None)
            body(c)
            c.end()
        c.sp.wait(c.ends[-1])
        c.sp.silent(lambda e: e.dma_start(out, c.X).then_inc(x_out, 16))
        c.sp.wait((x_out, 16))

        block = ctx.enter_context(nc.Block())

        @block.sync
        def _(e):
            for op in c.sp.ops:
                op(e)

        @block.tensor
        def _(e):
            for op in c.pe.ops:
                op(e)

        @block.vector
        def _(e):
            for op in c.dve.ops:
                op(e)

        @block.scalar
        def _(e):
            for op in c.act.ops:
                op(e)

        @block.gpsimd
        def _(e):
            for op in c.pool.ops:
                op(e)


def kernel(**inputs):
    import concourse.bacc as _bacc
    from concourse.bass_utils import run_bass_kernel_spmd as _run

    at, arrays = host_layout(inputs)
    nc = _bacc.Bacc("TRN2", target_bir_lowering=False, num_devices=1)
    dram = {}
    for name, a in arrays.items():
        dram[name] = nc.dram_tensor(f"in_{name}", a.shape, mybir.dt.from_np(a.dtype), kind="ExternalInput").ap()
    out = nc.dram_tensor("out_x", (P, TILES, D), F32, kind="ExternalOutput").ap()
    build(nc, dram, out, at)
    r = _run(nc, [{f"in_{n}": a for n, a in arrays.items()}], core_ids=[0])
    x = r.results[0]["out_x"]
    return x.reshape(P, TILES, D).transpose(1, 0, 2).reshape(NB, NS, D)
```

```python
from contextlib import ExitStack

import numpy as np

import concourse.bass as bass
from concourse import mybir

F32 = mybir.dt.float32
BF16 = mybir.dt.bfloat16
U8 = mybir.dt.uint8
U32 = mybir.dt.uint32
I32 = mybir.dt.int32
ALU = mybir.AluOpType
ACT = mybir.ActivationFunctionType
AX = mybir.AxisListType.X

P = 128
NB, NS, D = 32, 32, 256
NT = NB * NS
TILES = NT // P
BT = P // NS
DC = D // P
G, DV = 257, 192
V1 = DV - P
CT0, CT1, CK = 0, G, 2 * G
NEG = -1.0e30
HALF = 512
LN_EPS = 1e-5
ROUND = 12582912.0
TWO_PI_HI, TWO_PI_LO = 6.28125, 0.0019353071795864769
PI_CLAMP = 3.1415925


class Queue:

    def __init__(self, name):
        self.name, self.ops, self.sem, self.n, self.seen = name, [], None, 0, {}

    def wait(self, *tickets):
        for t in tickets:
            if t is None:
                continue
            if isinstance(t, list):
                self.wait(*t)
                continue
            s, v = t
            if self.seen.get(id(s), 0) < v:
                self.seen[id(s)] = v
                self.ops.append(lambda e, s=s, v=v: e.wait_ge(s, v))

    def __call__(self, fn, *tickets):
        self.wait(*tickets)
        self.n += 1
        self.ops.append(lambda e, s=self.sem: fn(e).then_inc(s, 1))
        return (self.sem, self.n)

    def silent(self, fn, *tickets):
        self.wait(*tickets)
        self.ops.append(fn)

    def now(self):
        return (self.sem, self.n) if self.n else None


class Slot:

    def __init__(self, t, sem=None):
        self.t, self.free, self.sem, self.n = t, [], sem, 0


class Ring:
    def __init__(self, slots):
        self.slots, self.i = slots, 0

    def next(self):
        self.i += 1
        return self.slots[(self.i - 1) % len(self.slots)]



def chunks(w, rows=P):
    k = -(-w.shape[0] // rows)
    out = np.zeros((k * rows, w.shape[1]), w.dtype)
    out[:w.shape[0]] = w
    return out.reshape(k, rows, w.shape[1]).transpose(1, 0, 2).reshape(rows, -1)


def col(b):
    return chunks(b.reshape(-1, 1))


def row(b):
    return b.reshape(1, -1)


def wide(b):
    return np.broadcast_to(b.reshape(1, -1), (P, b.size))


def layout(pieces):
    at, n = {}, 0
    for name, a in pieces.items():
        at[name] = (a.shape[0], n, n + a.shape[1])
        n += a.shape[1]
    out = np.zeros((P, n), np.float32)
    for name, a in pieces.items():
        r, c0, c1 = at[name]
        out[:r, c0:c1] = a
    return at, out


def words(mask):
    pad = -mask.shape[1] % 4
    return np.ascontiguousarray(np.pad(mask, ((0, 0), (0, pad)))).view(np.uint32)


def head_pad_k(wk, dh, aug):
    h = wk.shape[1] // dh
    out = np.zeros((P, h, aug), np.float32)
    for i in range(h):
        f = i * dh % P
        out[f:f + dh, i, :] = wk[:, i * dh:(i + 1) * dh].T
    return out.reshape(P, -1)


def head_pad_v(wv, dh):
    h = wv.shape[1] // dh
    out = np.zeros((wv.shape[0], h, P), np.float32)
    for i in range(h):
        f = i * dh % P
        out[:, i, f:f + dh] = wv[:, i * dh:(i + 1) * dh]
    return out.reshape(wv.shape[0], -1)


def host_layout(a):
    p, s = {}, {}
    eye = np.eye(P, dtype=np.float32)
    tok = np.arange(P)
    same = (tok[:, None] // NS == tok[None, :] // NS)
    causal = same & (tok[:, None] % NS <= tok[None, :] % NS)
    head16 = (np.arange(P)[:, None] // 16 == np.arange(8)[None, :]).astype(np.float32)
    p["const"] = {
        "eye": eye, "ones": np.ones((P, HALF), np.float32), "causal": causal.astype(np.float32),
        "mhalf": np.full((P, P), -0.5, np.float32), "half": np.full((P, P), 0.5, np.float32),
        "head16": head16, "iota8": wide(np.arange(8, dtype=np.float32)),
        "causal_neg": np.tile(np.where(np.arange(NS)[None, :] <= np.arange(NS)[:, None], 0.0, NEG)
                              .astype(np.float32), (BT, 1)),
        "diag32": np.tile(np.eye(NS, dtype=np.float32), (BT, 1)),
        "pos": wide(np.arange(NS, dtype=np.float32)),
        "not_first": wide((np.arange(NT) % NS != 0).astype(np.float32)),
    }
    L = lambda b, n: np.asarray(a[f"{b}_{n}"])
    b = "L0_xattn"
    p[b] = {"wq": chunks(L(b, "Wq").T), "wkv0": L(b, "Wkv").T[:P], "wkv1": L(b, "Wkv").T[P:],
            "wlkv": chunks(L(b, "Wlkv").T), "wo": chunks(L(b, "Wo").T), "bo": row(L(b, "bo")),
            "gx0": col(L(b, "ln_x_g")[:P]), "gx1": L(b, "ln_x_g")[P:, None],
            "bx0": col(L(b, "ln_x_b")[:P]), "bx1": L(b, "ln_x_b")[P:, None],
            "gl": col(L(b, "ln_l_g")), "bl": col(L(b, "ln_l_b")),
            "qn": wide(L(b, "qn_g")), "kn": wide(L(b, "kn_g"))}
    b = "L0_attn"
    flat = lambda w: w.transpose(1, 0, 2).reshape(D, -1)
    p[b] = {"wq": chunks(flat(L(b, "P_q"))), "wk": chunks(flat(L(b, "P_k"))),
            "wv": chunks(flat(L(b, "P_v")))}
    p[b] |= {"wo": chunks(L(b, "P_o").transpose(0, 2, 1).reshape(-1, D))}
    b = "L0_ffn"
    p[b] = {"gw1": chunks(L(b, "gW1").T), "gb1": col(L(b, "gb1")), "gw2": chunks(L(b, "gW2").T),
            "gw2b": chunks(np.repeat(L(b, "gW2").T[:, :, None], P, 2).reshape(D, -1)),
            "gb2w": wide(L(b, "gb2")), "gb2": L(b, "gb2")[:, None],
            "eb1": L(b, "eb1"), "eb2": L(b, "eb2")}
    s["eW1"] = np.ascontiguousarray(L(b, "eW1").reshape(8, 8, P, DC, P).transpose(1, 4, 0, 3, 2)
                                    .reshape(8, P, 8 * DC * P))
    s["eW2"] = np.ascontiguousarray(L(b, "eW2").reshape(4, 2, D, 8, P).transpose(0, 4, 3, 1, 2)
                                    .reshape(4, P, 8 * 2 * D))
    b = "L1_xattn"
    wk = L(b, "Wk")
    p[b] = {"wq": chunks(L(b, "Wq")), "wk0": head_pad_k(wk, 32, DV),
            "wv0": L(b, "Wv")[:P], "wv1": L(b, "Wv")[P:],
            "fi": chunks(L(b, "W_film_in")), "bfi": col(L(b, "b_film_in")),
            "fo": chunks(L(b, "W_film_out")), "bfo": col(L(b, "b_film_out")),
            "gi": col(L(b, "g_norm_in")), "bi": col(L(b, "b_norm_in")),
            "gf": col(L(b, "g_ffn")), "bf": col(L(b, "b_ffn")),
            "go": wide(L(b, "g_norm_out")), "bo": wide(L(b, "b_norm_out")),
            "b1": col(L(b, "b1")), "b2": row(L(b, "b2")), "logdt": col(L(b, "log_dt")),
            "are": chunks(L(b, "A_re")), "aim": chunks(L(b, "A_im")),
            "cre": chunks(L(b, "C_re")), "cim": chunks(L(b, "C_im")),
            "dskip": col(L(b, "D_skip")), "mg": wide(L(b, "mod_gate"))}
    p[b] |= {"w1": chunks(L(b, "W1")), "w2": chunks(L(b, "W2"))}
    b = "L1_attn"
    p[b] = {"wq": chunks(L(b, "W_q").T), "wk": chunks(L(b, "W_k").T), "wv": chunks(L(b, "W_v").T),
            "wo": chunks(L(b, "W_o").T), "logc": wide(L(b, "log_c")), "beta": wide(L(b, "beta")),
            "ab": wide(L(b, "attention_bias"))}
    b = "L1_ffn"
    p[b] = {"ws": chunks(L(b, "Ws")), "bs": row(L(b, "bs"))}
    s["Wgu"] = np.stack([np.concatenate([chunks(L(b, "Wg")[e]), chunks(L(b, "Wu")[e]),
                                         chunks(L(b, "Wd")[e])], 1) for e in range(8)])
    b = "L2_xattn"
    p[b] = {"wq": chunks(L(b, "Wq")),
            "wk": L(b, "Wk").T.reshape(8, P, DV).transpose(1, 0, 2).reshape(P, -1),
            "bo": row(L(b, "bo"))}
    p[b] |= {"wv0": L(b, "Wv")[:P], "wv1": L(b, "Wv")[P:], "wo": chunks(L(b, "Wo"))}
    b = "L2_attn"
    p[b] = {n.lower(): chunks(L(b, n)) for n in ("Wk", "Wv", "Wq", "Wkp", "Wqp", "Wo")}
    p[b] |= {n: col(L(b, n)) for n in ("bk", "bv", "bq", "bkp", "bqp", "phase_scale", "ln_g", "ln_b")}
    p[b] |= {"bo": row(L(b, "bo"))}
    b = "L2_ffn"
    p[b] = {"w": chunks(L(b, "weight").T), "bias": wide(L(b, "bias"))}
    b = "L3_xattn"
    wka = np.concatenate([L(b, "Wk"), L(b, "bk")[None]], 0)
    wva = np.concatenate([L(b, "Wv"), L(b, "bv")[None]], 0)
    p[b] = {"wq": chunks(L(b, "Wq")), "bq": col(L(b, "bq")), "wk": head_pad_k(wka, 16, DV + 1),
            "wv0": head_pad_v(wva[:P], 16), "wv1": head_pad_v(wva[P:], 16),
            "wo": chunks(L(b, "Wo")), "bo": row(L(b, "bo"))}
    b = "L3_attn"
    qc = np.zeros((DC, P, 4, 2, 64), np.float32)
    for h in range(16):
        qc[h // 8, h % 8 * 16:h % 8 * 16 + 16, h % 8 // 2, h % 2] = L(b, "q_c")[:, h * 16:h * 16 + 16].T
    p[b] = {n.lower(): chunks(L(b, n).T) for n in ("Wq", "Wk", "Wv", "Wo")}
    p[b] |= {"bq": col(L(b, "bq")), "bk": col(L(b, "bk")), "bv": row(L(b, "bv")), "bo": row(L(b, "bo")),
             "qc": qc.transpose(1, 0, 2, 3, 4).reshape(P, -1), "beta": col(np.repeat(L(b, "beta"), 16))}
    b = "L3_ffn"
    p[b] = {"gate": chunks(L(b, "w_gate")), "up": chunks(L(b, "w_up")), "down": chunks(L(b, "w_down"))}
    at, arrays = {}, {}
    for name, pieces in p.items():
        at[name], arrays[f"w_{name}"] = layout(pieces)
    for name, x in s.items():
        arrays[f"s_{name}"] = x
    arrays["x"] = np.ascontiguousarray(np.asarray(a["x"]).reshape(TILES, P, D).transpose(1, 0, 2))
    ctx = np.asarray(a["ctx_768"])
    aug = np.concatenate([ctx, np.ones((NB, G, 1), np.float32)], 2)
    pack = np.zeros((NB, P, 2 * G + 3 * (DV + 1)), np.float32)
    tr = aug.transpose(0, 2, 1)
    pack[:, :, CT0:CT0 + G], pack[:, :V1 + 1, CT1:CT1 + G] = tr[:, :P], tr[:, P:]
    for i in range(3):
        part = aug[:, i * P:(i + 1) * P]
        pack[:, :part.shape[1], CK + i * (DV + 1):CK + (i + 1) * (DV + 1)] = part
    arrays["ctx"] = pack
    arrays["ctx_last"] = np.ascontiguousarray(ctx[:, G - 1])
    arrays["keep0"] = words(np.asarray(a["mask_BxS2_bk0"]))
    arrays["keep1"] = words(np.asarray(a["mask_BxS2_bf1"]))
    arrays["qmask"] = words(np.tile(np.asarray(a["mask_BxS_bf1"]).T, (4, 1)))
    return at, arrays


class Core:

    WEIGHTS = 9500
    SCRATCH = 25400

    def __init__(self, nc, ctx, dram, at):
        self.nc, self.ctx, self.dram, self.at = nc, ctx, dram, at
        self.pe, self.dve, self.act, self.pool, self.sp = (Queue(n) for n in ("pe", "dve", "act", "pool", "sp"))
        self.X = self.sb("X", TILES * D).rearrange("p (t d) -> p t d", t=TILES)
        self.XN = self.sb("XN", TILES * D).rearrange("p (t d) -> p t d", t=TILES)
        self.XT = self.sb("XT", DC * NT).rearrange("p (c n) -> p c n", c=DC)
        self.consts = self.sb("consts", max(c1 for _, _, c1 in at["const"].values()))
        self.stats = self.sb("stats", TILES * 6).rearrange("p (t k) -> p t k", t=TILES)
        self.meanvar = self.sb("meanvar", TILES * 2).rearrange("p (t k) -> p t k", t=TILES)
        self.rstd = self.sb("rstd", TILES)
        self.kern = self.sb("kern", DC * NS).rearrange("p (k l) -> p k l", k=DC)
        self.kern_ok = None
        self.areas = [self.sb(f"weights{i}", self.WEIGHTS) for i in range(2)]
        self.scratch = self.sb("scratch", self.SCRATCH)
        self.banks = Ring([Slot(ctx.enter_context(nc.psum_tensor(f"bank{i}", [P, HALF], F32))[:, :])
                           for i in range(8)])
        self.weight_sem = [self.new_sem(f"weights{i}_loaded") for i in range(2)]
        self.block_no = 0
        self.prefetched = None
        self.ends = []

    def sb(self, name, cols):
        return self.ctx.enter_context(self.nc.sbuf_tensor(name, [P, cols], F32))[:, :]

    def new_sem(self, name):
        return self.ctx.enter_context(self.nc.semaphore(name))

    def const(self, name):
        r, c0, c1 = self.at["const"][name]
        return self.consts[:r, c0:c1]

    def load_weights(self, name, area):
        cols = self.dram[f"w_{name}"].shape[1]
        assert cols <= self.WEIGHTS, (name, cols)
        sem, n = self.weight_sem[area], 16 * (self.loads.get(area, 0) + 1)
        self.loads[area] = self.loads.get(area, 0) + 1
        if len(self.ends) >= 1:
            self.sp.wait(self.ends[-1])
        self.sp.silent(lambda e: e.dma_start(self.areas[area][:, :cols], self.dram[f"w_{name}"]).then_inc(sem, 16))
        return (sem, n)

    loads = {}

    def begin(self, name, nxt):
        for q in (self.pe, self.dve, self.act, self.pool):
            q.sem, q.n = self.new_sem(f"{name}_{q.name}"), 0
            if self.ends:
                q.wait(self.ends[-1])
        area = self.block_no % 2
        self.w_ready = self.prefetched or self.load_weights(name, area)
        self.prefetched = self.load_weights(nxt, 1 - area) if nxt else None
        for q in (self.pe, self.dve, self.act, self.pool):
            q.wait(self.w_ready)
        self.area, self.name, self.used = self.areas[area], name, 0
        self.tail = self.WEIGHTS
        self.next = (nxt, self.areas[1 - area])
        self.block_no += 1
        for b in self.banks.slots:
            b.free = []

    def fence(self):
        now = [q.now() for q in (self.pe, self.dve, self.act, self.pool)]
        for q in (self.pe, self.dve, self.act, self.pool, self.sp):
            q.wait(now)

    def end(self):
        self.ends.append([q.now() for q in (self.pe, self.dve, self.act, self.pool)])

    def w(self, piece):
        r, c0, c1 = self.at[self.name][piece]
        return self.area[:r, c0:c1]

    def w_next(self, piece):
        name, area = self.next
        r, c0, c1 = self.at[name][piece]
        return area[:r, c0:c1]

    def wc(self, piece, k):
        return self.w(piece).rearrange("p (k n) -> p k n", k=k)

    def tmp(self, cols, rows=P):
        a = self.scratch[:rows, self.used:self.used + cols]
        self.used += cols
        assert self.used <= self.SCRATCH, (self.name, self.used)
        return a

    def spare(self, cols, rows=P):
        self.tail -= cols
        assert self.tail >= self.dram[f"w_{self.name}"].shape[1], self.name
        return self.area[:rows, self.tail:self.tail + cols]

    def mm(self, out, terms, *tickets):
        self.pe.wait(*tickets)
        for i, (l, r) in enumerate(terms):
            last = i == len(terms) - 1
            f = lambda e, l=l, r=r, i=i, last=last: e.matmul(out, lhsT=l, rhs=r, start=i == 0, stop=last)
            t = self.pe(f) if last else self.pe.silent(f)
        return t

    def transpose(self, out, in_, *tickets):
        k = in_.shape[0]
        return self.pe(lambda e: e.transpose(out, in_, self.const("eye")[:k, :k]), *tickets)

    def copy(self, q, out, in_, *tickets):
        if q is self.act:
            return q(lambda e: e.activation(out, in_, ACT.Copy), *tickets)
        return q(lambda e: e.tensor_copy(out, in_), *tickets)

    def tt(self, out, a, b, op, *tickets, q=None):
        return (q or self.dve)(lambda e: e.tensor_tensor(out, a, b, op), *tickets)

    def ts(self, out, a, s1, s2, op0, op1, *tickets, q=None):
        if op1 is None:
            return (q or self.dve)(lambda e: e.tensor_scalar(out, a, s1, None, op0), *tickets)
        return (q or self.dve)(lambda e: e.tensor_scalar(out, a, s1, s2, op0, op1), *tickets)

    def stt(self, out, a, s, b, op0, op1, *tickets):
        return self.dve(lambda e: e.scalar_tensor_tensor(out=out, in0=a, scalar=s, in1=b, op0=op0, op1=op1),
                        *tickets)

    def recip(self, x, *tickets, out=None):
        out = x if out is None else out
        return self.dve(lambda e: e.reciprocal(out, x), *tickets)

    def power(self, x, which, *tickets, out=None):
        out = x if out is None else out
        return self.tt(out, x, self.const(which)[:x.shape[0], :x.shape[1]], ALU.pow, *tickets, q=self.pool)

    def reduce(self, out, in_, op, *tickets):
        return self.dve(lambda e: e.tensor_reduce(out, in_, AX.X, op), *tickets)

    def af(self, out, in_, func, *tickets, bias=0.0, scale=1.0, accum=None):
        if accum is None:
            return self.act(lambda e: e.activation(out, in_, func, bias=bias, scale=scale), *tickets)
        return self.act(lambda e: e.activation(out, in_, func, bias=bias, scale=scale, accum_out=accum), *tickets)


    def normalise(self, src, dst, *tickets):
        for t in range(TILES):
            st = self.dve(lambda e, t=t: e.bn_stats(self.stats[:, t, :], src[:, t, :]), *tickets)
        for t in range(TILES):
            st = self.dve(lambda e, t=t: e.bn_aggr(self.meanvar[:, t, :], self.stats[:, t, :]), st)
        r = self.ts(self.rstd, self.meanvar[:, :, 1], LN_EPS, None, ALU.add, None, st)
        r = self.power(self.rstd, "mhalf", r)
        return [self.ts(dst[:, t, :], src[:, t, :], self.meanvar[:, t, 0:1], self.rstd[:, t:t + 1],
                        ALU.subtract, ALU.mult, r) for t in range(TILES)]

    def to_features(self, src, dst, src_ready, gain=None, shift=None, *tickets):
        done = []
        for c in range(DC):
            for h in range(2):
                b = self.banks.next()
                for j in range(4):
                    t = 4 * h + j
                    tr = self.transpose(b.t[:, j * P:(j + 1) * P], src[:, t, c * P:(c + 1) * P],
                                        b.free, src_ready[t], *tickets)
                o = dst[:, c, h * HALF:(h + 1) * HALF]
                if gain is not None:
                    d = self.ts(o, b.t, gain[:, c:c + 1], shift[:, c:c + 1], ALU.mult, ALU.add, tr)
                else:
                    d = self.copy(self.act if h else self.dve, o, b.t, tr)
                b.free = [d]
                done.append(d)
        return done

    def enter(self):
        ready = self.normalise(self.X, self.XN)
        return ready, self.to_features(self.XN, self.XT, ready)

    def project(self, dst, w, k, src, outs, ready, bias=None, scale=None, func=None):
        done = []
        for o in range(outs):
            for h in range(2):
                b = self.banks.next()
                cols = slice(h * HALF, (h + 1) * HALF)
                m = self.mm(b.t, [(w[:, c, o * P:(o + 1) * P], src[:, c, cols]) for c in range(k)],
                            b.free, ready, self.w_ready)
                bb = 0.0 if bias is None else bias[:, o:o + 1]
                if func is not None:
                    d = self.af(dst[:, o, cols], b.t, func, m, bias=bb)
                elif bias is None:
                    d = self.copy(self.act if (o + h) % 2 else self.dve, dst[:, o, cols], b.t, m)
                else:
                    d = self.ts(dst[:, o, cols], b.t, bb, None, ALU.add, None, m)
                b.free = [d]
                done.append(d)
        return done

    def add_output(self, src, w, k, ready, bias=None, tiles=range(TILES), cols=None):
        done = []
        for t in tiles:
            b = self.banks.next()
            o = b.t[:, :D]
            sel = cols if cols is not None else slice(t * P, (t + 1) * P)
            terms = [(src[:, c, sel], w[:, c, :]) for c in range(k)]
            if bias is not None:
                terms.append((self.const("ones")[0:1, :P], bias))
            m = self.mm(o, terms, b.free, ready, self.w_ready)
            d = self.tt(self.X[:, t, :], o, self.X[:, t, :], ALU.add, m)
            b.free = [d]
            done.append(d)
        return done


def l1_ffn(c):
    E, F = 8, 688
    FC = -(-F // P)
    sizes = [min(P, F - P * f) for f in range(FC)]
    stream = [Slot(c.tmp(2 * DC * F + FC * D), c.new_sem(f"expert_weights{i}")) for i in range(2)]
    loaded = []

    def load(e):
        s = stream[e % 2]
        c.sp.wait(s.free)
        c.sp.silent(lambda q: q.dma_start(s.t, c.dram["s_Wgu"][e]).then_inc(s.sem, 16))
        s.n += 16
        loaded.append((s.sem, s.n))

    c.sp.wait(c.ends[-1] if c.ends else None)
    load(0)
    load(1)
    ready, xt = c.enter()
    logit = c.tmp(TILES * E).rearrange("p (t e) -> p t e", t=TILES)
    top = c.tmp(TILES * 8).rearrange("p (t e) -> p t e", t=TILES)
    idx = c.tmp(TILES * 8).bitcast(U32).rearrange("p (t e) -> p t e", t=TILES)
    idf = c.tmp(TILES * 8).rearrange("p (t e) -> p t e", t=TILES)
    comb = c.tmp(TILES * E).rearrange("p (t e) -> p t e", t=TILES)
    hot = c.tmp(TILES * E).rearrange("p (t e) -> p t e", t=TILES)
    wt = c.tmp(TILES * 2).rearrange("p (t k) -> p t k", t=TILES)
    b = c.banks.next()
    for t in range(TILES):
        m = c.mm(b.t[:, t * E:(t + 1) * E],
                 [(c.XT[:, k, t * P:(t + 1) * P], c.wc("ws", DC)[:, k, :]) for k in range(DC)]
                 + [(c.const("ones")[0:1, :P], c.w("bs"))], b.free, xt, c.w_ready)
    cp = c.copy(c.dve, logit, b.t[:, :TILES * E], m)
    b.free = [cp]
    for t in range(TILES):
        mx = c.dve(lambda e, t=t: e.max(top[:, t, :], logit[:, t, :]), cp)
        mi = c.dve(lambda e, t=t: e.max_index(idx[:, t, :], top[:, t, :], logit[:, t, :]), mx)
    ix = c.copy(c.dve, idf, idx, mi)
    d1 = c.tt(wt[:, :, 1], top[:, :, 1], top[:, :, 0], ALU.subtract, mx)
    ex = c.af(wt[:, :, 1], wt[:, :, 1], ACT.Exp, d1)
    s1 = c.ts(wt[:, :, 0], wt[:, :, 1], 1.0, None, ALU.add, None, ex)
    s2 = c.dve(lambda e: e.reciprocal(wt[:, :, 0], wt[:, :, 0]), s1)
    s3 = c.tt(wt[:, :, 1], wt[:, :, 1], wt[:, :, 0], ALU.mult, s2)
    for t in range(TILES):
        h1 = c.ts(comb[:, t, :], c.const("iota8"), idf[:, t, 0:1], wt[:, t, 0:1], ALU.is_equal, ALU.mult, ix, s3)
        h2 = c.ts(hot[:, t, :], c.const("iota8"), idf[:, t, 1:2], wt[:, t, 1:2], ALU.is_equal, ALU.mult, ix, s3)
    comb_ready = c.tt(comb, comb, hot, ALU.add, h1, h2)
    hid = c.tmp(FC * NT).rearrange("p (f n) -> p f n", f=FC)
    gact = Ring([Slot(c.tmp(HALF)) for _ in range(4)])
    hid_free = [[], []]
    for e_ in range(E):
        s = stream[e_ % 2]
        wg = s.t[:, :DC * F].rearrange("p (k f) -> p k f", k=DC)
        wu = s.t[:, DC * F:2 * DC * F].rearrange("p (k f) -> p k f", k=DC)
        wd = s.t[:, 2 * DC * F:].rearrange("p (k d) -> p k d", k=FC)
        hid_done = [[], []]
        for h in range(2):
            cols = slice(h * HALF, (h + 1) * HALF)
            for f in range(FC):
                n = sizes[f]
                bg, bu = c.banks.next(), c.banks.next()
                mg = c.mm(bg.t[:n], [(wg[:, k, f * P:f * P + n], c.XT[:, k, cols]) for k in range(DC)],
                          bg.free, xt, loaded[e_])
                mu = c.mm(bu.t[:n], [(wu[:, k, f * P:f * P + n], c.XT[:, k, cols]) for k in range(DC)],
                          bu.free)
                g = gact.next()
                a = c.af(g.t[:n], bg.t[:n], ACT.Silu, mg, g.free)
                bg.free = [a]
                v = c.tt(hid[:n, f, cols], g.t[:n], bu.t[:n], ALU.mult, a, mu, hid_free[h])
                g.free = bu.free = [v]
                hid_done[h].append(v)
        for h in range(2):
            for t in range(4 * h, 4 * h + 4):
                b = c.banks.next()
                m = c.mm(b.t[:, :D], [(hid[:sizes[f], f, t * P:(t + 1) * P], wd[:sizes[f], f, :])
                                      for f in range(FC)], b.free, hid_done[h])
                v = c.stt(c.X[:, t, :], b.t[:, :D], comb[:, t, e_:e_ + 1], c.X[:, t, :],
                          ALU.mult, ALU.add, m, comb_ready, ready, last_x[t] if e_ else None)
                if t == 0:
                    nxt = []
                nxt.append(v)
                b.free = [v]
            hid_free[h] = [m]
        last_x = nxt
        s.free = [m]
        if e_ + 2 < E:
            load(e_ + 2)


def phase_sin(c, out, y, tmp, shift, ready):
    a = c.ts(out, y, 1.0, shift, ALU.mult, ALU.add, ready)
    n = c.ts(tmp, out, 1.0 / (2.0 * np.pi), ROUND, ALU.mult, ALU.add, a)
    n = c.ts(tmp, tmp, ROUND, None, ALU.subtract, None, n)
    r = c.stt(out, tmp, -TWO_PI_HI, out, ALU.mult, ALU.add, n)
    r = c.stt(out, tmp, -TWO_PI_LO, out, ALU.mult, ALU.add, r)
    r = c.ts(out, out, PI_CLAMP, -PI_CLAMP, ALU.min, ALU.max, r)
    return c.af(out, out, ACT.Sin, r)


def l2_attn(c):
    big = lambda: c.tmp(DC * NT).rearrange("p (k n) -> p k n", k=DC)
    flat = lambda a: a.rearrange("p k n -> p (k n)")
    ready, xt = c.enter()
    key, val, qry, kp, qp, cs, tmp = (big() for _ in range(7))
    k = c.project(key, c.wc("wk", DC), DC, c.XT, DC, xt, bias=c.w("bk"))
    v = c.project(val, c.wc("wv", DC), DC, c.XT, DC, xt, bias=c.w("bv"))
    q = c.project(qry, c.wc("wq", DC), DC, c.XT, DC, xt, bias=c.w("bq"))
    kt = c.project(kp, c.wc("wkp", DC), DC, key, DC, k, bias=c.w("bkp"), func=ACT.Tanh)
    qt = c.project(qp, c.wc("wqp", DC), DC, qry, DC, q, bias=c.w("bqp"), func=ACT.Tanh)
    for i in range(DC):
        kt.append(c.ts(kp[:, i], kp[:, i], c.w("phase_scale")[:, i:i + 1], None, ALU.mult, None, kt))
        qt.append(c.ts(qp[:, i], qp[:, i], c.w("phase_scale")[:, i:i + 1], None, ALU.mult, None, qt))
    last = [kt, qt]
    for phase, shift, mem in ((kp, np.pi / 2, key), (kp, 0.0, qry)):
        s = phase_sin(c, flat(cs), flat(phase), flat(tmp), shift, last)
        m = c.tt(flat(cs), flat(cs), flat(val), ALU.mult, s, v)
        last = []
        for i in range(DC):
            last.append(c.dve(lambda e, i=i, mem=mem: e.tensor_tensor_scan(
                mem[:, i], c.const("not_first"), cs[:, i], 0.0, ALU.mult, ALU.add), m))
    s = phase_sin(c, flat(cs), flat(qp), flat(tmp), np.pi / 2, last)
    m = c.tt(flat(key), flat(key), flat(cs), ALU.mult, s)
    s = phase_sin(c, flat(cs), flat(qp), flat(tmp), 0.0, m)
    m = c.tt(flat(qry), flat(qry), flat(cs), ALU.mult, s)
    m = c.tt(flat(key), flat(key), flat(qry), ALU.add, m)
    r = c.ts(flat(key), flat(key), 1.0 / np.sqrt(D), None, ALU.mult, None, m)
    tm = val.rearrange("p k n -> p (k n)").rearrange("p (t d) -> p t d", t=TILES)
    back = to_tokens(c, key, tm, [r] * DC)
    tm2 = kp.rearrange("p k n -> p (k n)").rearrange("p (t d) -> p t d", t=TILES)
    n = c.normalise(tm, tm2, back)
    f = c.to_features(tm2, qp, n, c.w("ln_g"), c.w("ln_b"), s)
    c.add_output(qp, c.wc("wo", DC), DC, [f, ready], c.w("bo"))
    for t in range(TILES):
        c.tt(c.X[:, t, :], c.X[:, t, :], c.XN[:, t, :], ALU.add, c.dve.now())


def to_tokens(c, src, dst, ready):
    done = []
    for t in range(0, TILES, 2):
        b = c.banks.next()
        for j in range(2):
            for k in range(DC):
                tr = c.transpose(b.t[:, j * D + k * P:j * D + (k + 1) * P],
                                 src[:, k, (t + j) * P:(t + j + 1) * P], b.free, ready[k])
        d = c.copy(c.act if t % 4 else c.dve, dst[:, t:t + 2, :], b.t, tr)
        b.free = [d]
        done.append(d)
    return done


def global_max(c, parts, ready):
    one, allp = c.tmp(1), c.tmp(1)
    line = c.tmp(P, 1)
    m = c.reduce(one, parts, ALU.max, ready)
    b = c.banks.next()
    t = c.transpose(b.t[0:1, :P], one, b.free, m)
    m = c.reduce(line[:, 0:1], b.t[0:1, :P], ALU.max, t)
    t = c.mm(b.t[:, 256:257], [(c.const("ones")[0:1, :P], line[:, 0:1])], m)
    m = c.copy(c.dve, allp, b.t[:, 256:257], t)
    b.free = [m]
    return allp, m


def absmax(c, out, in_, ready):
    return c.dve(lambda e: e.tensor_reduce(out, in_, AX.X, ALU.max, apply_absolute_value=True), ready)


def l2_ffn(c):
    FP8_MAX = 448.0
    ready, xt = c.enter()

    def quantise(x, n, ready):
        q, step = c.tmp(n), c.tmp(n)
        out = c.tmp(n // 2).bitcast(BF16)
        part, sc, inv = c.tmp(1), c.tmp(1), c.tmp(1)
        a = absmax(c, part, x, ready)
        big, a = global_max(c, part, a)
        a = c.ts(sc, big, 1e-12, None, ALU.max, None, a)
        a = c.recip(sc, a)
        a = c.ts(sc, sc, FP8_MAX, FP8_MAX, ALU.mult, ALU.min, a)
        i = c.recip(sc, a, out=inv)
        a = c.ts(q, x, sc, FP8_MAX, ALU.mult, ALU.min, a)
        a = c.ts(q, q, -FP8_MAX, None, ALU.max, None, a)
        b = c.dve(lambda e: e.tensor_scalar(step.bitcast(U32), q.bitcast(U32), 0x7F800000, None,
                                            ALU.bitwise_and), a)
        b = c.ts(step, step, 2.0 ** -6, 1.5 * 2.0 ** 20, ALU.max, ALU.mult, b)
        b = c.tt(q, q, step, ALU.add, b)
        b = c.tt(out, q, step, ALU.subtract, b)
        return out, inv, [b, i]

    wq, w_inv, wr = quantise(c.w("w"), DC * D, c.w_ready)
    xq, x_inv, xr = quantise(c.XT.rearrange("p c n -> p (c n)"), DC * NT, xt)
    wq = wq.rearrange("p (c n) -> p c n", c=DC)
    xq = xq.rearrange("p (c n) -> p c n", c=DC)
    sc = c.tmp(1)
    s = c.tt(sc, w_inv, x_inv, ALU.mult, wr, xr)
    res = Ring([Slot((c.tmp(D), c.tmp(D // 2).bitcast(BF16))) for _ in range(2)])
    for t in range(TILES):
        b = c.banks.next()
        m = c.mm(b.t[:, :D], [(xq[:, k, t * P:(t + 1) * P], wq[:, k, :]) for k in range(DC)], b.free, wr, xr)
        r = res.next()
        y, yb = r.t
        d = c.stt(y, b.t[:, :D], sc, c.w("bias"), ALU.mult, ALU.add, m, s, r.free)
        b.free = [d]
        d = c.copy(c.dve, yb, y, d)
        r.free = [c.tt(c.X[:, t, :], yb, c.X[:, t, :], ALU.add, d)]


def l3_ffn(c):
    H, HC, BLK = 768, 6, 32
    QMAX = 32767.0
    ready, xt = c.enter()
    one = c.const("ones")[:, 0:1]

    def dequant(w, cols, ready):
        nb = cols // BLK
        s, inv = c.tmp(nb), c.tmp(nb)
        sb, ib = (v.rearrange("p (b o) -> p b o", o=1).to_broadcast([P, nb, BLK]) for v in (s, inv))
        wv = w.rearrange("p (b k) -> p b k", k=BLK)
        a = absmax(c, s, wv, ready)
        a = c.ts(s, s, 1.0 / 7.0, 1e-12, ALU.mult, ALU.max, a)
        a = c.recip(s, a, out=inv)
        a = c.tt(wv, wv, ib, ALU.mult, a)
        a = c.ts(w, w, ROUND, None, ALU.add, None, a)
        a = c.ts(w, w, ROUND, None, ALU.subtract, None, a)
        a = c.ts(w, w, 7.0, -8.0, ALU.min, ALU.max, a)
        return c.tt(wv, wv, sb, ALU.mult, a)

    def flip(w, rows, cols, ready):
        rc, cc = rows // P, cols // P
        src = w.rearrange("p (r n) -> p r n", r=rc)
        dst = c.tmp(rows * cc).rearrange("p (k r) -> p k r", k=cc)
        done = []
        for k in range(cc):
            for r0 in range(0, rc, 4):
                b = c.banks.next()
                n = min(4, rc - r0)
                for r in range(n):
                    tr = c.transpose(b.t[:, r * P:(r + 1) * P], src[:, r0 + r, k * P:(k + 1) * P], b.free, ready)
                d = c.copy(c.act, dst[:, k, r0 * P:(r0 + n) * P], b.t[:, :n * P], tr)
                b.free = [d]
                done.append(d)
        return dst, done

    def act_scale(parts, ready):
        big, a = global_max(c, parts, ready)
        sc = c.tmp(1)
        a = c.ts(sc, big, 1.0 / QMAX, 1e-12, ALU.mult, ALU.max, a)
        inv = c.tmp(1)
        return (sc, inv), c.recip(sc, a, out=inv)

    def qdq(x, sc, ready):
        scale, inv = sc
        a = c.ts(x, x, inv, ROUND, ALU.mult, ALU.add, ready)
        a = c.ts(x, x, ROUND, QMAX, ALU.subtract, ALU.min, a)
        return c.ts(x, x, -QMAX - 1.0, scale, ALU.max, ALU.mult, a)

    wg, gr = flip(c.w("gate"), H, D, dequant(c.w("gate"), HC * D, c.w_ready))
    wu, ur = flip(c.w("up"), H, D, dequant(c.w("up"), HC * D, c.w_ready))
    wd, dr = flip(c.w("down"), D, H, dequant(c.w("down"), DC * H, c.w_ready))
    part = c.tmp(1)
    x = c.XT.rearrange("p c n -> p (c n)")
    sc, a = act_scale(part, absmax(c, part, x, xt))
    xq = qdq(x, sc, a)
    up = c.tmp(HC * NT).rearrange("p (f n) -> p f n", f=HC)
    gate = c.tmp(HC * NT).rearrange("p (f n) -> p f n", f=HC)
    parts = c.tmp(HC), c.tmp(HC)

    def branch(y, w, part, wr):
        d = c.project(y, w, DC, c.XT, HC, [xq, wr])
        m = [absmax(c, part[:, f:f + 1], y[:, f], d) for f in range(HC)]
        sc, a = act_scale(part, m)
        return [qdq(y[:, f], sc, a) for f in range(HC)]

    g = branch(gate, wg, parts[0], gr)
    u = branch(up, wu, parts[1], ur)
    sig = Ring([Slot(c.tmp(NT)) for _ in range(1)])
    m = []
    for f in range(HC):
        s = sig.next()
        a = c.af(s.t, gate[:, f], ACT.Sigmoid, g[f], s.free)
        a = c.ts(s.t, s.t, 65536.0, ROUND, ALU.mult, ALU.add, a)
        a = c.ts(s.t, s.t, ROUND, 65535.0, ALU.subtract, ALU.min, a)
        a = c.ts(s.t, s.t, 0.0, 1.0 / 65536.0, ALU.max, ALU.mult, a)
        a = c.tt(gate[:, f], gate[:, f], s.t, ALU.mult, a)
        s.free = [a]
        m.append(absmax(c, parts[0][:, f:f + 1], gate[:, f], a))
    sc, a = act_scale(parts[0], m)
    m = []
    for f in range(HC):
        b = qdq(gate[:, f], sc, a)
        b = c.tt(gate[:, f], gate[:, f], up[:, f], ALU.mult, b, u)
        m.append(absmax(c, parts[1][:, f:f + 1], gate[:, f], b))
    sc, a = act_scale(parts[1], m)
    o = [qdq(gate[:, f], sc, a) for f in range(HC)]
    c.add_output(gate, wd, HC, [o, dr])



def each(a, n):
    m = a.shape[1]
    return a.rearrange("p (m o) -> p m o", o=1).to_broadcast([P, m, n])


def rows_of(a, m):
    n = a.shape[1]
    return a.rearrange("p (o n) -> p o n", o=1).to_broadcast([P, m, n])


def softmax_rows(c, s3, n, ready, normalise=True):
    m = s3.shape[1]
    mx, sm = c.tmp(m), c.tmp(m)
    a = c.reduce(mx, s3, ALU.max, ready)
    a = c.tt(s3, s3, each(mx, n), ALU.subtract, a)
    a = c.af(s3, s3, ACT.Exp, a)
    a = c.reduce(sm, s3, ALU.add, a)
    a = c.recip(sm, a)
    if normalise:
        a = c.tt(s3, s3, each(sm, n), ALU.mult, a)
    return a, sm


def l0_attn(c):
    H, DK = 16, 64
    HC = H * DK // P
    ready, xt = c.enter()
    q3 = c.tmp(HC * NT).rearrange("p (k n) -> p k n", k=HC)
    k3 = c.tmp(HC * NT).rearrange("p (k n) -> p k n", k=HC)
    q = c.project(q3, c.wc("wq", DC), DC, c.XT, HC, xt)
    k = c.project(k3, c.wc("wk", DC), DC, c.XT, HC, xt)
    wv = c.wc("wv", DC)
    slots = Ring([Slot((c.tmp(H * NS), c.tmp(H), c.tmp(H), c.tmp(H))) for _ in range(2)])
    vals = Ring([Slot(c.tmp(H * DK)) for _ in range(2)])
    outs = Ring([Slot(c.tmp(HC * P)) for _ in range(2)])
    own_buf = Slot(c.tmp(H * NS))
    for t in range(TILES):
        sl = slots.next()
        sc, mx, sm, own = sl.t
        s3 = sc.rearrange("p (h n) -> p h n", h=H)
        a = []
        for odd in range(2):
            b = c.banks.next()
            r = slice(odd * DK, odd * DK + DK)
            for s in range(BT):
                cols = slice(t * P + s * NS, t * P + (s + 1) * NS)
                for i in range(H // 2):
                    m = c.mm(b.t[s * NS:(s + 1) * NS, i * NS:(i + 1) * NS],
                             [(q3[r, i, cols], k3[r, i, cols])], b.free, q, k)
            d = c.stt(s3[:, odd::2], b.t[:, :H // 2 * NS].rearrange("p (h n) -> p h n", n=NS), float(np.sqrt(DK)),
                      rows_of(c.const("causal_neg"), H // 2), ALU.mult, ALU.add, m, sl.free)
            b.free = [d]
            a.append(d)
        a = c.reduce(mx, s3, ALU.max, a)
        a = c.tt(s3, s3, each(mx, NS), ALU.subtract, a)
        a = c.af(s3, s3, ACT.Exp, a)
        a1 = c.reduce(sm, s3, ALU.add, a)
        a1 = c.recip(sm, a1)
        o3 = own_buf.t.rearrange("p (h n) -> p h n", h=H)
        a2 = c.tt(o3, s3, rows_of(c.const("diag32"), H), ALU.mult, a, own_buf.free)
        a2 = c.reduce(own, o3, ALU.add, a2)
        own_buf.free = [a2]
        a = c.tt(own, own, sm, ALU.mult, a1, a2)
        v = vals.next()
        vd = []
        for half in range(2):
            b = c.banks.next()
            m = c.mm(b.t, [(c.XT[:, i, t * P:(t + 1) * P], wv[:, i, half * HALF:(half + 1) * HALF])
                           for i in range(DC)], b.free, xt)
            n = HALF // DK
            d = c.tt(v.t[:, half * HALF:(half + 1) * HALF].rearrange("p (h d) -> p h d", h=n),
                     b.t.rearrange("p (h d) -> p h d", h=n), each(own[:, half * n:(half + 1) * n], DK),
                     ALU.mult, m, a, v.free)
            b.free = [d]
            vd.append(d)
        sl.free = [d]
        o = outs.next()
        od = []
        for half in range(2):
            b = c.banks.next()
            for i in range(4):
                m = c.transpose(b.t[:, i * P:(i + 1) * P], v.t[:, half * HALF + i * P:half * HALF + (i + 1) * P],
                                b.free, vd[half])
            d = c.copy(c.act, o.t[:, half * HALF:(half + 1) * HALF], b.t, m, o.free)
            b.free = [d]
            od.append(d)
        v.free = [m]
        c.add_output(o.t.rearrange("p (k n) -> p k n", k=HC), c.wc("wo", HC), HC, od, tiles=[t], cols=slice(0, P))
        o.free = [c.pe.now()]


def l0_ffn(c):
    E, HC = 8, 8
    w1_ring = Ring([Slot(c.tmp(E * DC * P), c.new_sem(f"hidden_weights{i}")) for i in range(2)])
    c.sp.wait(c.ends[-1] if c.ends else None)

    def load(ring, src):
        s = ring.next()
        c.sp.wait(s.free)
        c.sp.silent(lambda q: q.dma_start(s.t, src).then_inc(s.sem, 16))
        s.n += 16
        return s, (s.sem, s.n)

    first = [load(w1_ring, c.dram["s_eW1"][i]) for i in range(2)]
    ready, xt = c.enter()
    hid = c.tmp(HC * NT).rearrange("p (k n) -> p k n", k=HC)
    h = hid[:, 0:DC]
    d = c.project(h, c.wc("gw1", DC), DC, c.XT, DC, xt, bias=c.w("gb1"), func=ACT.Relu)
    mean = c.tmp(DC * NB).rearrange("p (k b) -> p k b", k=DC)
    for k in range(DC):
        a = c.reduce(mean[:, k], h[:, k].rearrange("p (s b) -> p b s", b=NB), ALU.add, d)
    a = c.ts(mean, mean, 1.0 / NS, None, ALU.mult, None, a)
    rep = c.tmp(DC * P).rearrange("p (k s b) -> p k s b", k=DC, s=BT)
    for k in range(DC):
        r = c.copy(c.dve, rep[:, k], rows_of(mean[:, k], BT), a)
    gate_tok, gate_row = c.tmp(E), c.tmp(E * NB)
    gate_col = c.tmp(HALF, E)
    b = c.banks.next()
    rep2 = rep.rearrange("p k s b -> p k (s b)")
    c.mm(b.t[:, 0:E], [(rep2[:, k], c.wc("gw2", DC)[:, k]) for k in range(DC)], b.free, r)
    c.mm(b.t[0:E, 32:32 + NB], [(c.wc("gw2", DC)[:, k], mean[:, k]) for k in range(DC)])
    gw = c.w("gw2b").rearrange("p (k e m) -> p k e m", k=DC, e=E)
    for e in range(E):
        m3 = c.mm(b.t[:, 64 + e * NB:64 + (e + 1) * NB], [(gw[:, k, e], mean[:, k]) for k in range(DC)])
    g1 = c.tt(gate_tok, b.t[:, 0:E], c.w("gb2w"), ALU.add, m3)
    g2 = c.ts(gate_col.rearrange("p (s b) -> p s b", b=NB),
              b.t[0:E, 32:32 + NB].rearrange("p (o b) -> p o b", o=1).to_broadcast([E, HALF // NB, NB]),
              c.w("gb2"), None, ALU.add, None, m3)
    gr3 = gate_row.rearrange("p (e b) -> p e b", e=E)
    g3 = c.tt(gr3, b.t[:, 64:64 + E * NB].rearrange("p (e b) -> p e b", e=E), each(c.w("gb2w"), NB), ALU.add, m3)
    b.free = [g1, g2, g3]
    xs = c.tmp(E * DC * HALF)
    xs4 = xs.rearrange("p (e k n) -> p e k n", e=E, k=DC)
    xs_free, hid_done = [], []
    for half in range(2):
        cols = slice(half * HALF, (half + 1) * HALF)
        sd = []
        for e in range(E):
            for k in range(DC):
                sd.append(c.tt(xs4[:, e, k].rearrange("p (s b) -> p s b", b=NB),
                               c.XT[:, k, cols].rearrange("p (s b) -> p s b", b=NB),
                               rows_of(gr3[:, e], HALF // NB), ALU.mult, g3, xt, xs_free,
                               q=c.pool if k else c.dve))
        if half == 0 and c.next[0] == "L1_xattn":
            s4d_kernel(c, c.w_next, lambda n: c.spare(n) if c.tail - n > 4200 else c.tmp(n), c.prefetched)
        for f in range(HC):
            s, got = first.pop(0)
            w = s.t.rearrange("p (e k n) -> p e k n", e=E, k=DC)
            b = c.banks.next()
            m = c.mm(b.t, [(w[:, e, k], xs4[:, e, k]) for e in range(E) for k in range(DC)]
                     + [(c.w("eb1")[:, f * P:(f + 1) * P], gate_col)], b.free, sd, got, g2)
            d = c.af(hid[:, f, cols], b.t, ACT.Relu, m)
            b.free = [d]
            hid_done.append(d)
            s.free = [m]
            if half * HC + f + 2 < 2 * HC:
                first.append(load(w1_ring, c.dram["s_eW1"][(f + 2) % HC]))
        xs_free = [m]
    w2_ring = Ring([Slot(xs[:, i * HC * HALF:(i + 1) * HC * HALF], c.new_sem(f"output_weights{i}")) for i in range(2)])
    for s in w2_ring.slots:
        s.free = [m]
    nxt = [load(w2_ring, c.dram["s_eW2"][i]) for i in range(2)]
    x_done = [[] for _ in range(TILES)]
    for t in range(TILES):
        b = c.banks.next()
        m = c.mm(b.t[:, :D], [(gate_col[:, :P], c.w("eb2"))], b.free, g2)
        x_done[t] = b.free = [c.tt(c.X[:, t], b.t[:, :D], c.X[:, t], ALU.add, m, ready)]
    for p_ in range(E // 2):
        s, got = nxt.pop(0)
        w = s.t.rearrange("p (k n) -> p k n", k=HC)
        for t in range(TILES):
            b = c.banks.next()
            m = c.mm(b.t, [(hid[:, k, t * P:(t + 1) * P], w[:, k]) for k in range(HC)], b.free, hid_done, got)
            for i in range(2):
                e = 2 * p_ + i
                x_done[t] = c.stt(c.X[:, t], b.t[:, i * D:(i + 1) * D], gate_tok[:, e:e + 1], c.X[:, t],
                                  ALU.mult, ALU.add, m, g1, x_done[t])
            b.free = [x_done[t]]
        s.free = [m]
        if p_ + 2 < E // 2:
            nxt.append(load(w2_ring, c.dram["s_eW2"][p_ + 2]))


def l1_attn(c):
    H, DH, EPS = 16, 16, 1e-5
    NH = TILES * H
    ready, xt = c.enter()

    def softplus(x):
        y, z = c.tmp(1), c.tmp(1)
        a = c.ts(y, x, -1.0, None, ALU.mult, None, c.w_ready)
        a = c.tt(y, y, x, ALU.min, a)
        a = c.af(y, y, ACT.Exp, a)
        a = c.af(y, y, ACT.Ln, a, bias=1.0)
        a2 = c.ts(z, x, 0.0, None, ALU.max, None, c.w_ready)
        return z, c.tt(z, z, y, ALU.add, a, a2)

    cc, a0 = softplus(c.w("logc"))
    bp, a1 = softplus(c.w("beta"))
    rc, irc, edge, negc, twoc, slope, negab = (c.tmp(1) for _ in range(7))
    a = c.af(rc, cc, ACT.Sqrt, a0)
    a = c.recip(rc, a, out=irc)
    consts = [c.ts(edge, irc, EPS, None, ALU.subtract, None, a),
              c.ts(negc, cc, -1.0, None, ALU.mult, None, a0),
              c.ts(twoc, cc, 2.0, None, ALU.mult, None, a0),
              c.ts(slope, bp, irc, -1.0, ALU.mult, ALU.mult, a, a1),
              c.ts(negab, c.w("ab"), -1.0, None, ALU.mult, None, c.w_ready)]

    tok = lambda a: a.rearrange("p (t d) -> p t d", t=TILES)
    heads = lambda a: a.rearrange("p t (h d) -> p (t h) d", h=H)
    qkv, done = [], []
    for n in ("wq", "wk", "wv"):
        dst = tok(c.tmp(TILES * D))
        dd = []
        for t in range(0, TILES, 2):
            b = c.banks.next()
            for j in range(2):
                m = c.mm(b.t[:, j * D:(j + 1) * D],
                         [(c.XT[:, k, (t + j) * P:(t + j + 1) * P], c.wc(n, DC)[:, k]) for k in range(DC)],
                         b.free, xt)
            d = c.copy(c.act if t % 4 else c.dve, dst[:, t:t + 2], b.t, m)
            b.free = [d]
            dd.append(d)
        qkv.append(dst)
        done.append(dd)
    sq = tok(c.tmp(TILES * D))

    def norm2(v, ready):
        n2 = c.tmp(NH)
        a = c.tt(sq, v, v, ALU.mult, ready, c.dve.now())
        return n2, c.reduce(n2, heads(sq), ALU.add, a)

    def exp_factor(n2, ready):
        vn, f = c.tmp(NH), c.tmp(NH)
        a = c.af(vn, n2, ACT.Sqrt, ready)
        a = c.ts(vn, vn, EPS, rc, ALU.max, ALU.mult, a, consts)
        a = c.af(f, vn, ACT.Tanh, a)
        a = c.recip(vn, a)
        return f, c.tt(f, f, vn, ALU.mult, a)

    def log_factor(n2, ready):
        y, z, g = c.tmp(NH), c.tmp(NH), c.tmp(NH)
        a = c.af(y, n2, ACT.Sqrt, ready)
        a = c.ts(y, y, EPS, None, ALU.max, None, a)
        b = c.ts(z, y, edge, rc, ALU.min, ALU.mult, a, consts)
        a = c.ts(y, y, rc, 2.0, ALU.mult, ALU.mult, b)
        a = c.recip(y, a)
        b = c.ts(g, z, -1.0, 1.0, ALU.mult, ALU.add, b)
        b = c.recip(g, b)
        b = c.stt(g, z, 1.0, g, ALU.add, ALU.mult, b)
        b = c.af(g, g, ACT.Ln, b)
        return g, c.tt(g, g, y, ALU.mult, a, b)

    def times(v, f, ready):
        return c.tt(heads(v), heads(v), each(f, DH), ALU.mult, ready)

    def to_ball_and_back(v, ready):
        n2, a = norm2(v, ready)
        f, b = exp_factor(n2, a)
        a = times(v, f, b)
        n2, a = norm2(v, a)
        f, b = log_factor(n2, a)
        return times(v, f, b)

    q, k, v = qkv
    sides = []
    for x, d in ((q, done[0]), (k, done[1])):
        n2, a = norm2(x, d)
        f, a = exp_factor(n2, a)
        a = times(x, f, a)
        n2, b = norm2(x, a)
        sides.append((n2, b, a))
    vdone = to_ball_and_back(v, done[2])
    (xns, xns_ok, q_ok), (_, kb, k_ok) = sides
    onemc = c.tmp(NH)
    om = c.ts(onemc, xns, negc, 1.0, ALU.mult, ALU.add, xns_ok, consts)
    qT = c.XT
    kT = c.XN.rearrange("p t d -> p (t d)").rearrange("p (k n) -> p k n", k=DC)
    qd = c.to_features(q, qT, [[q_ok, m]] * TILES)
    kd = c.to_features(k, kT, [[k_ok, xt]] * TILES)
    work = q.rearrange("p t d -> p (t d)"), k.rearrange("p t d -> p (t d)")
    kbd = Slot(work[0].rearrange("p (k h n) -> p k h n", k=DC, h=8))
    kbd.free = [qd]
    k2 = Slot(work[1].rearrange("p (k h n) -> p k h n", k=DC, h=8))
    k2.free = [kd]
    dist = c.tmp(TILES * H * NS).rearrange("p (t n) -> p t n", t=TILES)
    yns = Slot(c.tmp(H * NS))
    dd = []
    for t in range(TILES):
        for i in range(DC):
            e1 = c.tt(kbd.t[:, i], rows_of(kT[:, i, t * P:(t + 1) * P], 8), each(c.const("head16"), P),
                      ALU.mult, kd, kbd.free)
        e2 = c.tt(k2.t, kbd.t, kbd.t, ALU.mult, e1, k2.free)
        bxy, by = c.banks.next(), c.banks.next()
        for s in range(BT):
            r = slice(s * NS, (s + 1) * NS)
            for i in range(DC):
                m1 = c.mm(bxy.t[r, i * D:(i + 1) * D],
                          [(qT[:, i, t * P + s * NS:t * P + (s + 1) * NS], kbd.t[:, i, :, r])], bxy.free, qd, e1)
                m2 = c.mm(by.t[r, i * D:(i + 1) * D], [(c.const("ones")[:, :NS], k2.t[:, i, :, r])], by.free, e2)
        kbd.free, k2.free = [m1, e2], [m2]
        hs = slice(t * H, (t + 1) * H)
        y3 = yns.t.rearrange("p (h n) -> p h n", h=H)
        d3 = dist[:, t].rearrange("p (h n) -> p h n", h=H)
        a = c.copy(c.act, yns.t, by.t, m2, yns.free)
        by.free = [a]
        b = c.stt(dist[:, t], bxy.t, -2.0, yns.t, ALU.mult, ALU.add, m1, a)
        bxy.free = [b]
        b = c.tt(d3, d3, each(xns[:, hs], NS), ALU.add, b)
        a = c.ts(yns.t, yns.t, negc, 1.0, ALU.mult, ALU.add, b)
        a = c.tt(y3, y3, each(onemc[:, hs], NS), ALU.mult, a, om)
        a = c.ts(yns.t, yns.t, EPS, None, ALU.max, None, a)
        a = c.recip(yns.t, a)
        b = c.tt(dist[:, t], dist[:, t], yns.t, ALU.mult, a)
        yns.free = [b]
        dd.append(b)
    u = dist.rearrange("p t n -> p (t n)")
    r2 = c.tmp(TILES * H * NS)
    a = c.ts(u, u, twoc, EPS, ALU.mult, ALU.max, dd)
    a = c.stt(r2, u, 2.0, u, ALU.add, ALU.mult, a)
    a = c.af(r2, r2, ACT.Sqrt, a)
    a = c.tt(u, u, r2, ALU.add, a)
    a = c.af(u, u, ACT.Ln, a, bias=1.0)
    a = c.ts(u, u, slope, negab, ALU.mult, ALU.add, a)
    u3 = u.rearrange("p (m n) -> p m n", n=NS)
    a, _ = softmax_rows(c, u3, NS, a)
    wt = r2
    z = c.pool(lambda e: e.memset(q.rearrange("p t d -> p (t d)"), 0.0), kbd.free)
    bd = Slot(q.rearrange("p t d -> p (t d)").rearrange("p (h m) -> p h m", h=H))
    out = sq
    od = []
    for t in range(TILES):
        w = wt[:, t * H * NS:(t + 1) * H * NS]
        x = c.dve(lambda e, t=t, w=w: e.transpose(w, dist[:, t]), a)
        w3 = w.rearrange("p (h m) -> p h m", h=H)
        for s in range(BT):
            r = slice(s * NS, (s + 1) * NS)
            x2 = c.copy(c.dve, bd.t[r, :, r], w3[r], x, bd.free, z)
        b = c.banks.next()
        for h in range(H):
            m = c.mm(b.t[:, h * DH:(h + 1) * DH], [(bd.t[:, h], v[:, t, h * DH:(h + 1) * DH])], b.free, x2, vdone)
        bd.free = [m]
        d = c.copy(c.act, out[:, t], b.t[:, :D], m)
        b.free = [d]
        od.append(d)
    sq = tok(r2[:, :TILES * D])
    a = to_ball_and_back(out, [od, c.dve.now(), m])
    oT = c.XT
    f = c.to_features(out, oT, [a] * TILES)
    c.add_output(oT, c.wc("wo", DC), DC, f)


def l3_attn(c):
    H, DH, C = 16, 16, 64
    HP = H // 2
    ready, xt = c.enter()
    big = lambda: c.tmp(DC * NT).rearrange("p (k n) -> p k n", k=DC)
    xs = c.XN.rearrange("p t d -> p (t d)").rearrange("p (k n) -> p k n", k=DC)
    perm = [c.copy(q, xs[:, k].rearrange("p (b s) -> p b s", b=NB), c.XT[:, k].rearrange("p (s b) -> p b s", b=NB), xt)
            for k, q in ((0, c.dve), (1, c.pool))]
    q3, k3 = big(), big()
    kd = c.project(k3, c.wc("wk", DC), DC, xs, DC, perm, bias=c.w("bk"))
    qd = c.project(q3, c.wc("wq", DC), DC, xs, DC, perm, bias=c.w("bq"))
    temp = c.tmp(DC)
    a = c.af(temp, c.w("beta"), ACT.Exp, c.w_ready, scale=-1.0)
    qd = [c.ts(q3[:, k], q3[:, k], temp[:, k:k + 1], 1.0 / np.sqrt(DH), ALU.mult, ALU.mult, a, qd) for k in range(DC)]
    v3 = c.tmp(TILES * D).rearrange("p (t d) -> p t d", t=TILES)
    vd = []
    for t in range(TILES):
        b = c.banks.next()
        m = c.mm(b.t[:, :D], [(xs[:, k, t * P:(t + 1) * P], c.wc("wv", DC)[:, k]) for k in range(DC)]
                 + [(c.const("ones")[0:1, :P], c.w("bv"))], b.free, perm)
        d = c.copy(c.act, v3[:, t], b.t[:, :D], m)
        b.free = [d]
        vd.append(d)
    cw = c.tmp(HP * NT).rearrange("p (g n) -> p g n", g=HP)
    mx = Ring([Slot(c.tmp(NB // 2)) for _ in range(4)])
    qc = c.w("qc").rearrange("p (k g m) -> p k g m", k=DC, g=HP // DC)
    cd = [[], []]
    for half in range(2):
        for g in range(HP):
            cols = slice(half * HALF, (half + 1) * HALF)
            b = c.banks.next()
            k = g * DC // HP
            m = c.mm(b.t, [(qc[:, k, g % (HP // DC)], k3[:, k, cols])], b.free, kd)
            x = mx.next()
            b3 = b.t.rearrange("p (b s) -> p b s", s=NS)
            a = c.reduce(x.t, b3, ALU.max, m, x.free)
            a = c.tt(cw[:, g, cols].rearrange("p (b s) -> p b s", s=NS), b3, each(x.t, NS), ALU.subtract, a)
            b.free = x.free = [a]
            cd[half].append(c.af(cw[:, g, cols], cw[:, g, cols], ACT.Exp, a))
    HU = H // DC
    ring = lambda n, cols: Ring([Slot(c.tmp(cols)) for _ in range(n)])
    cwTs, rns, scs, wTs = ring(2, HU * C), ring(2, HU * C), ring(3, HU * C), ring(1, HU * C)
    qbds, ams, bms = ring(1, HU * P), ring(2, HU * P), ring(1, HU * P)
    o_ = Slot(c.tmp(D))
    maxima, totals = ring(2, HU), ring(3, HU)
    oT = c.XT
    outd = []
    UNITS = TILES * DC
    of = [{} for _ in range(UNITS)]

    def turn_keys(u):
        t, k = divmod(u, DC)
        cols = slice(t * P, (t + 1) * P)
        of[u]["cwT"] = cwT = cwTs.next()
        b = c.banks.next()
        for g in range(4):
            m = c.transpose(b.t[:, g * P:(g + 1) * P], cw[:, 4 * k + g, cols], b.free, cd[t // 4])
        of[u]["cwT_ok"] = d = c.copy(c.act, cwT.t, b.t, m, cwT.free)
        b.free = [d]
        of[u]["qbd"] = qbd = qbds.next()
        of[u]["qbd_ok"] = c.tt(qbd.t.rearrange("p (h n) -> p h n", h=HU), rows_of(q3[:, k, cols], HU),
                               each(c.const("head16"), P), ALU.mult, qd, qbd.free, q=c.pool)

    def norms(u):
        t, k = divmod(u, DC)
        cols = slice(t * P, (t + 1) * P)
        of[u]["rn"], of[u]["am"] = rn, am = rns.next(), ams.next()
        b = c.banks.next()
        m = c.mm(b.t, [(c.const("causal"), of[u]["cwT"].t)], b.free, of[u]["cwT_ok"])
        of[u]["rn_ok"] = d = c.recip(b.t, m, rn.free, out=rn.t)
        b.free = [d]
        ad = []
        for g in range(2):
            b = c.banks.next()
            m = c.mm(b.t, [(k3[:, k, cols], of[u]["qbd"].t[:, g * HALF:(g + 1) * HALF])], b.free, kd, of[u]["qbd_ok"])
            d = c.tt(am.t[:, g * HALF:(g + 1) * HALF].rearrange("p (h n) -> p h n", h=4),
                     b.t.rearrange("p (h n) -> p h n", h=4), rows_of(c.const("causal"), 4), ALU.mult, m, am.free)
            b.free = [d]
            ad.append(d)
        of[u]["qbd"].free = [m]
        of[u]["am_ok"] = ad

    def scores(u):
        cwT, rn, am = of[u]["cwT"], of[u]["rn"], of[u]["am"]
        of[u]["s"], mx = scs.next(), maxima.next()
        s_ = of[u]["s"]
        b = c.banks.next()
        for h in range(HU):
            m = c.mm(b.t[:, h * C:(h + 1) * C], [(am.t[:, h * P:(h + 1) * P], cwT.t[:, h * C:(h + 1) * C])], b.free,
                     of[u]["am_ok"])
        cwT.free = am.free = [m]
        a = c.tt(s_.t, b.t, rn.t, ALU.mult, m, of[u]["rn_ok"], s_.free)
        b.free = [a]
        s3 = s_.t.rearrange("p (h n) -> p h n", h=HU)
        a = c.reduce(mx.t, s3, ALU.max, a, mx.free)
        a = c.tt(s3, s3, each(mx.t, C), ALU.subtract, a)
        mx.free = [a]
        of[u]["exp"] = c.af(s3, s3, ACT.Exp, a)

    def weights(u):
        s_, rn, sm = of[u]["s"], of[u]["rn"], totals.next()
        s3 = s_.t.rearrange("p (h n) -> p h n", h=HU)
        a1 = c.reduce(sm.t, s3, ALU.add, of[u]["exp"], sm.free)
        a1 = c.recip(sm.t, a1)
        a2 = c.tt(s_.t, s_.t, rn.t, ALU.mult, of[u]["exp"], a1)
        rn.free = [a2]
        of[u]["w_ok"] = c.tt(s3, s3, each(sm.t, C), ALU.mult, a1, a2)
        sm.free = [of[u]["w_ok"]]

    def turn_weights(u):
        s_ = of[u]["s"]
        of[u]["wT"] = wT = wTs.next()
        b = c.banks.next()
        for g in range(4):
            m = c.transpose(b.t[:, g * P:(g + 1) * P], s_.t[:, g * P:(g + 1) * P], b.free, of[u]["w_ok"])
        of[u]["wT_ok"] = d = c.copy(c.act, wT.t, b.t, m, wT.free)
        b.free = s_.free = [d]

    def pairs(u):
        t, k = divmod(u, DC)
        cols = slice(t * P, (t + 1) * P)
        of[u]["bm"] = bm = bms.next()
        b3 = bm.t.rearrange("p (h n) -> p h n", h=HU)
        bd = []
        for odd in range(2):
            b = c.banks.next()
            r = slice(odd * C, odd * C + C)
            for g in range(4):
                m = c.mm(b.t[:, g * P:(g + 1) * P], [(cw[r, 4 * k + g, cols], of[u]["wT"].t[r, g * P:(g + 1) * P])],
                         b.free, of[u]["wT_ok"])
            d = c.tt(b3[:, odd::2], b.t.rearrange("p (h n) -> p h n", h=4), rows_of(c.const("causal"), 4),
                     ALU.mult, m, bm.free)
            b.free = [d]
            bd.append(d)
        of[u]["wT"].free = [m]
        of[u]["bm_ok"] = bd

    def outputs(u):
        t, k = divmod(u, DC)
        bm = of[u]["bm"]
        b = c.banks.next()
        for h in range(HU):
            f = k * P + h * DH
            m = c.mm(b.t[:, h * DH:(h + 1) * DH], [(bm.t[:, h * P:(h + 1) * P], v3[:, t, f:f + DH])], b.free,
                     of[u]["bm_ok"], vd)
        bm.free = [m]
        of[u]["o_ok"] = d = c.copy(c.act, o_.t[:, k * P:(k + 1) * P], b.t[:, :P], m, o_.free)
        b.free = [d]

    def turn_outputs(t):
        b = c.banks.next()
        for k in range(DC):
            m = c.transpose(b.t[:, k * P:(k + 1) * P], o_.t[:, k * P:(k + 1) * P], b.free, of[DC * t + k]["o_ok"])
        o_.free = [m]
        for k in range(DC):
            d = c.copy(c.dve, oT[:, k].rearrange("p (s b) -> p b s", b=NB)[:, t * BT:(t + 1) * BT],
                       b.t[:, k * P:(k + 1) * P].rearrange("p (b s) -> p b s", b=BT), m, perm)
            outd.append(d)
        b.free = [d]

    for i in range(UNITS + 3):
        if 1 <= i <= UNITS:
            weights(i - 1)
        if i >= 3 and (i - 3) % DC == DC - 1:
            turn_outputs((i - 3) // DC)
        if i < UNITS:
            turn_keys(i)
        if 2 <= i < UNITS + 2:
            turn_weights(i - 2)
        if i < UNITS:
            norms(i)
        if 2 <= i < UNITS + 2:
            pairs(i - 2)
        if i < UNITS:
            scores(i)
        if 2 <= i < UNITS + 2:
            outputs(i - 2)
    c.add_output(oT, c.wc("wo", DC), DC, [outd, ready], c.w("bo"))



class Context:

    def __init__(self, c, slots):
        self.c = c
        self.cols = 2 * G + 3 * (DV + 1)
        self.ring = Ring([Slot(c.tmp(self.cols), c.new_sem(f"{c.name}_context{i}")) for i in range(slots)])
        c.sp.wait(c.ends[-1] if c.ends else None)
        self.queue, self.asked = [], 0
        for _ in range(slots):
            self.ask()

    def ask(self):
        if self.asked < NB:
            s, b = self.ring.next(), self.asked
            self.c.sp.wait(s.free)
            self.c.sp.silent(lambda q: q.dma_start(s.t, self.c.dram["ctx"][b]).then_inc(s.sem, 16))
            s.n += 16
            self.queue.append((s, (s.sem, s.n)))
            self.asked += 1

    def next(self):
        return self.queue.pop(0)


def head_queries(c, wk, heads, aug, src, q_tile, scale, ready, slot):
    qa, qb = slot.t
    done = []
    for part, rows, c0 in ((qa, P, 0), (qb, aug - P, P)):
        for g in range(0, heads, 4):
            b = c.banks.next()
            for j in range(4):
                m = c.mm(b.t[:rows, j * P:(j + 1) * P], [(wk(g + j)[:, c0:c0 + rows], src(g + j)[:, q_tile])],
                         b.free, ready, slot.free)
            done.append(c.copy(c.act if c0 else c.dve, part[:rows, :, g:g + 4, :].rearrange("p s h q -> p h s q"),
                               b.t[:rows].rearrange("p (h s q) -> p h s q", h=4, s=BT), m, slot.free))
            b.free = done[-1:]
    return done


def exp_keys(c, bank, n, p_slot, stat, m):
    nmax, total = stat.t
    a = c.dve(lambda e: e.tensor_reduce(nmax, bank.t[:, :n], AX.X, ALU.max, negate=True), m, stat.free)
    a = c.af(p_slot.t[:, :n], bank.t[:, :n], ACT.Exp, a, p_slot.free, bias=nmax, accum=total)
    bank.free = [a]
    return a


def divide_keys(c, n, p_slot, stat, ready):
    _, total = stat.t
    a = c.recip(total, ready)
    a = c.ts(p_slot.t[:, :n], p_slot.t[:, :n], total, None, ALU.mult, None, a, q=c.pool)
    stat.free = [a]
    return a


def raw_attention(c, heads, aug_k, aug_v, queries, finish):
    R = heads // 4
    ctx = Context(c, 4)
    qslots = Ring([Slot((c.tmp(BT * heads * NS).rearrange("p (s h q) -> p s h q", s=BT, h=heads),
                         c.tmp(BT * heads * NS).rearrange("p (s h q) -> p s h q", s=BT, h=heads)))
                   for _ in range(2)])
    probs = Ring([Slot(c.tmp(G)) for _ in range(2 * R)])
    stats = Ring([Slot((c.tmp(1), c.tmp(1))) for _ in range(2 * R)])
    pts = Ring([Slot((c.tmp(R * P), c.tmp(R * P), c.tmp(R * P))) for _ in range(2)])
    pc = Slot((c.tmp(heads * P).rearrange("p (h n) -> p h n", h=heads),
               c.tmp(heads * P).rearrange("p (h n) -> p h n", h=heads)))
    of = [{} for _ in range(NB)]
    turned, sums = {}, {}

    def turn(t):
        slot = qslots.next()
        turned[t] = slot, queries(t, slot)

    def scores(s):
        t, i = divmod(s, BT)
        slot, qd = turned[t]
        qa, qb = slot.t
        cx, got = ctx.next()
        of[s]["cx"] = cx
        out = []
        for r in range(R):
            b, p, st = c.banks.next(), probs.next(), stats.next()
            m = c.mm(b.t[:, :G], [(qa[:, i, 4 * r:4 * r + 4].rearrange("p h q -> p (h q)"), cx.t[:, CT0:CT0 + G]),
                                  (qb[:aug_k - P, i, 4 * r:4 * r + 4].rearrange("p h q -> p (h q)"),
                                   cx.t[:aug_k - P, CT1:CT1 + G])], b.free, qd, got)
            out.append((p, st, exp_keys(c, b, G, p, st, m)))
        out = [(p, divide_keys(c, G, p, st, a)) for p, st, a in out]
        slot.free = [m]
        of[s]["p"] = out

    def weights_to_keys(s):
        of[s]["pt"] = pt = pts.next()
        done = []
        for k, (k0, n) in enumerate(((0, P), (P, P), (2 * P, 1))):
            b = c.banks.next()
            for r, (p, ready) in enumerate(of[s]["p"]):
                m = c.transpose(b.t[:n, r * P:(r + 1) * P], p.t[:, k0:k0 + n], b.free, ready)
            d = c.copy((c.act, c.dve, c.dve)[k], pt.t[k][:n], b.t[:n, :R * P], m, pt.free)
            b.free = [d]
            done.append(d)
        for p, _ in of[s]["p"]:
            p.free = [m]
        of[s]["pt_ok"] = done

    def products(s):
        t, i = divmod(s, BT)
        pt, cx = of[s]["pt"], of[s]["cx"]
        for part, rows, f0 in ((pc.t[0], P, 0), (pc.t[1], aug_v - P, P)):
            b = c.banks.next()
            m = c.mm(b.t[:rows, :R * P],
                     [(cx.t[:n, CK + k * (DV + 1) + f0:CK + k * (DV + 1) + f0 + rows], pt.t[k][:n])
                      for k, n in enumerate((P, P, 1))], b.free, of[s]["pt_ok"])
            d = c.copy(c.dve if f0 else c.act, part[:rows, :, i * NS:(i + 1) * NS],
                       b.t[:rows, :R * P].rearrange("p (h q) -> p h q", h=heads), m, pc.free)
            b.free = [d]
            sums.setdefault(t, []).append(d)
        pt.free = cx.free = [m]
        ctx.ask()

    turn(0)
    for s in range(NB + 3):
        if s < NB:
            scores(s)
        if 1 <= s <= NB:
            weights_to_keys(s - 1)
        if s % BT == 2 and s + BT < NB + BT and s // BT + 1 < TILES:
            turn(s // BT + 1)
        if s >= 3 and (s - 3) % BT == BT - 1:
            t = (s - 3) // BT
            finish(t, pc.t[0], pc.t[1], sums[t])
            pc.free = [c.pe.now()]
        if 2 <= s < NB + 2:
            products(s - 2)


def l2_xattn(c):
    H, DK = 16, 64
    ready, xt = c.enter()
    HC = H * DK // P
    qt = Slot(c.tmp(HC * P).rearrange("p (k n) -> p k n", k=HC))
    ot = Slot(c.tmp(HC * P).rearrange("p (k n) -> p k n", k=HC))
    wk = c.w("wk").rearrange("p (k f) -> p k f", k=HC)

    def queries(t, slot):
        d = []
        for g in range(0, HC, 4):
            b = c.banks.next()
            for j in range(4):
                m = c.mm(b.t[:, j * P:(j + 1) * P],
                         [(c.wc("wq", DC)[:, k, (g + j) * P:(g + j + 1) * P], c.XT[:, k, t * P:(t + 1) * P])
                          for k in range(DC)], b.free, xt)
            d.append(c.dve(lambda e, b=b, g=g: e.tensor_scalar(qt.t[:, g:g + 4].rearrange("p k n -> p (k n)"), b.t,
                                                              DK ** -0.5, None, ALU.mult), m, qt.free))
            b.free = [d[-1]]
        qa, qb = slot.t
        done = []
        for odd in range(2):
            r = slice(odd * DK, odd * DK + DK)
            for part, rows, c0 in ((qa, P, 0), (qb, V1, P)):
                for g in range(0, HC, 4):
                    b = c.banks.next()
                    for j in range(4):
                        m = c.mm(b.t[:rows, j * P:(j + 1) * P], [(wk[r, g + j, c0:c0 + rows], qt.t[r, g + j])],
                                 b.free, d)
                    done.append(c.copy(c.act if c0 else c.dve,
                                       part[:rows, :, 2 * g + odd:2 * g + odd + 7:2, :].rearrange("p s h q -> p h s q"),
                                       b.t[:rows].rearrange("p (h s q) -> p h s q", h=4, s=BT), m, slot.free))
                    b.free = done[-1:]
        qt.free = [m]
        return done

    def finish(t, pa, pb, pr):
        d = []
        for g in range(0, HC, 4):
            b = c.banks.next()
            for j in range(4):
                for odd in range(2):
                    h = 2 * (g + j) + odd
                    hc = slice(h * DK, (h + 1) * DK)
                    m = c.mm(b.t[odd * DK:(odd + 1) * DK, j * P:(j + 1) * P],
                             [(c.w("wv0")[:, hc], pa[:, h]), (c.w("wv1")[:, hc], pb[:V1, h])], b.free, pr)
            d.append(c.copy(c.act, ot.t[:, g:g + 4].rearrange("p k n -> p (k n)"), b.t, m, ot.free))
            b.free = [d[-1]]
        c.add_output(ot.t, c.wc("wo", HC), HC, [d, ready], c.w("bo"), tiles=[t], cols=slice(0, P))
        ot.free = [c.pe.now()]

    raw_attention(c, H, DV, DV, queries, finish)


def l3_xattn(c):
    H, DK = 16, 16
    ready, xt = c.enter()
    q3 = c.tmp(DC * NT).rearrange("p (k n) -> p k n", k=DC)
    ot = Slot(c.tmp(DC * P).rearrange("p (k n) -> p k n", k=DC))
    qd = c.project(q3, c.wc("wq", DC), DC, c.XT, DC, xt, bias=c.w("bq"))
    qd = [c.ts(q3[:, k], q3[:, k], DK ** -0.5, None, ALU.mult, None, qd) for k in range(DC)]
    wk = c.w("wk").rearrange("p (h f) -> p h f", h=H)
    wv = [c.w(n).rearrange("p (h f) -> p h f", h=H) for n in ("wv0", "wv1")]

    def queries(t, slot):
        return head_queries(c, lambda h: wk[:, h], H, DV + 1, lambda h: q3[:, h // 8], slice(t * P, (t + 1) * P),
                            None, qd, slot)

    def finish(t, pa, pb, pr):
        b = c.banks.next()
        for k in range(DC):
            m = c.mm(b.t[:, k * P:(k + 1) * P],
                     [x for h in range(8 * k, 8 * k + 8)
                      for x in ((wv[0][:, h], pa[:, h]), (wv[1][:, h], pb[:V1 + 1, h]))], b.free, pr)
        d = c.copy(c.act, ot.t.rearrange("p k n -> p (k n)"), b.t[:, :DC * P], m, ot.free)
        b.free = [d]
        c.add_output(ot.t, c.wc("wo", DC), DC, [d, ready], c.w("bo"), tiles=[t], cols=slice(0, P))
        ot.free = [c.pe.now()]

    raw_attention(c, H, DV + 1, DV + 1, queries, finish)


def mask_rows(c, src, cols, first, last, name):
    sem = c.new_sem(name)
    packed = c.tmp(-(-G // 4), NB).bitcast(U32)
    raw = packed.bitcast(U8)[:, :G]
    out = c.tmp(cols, NB)
    c.sp.wait(c.ends[-1] if c.ends else None)
    c.sp.silent(lambda q: q.dma_start(packed, c.dram[src]).then_inc(sem, 16))
    z = c.dve(lambda e: e.memset(out, 0.0))
    a = c.copy(c.dve, out[:, first:first + G - 1], raw[:, :G - 1], z, (sem, 16))
    a = c.copy(c.dve, out[:, last:last + 1], raw[:, G - 1:G], a)
    for x in (out[:, first:first + G - 1], out[:, last:last + 1]):
        a = c.ts(x, x, -NEG, NEG, ALU.mult, ALU.add, a)
    return out, a


def pick(c, b):
    return c.const("eye")[:NB, b:b + 1].to_broadcast([NB, P])


def l0_xattn(c):
    H, DK, RMS_EPS = 4, 64, 1e-8
    KEYS = G + NS
    L3 = NS + 1
    ctx = Context(c, 3)
    mask, mask_ok = mask_rows(c, "keep0", KEYS, 0, KEYS - 1, "keep0_loaded")
    ready = c.normalise(c.X, c.XN)
    tmp = c.tmp(TILES * D).rearrange("p (t d) -> p t d", t=TILES)
    n2 = c.normalise(c.XN, tmp, ready)
    lt = c.to_features(tmp, c.XT, n2, c.w("gl"), c.w("bl"))
    lnT = c.XT
    gq = c.tmp(DK)
    g = c.stt(gq, c.w("qn"), DK ** -0.5, c.w("kn"), ALU.mult, ALU.mult)
    q = tmp
    qd = []
    for t in range(0, TILES, 2):
        b = c.banks.next()
        for j in range(2):
            m = c.mm(b.t[:, j * D:(j + 1) * D],
                     [(lnT[:, k, (t + j) * P:(t + j + 1) * P], c.wc("wq", DC)[:, k]) for k in range(DC)], b.free, lt)
        d = c.copy(c.act if t % 4 else c.dve, q[:, t:t + 2], b.t, m)
        b.free = [d]
        qd.append(d)
    NH = TILES * H
    heads = lambda a: a.rearrange("p t (h d) -> p (t h) d", h=H)
    nrm = c.tmp(NH)
    qbd = c.tmp(DC * NB * P)

    def rms(n2, ready):
        a = c.ts(n2, n2, 1.0 / DK, RMS_EPS ** 2, ALU.mult, ALU.max, ready)
        return c.power(n2, "mhalf", a)

    a = c.tt(c.XN, q, q, ALU.mult, qd)
    a = c.reduce(nrm, heads(c.XN), ALU.add, a)
    a = rms(nrm, a)
    a = c.tt(heads(q), heads(q), each(nrm, DK), ALU.mult, a)
    a = c.tt(heads(q), heads(q), rows_of(gq, NH), ALU.mult, a, g)
    qT = c.XN.rearrange("p t d -> p (t d)").rearrange("p (k n) -> p k n", k=DC)
    qd = c.to_features(q, qT, [a] * TILES)
    z = c.pool(lambda e: e.memset(qbd, 0.0))
    q5 = qbd.rearrange("p (k b h q) -> p k b h q", k=DC, b=NB, h=H)
    bd = []
    for k in range(DC):
        for odd in range(2):
            r = slice(odd * DK, odd * DK + DK)
            bd.append(c.copy(c.dve if odd else c.act, q5[r, k, :, 2 * k + odd],
                             qT[r, k].rearrange("p (b q) -> p b q", b=NB), qd, z))
    sem = c.new_sem("last_rows_loaded")
    last = c.tmp(DV, NB)
    lT = [c.tmp(NB), c.tmp(NB, V1)]
    st = c.tmp(12)
    c.sp.silent(lambda e: e.dma_start(last, c.dram["ctx_last"]).then_inc(sem, 16))
    a = c.dve(lambda e: e.bn_stats(st[:NB, 0:6], last), (sem, 16))
    a = c.dve(lambda e: e.bn_aggr(st[:NB, 6:8], st[:NB, 0:6]), a)
    a = c.ts(st[:NB, 8:9], st[:NB, 7:8], LN_EPS, None, ALU.add, None, a)
    a = c.power(st[:NB, 8:9], "mhalf", a)
    a = c.ts(last, last, st[:NB, 6:7], st[:NB, 8:9], ALU.subtract, ALU.mult, a)
    b = c.banks.next()
    c.transpose(b.t[:, 0:NB], last[:, 0:P], b.free, a)
    m = c.transpose(b.t[:V1, 64:64 + NB], last[:, P:DV])
    l1 = c.ts(lT[0], b.t[:, 0:NB], c.w("gx0"), c.w("bx0"), ALU.mult, ALU.add, m)
    l2 = c.ts(lT[1], b.t[:V1, 64:64 + NB], c.w("gx1"), c.w("bx1"), ALU.mult, ALU.add, m)
    b.free = [l1, l2]
    xn = Ring([Slot((c.tmp(2 * DV).rearrange("p (k d) -> p k d", k=2), c.tmp(24))) for _ in range(2)])
    xnT = Ring([Slot((c.tmp(2 * P), c.tmp(2 * P))) for _ in range(2)])
    k3 = Ring([Slot(c.tmp(3 * D)) for _ in range(2)])
    v3 = Ring([Slot(c.tmp(3 * D)) for _ in range(3)])
    sq = Slot((c.tmp(3 * D), c.tmp(3 * H)))
    kT = Ring([Slot(c.tmp(DC * KEYS).rearrange("p (k n) -> p k n", k=DC)) for _ in range(2)])
    probs = Ring([Slot(c.tmp(KEYS)) for _ in range(2)])
    stats = Ring([Slot((c.tmp(1), c.tmp(1))) for _ in range(2)])
    pts = Ring([Slot(c.tmp(3 * P)) for _ in range(2)])
    ot = Slot(c.tmp(DC * P).rearrange("p (k n) -> p k n", k=DC))
    for s in k3.slots:
        s.free = [c.pool(lambda e, s=s: e.memset(s.t, 0.0))]
    every, sums = c.banks, c.banks.slots[6:]
    c.banks = Ring(every.slots[:6])
    of = [{} for _ in range(NB)]

    def context_stats(s):
        of[s]["cx"], of[s]["got"] = cx, got = ctx.next()
        of[s]["xn"] = xs = xn.next()
        x, st = xs.t
        for i in range(2):
            src = cx.t[:, CK + i * (DV + 1):CK + i * (DV + 1) + DV]
            a = c.dve(lambda e, src=src, i=i: e.bn_stats(st[:, 6 * i:6 * i + 6], src), got, xs.free)
        for i in range(2):
            a = c.dve(lambda e, i=i: e.bn_aggr(st[:, 12 + 2 * i:14 + 2 * i], st[:, 6 * i:6 * i + 6]), a)
        rs = st[:, 16:18]
        a = c.ts(rs, st[:, 12:16].rearrange("p (k v) -> p k v", k=2)[:, :, 1], LN_EPS, None, ALU.add, None, a)
        of[s]["rstd"] = c.power(rs, "mhalf", a)

    def context_normal(s):
        cx, xs = of[s]["cx"], of[s]["xn"]
        x, st = xs.t
        for i in range(2):
            src = cx.t[:, CK + i * (DV + 1):CK + i * (DV + 1) + DV]
            nd = c.ts(x[:, i], src, st[:, 12 + 2 * i:13 + 2 * i], st[:, 16 + i:17 + i], ALU.subtract, ALU.mult,
                      of[s]["rstd"])
        cx.free = [nd]
        ctx.ask()
        of[s]["normal"] = nd

    def context_features(s):
        xs = of[s]["xn"]
        x, _ = xs.t
        b = c.banks.next()
        for i in range(2):
            c.transpose(b.t[:, i * P:(i + 1) * P], x[:, i, 0:P], b.free, of[s]["normal"])
            m = c.transpose(b.t[:V1, 256 + i * P:256 + (i + 1) * P], x[:, i, P:DV])
        xs.free = [m]
        of[s]["xt"] = xt = xnT.next()
        d1 = c.ts(xt.t[0], b.t[:, :256], c.w("gx0"), c.w("bx0"), ALU.mult, ALU.add, m, xt.free)
        d2 = c.ts(xt.t[1][:V1], b.t[:V1, 256:], c.w("gx1"), c.w("bx1"), ALU.mult, ALU.add, m, xt.free)
        b.free = [d1, d2]
        of[s]["xt_ok"] = [d1, d2]

    def keys_values(s):
        xt = of[s]["xt"]
        of[s]["k"], of[s]["v"] = ks, vs = k3.next(), v3.next()
        kd, vd = [], []
        for i in range(3):
            b = c.banks.next()
            if i < 2:
                n = P
                m = c.mm(b.t, [(xt.t[0][:, i * P:(i + 1) * P], c.w("wkv0")),
                               (xt.t[1][:V1, i * P:(i + 1) * P], c.w("wkv1"))], b.free, of[s]["xt_ok"])
            else:
                n = L3
                c.mm(b.t[:NS], [(lnT[:, k, s * NS:(s + 1) * NS], c.wc("wlkv", DC)[:, k]) for k in range(DC)],
                     b.free, lt)
                m = c.mm(b.t[NS:L3], [(lT[0][:, s:s + 1], c.w("wkv0")), (lT[1][:, s:s + 1], c.w("wkv1"))], l1, l2)
            e = c.act
            kd.append(c.copy(e, ks.t[:n, i * D:(i + 1) * D], b.t[:n, :D], m, ks.free))
            vd.append(c.copy(e, vs.t[:n, i * D:(i + 1) * D], b.t[:n, D:], m, vs.free))
            b.free = [kd[-1], vd[-1]]
        xt.free = [m]
        of[s]["squares"] = c.af(sq.t[0], ks.t, ACT.Square, kd, sq.free)
        of[s]["v_ok"] = vd

    def keys_normal(s):
        s2, nr = sq.t
        ks = of[s]["k"]
        a = c.reduce(nr, s2.rearrange("p (m d) -> p m d", d=DK), ALU.add, of[s]["squares"])
        of[s]["k_norm"] = rms(nr, a)

    def keys_scale(s):
        ks, a = of[s]["k"], of[s]["k_norm"]
        nr = sq.t[1]
        k4 = ks.t.rearrange("p (m d) -> p m d", d=DK)
        a = c.tt(k4, k4, each(nr, DK), ALU.mult, a)
        sq.free = [a]
        of[s]["k_ok"] = a

    def keys_features(s):
        ks = of[s]["k"]
        of[s]["kt"] = kt = kT.next()
        td = []
        for k in range(DC):
            b = c.banks.next()
            for i, n in enumerate((P, P, L3)):
                m = c.transpose(b.t[:, i * P:i * P + n], ks.t[:n, i * D + k * P:i * D + (k + 1) * P], b.free,
                                of[s]["k_ok"])
            d = c.copy((c.act, c.dve)[k], kt.t[:, k], b.t[:, :KEYS], m, kt.free)
            b.free = [d]
            td.append(d)
        ks.free = [m]
        of[s]["kt_ok"] = td

    def scores(s):
        kt = of[s]["kt"]
        b, st = c.banks.next(), stats.next()
        of[s]["p"] = p = probs.next()
        q4 = qbd.rearrange("p (k b m) -> p k b m", k=DC, b=NB)
        m = c.mm(b.t[:, :KEYS], [(pick(c, s), mask)] + [(q4[:, k, s], kt.t[:, k]) for k in range(DC)],
                 b.free, bd, of[s]["kt_ok"], mask_ok)
        kt.free = [m]
        of[s]["sums"], of[s]["exp"] = st, exp_keys(c, b, KEYS, p, st, m)

    def weights_to_keys(s):
        p = of[s]["p"]
        of[s]["pt"] = pt = pts.next()
        b = c.banks.next()
        for k, n in enumerate((P, P, L3)):
            m = c.transpose(b.t[:n, k * P:(k + 1) * P], p.t[:, k * P:k * P + n], b.free, of[s]["p_ok"])
        p.free = [m]
        d1 = c.copy(c.act, pt.t[:, :2 * P], b.t[:, :2 * P], m, pt.free)
        d2 = c.copy(c.act, pt.t[:L3, 2 * P:], b.t[:L3, 2 * P:3 * P], m, pt.free)
        b.free = [d1, d2]
        of[s]["pt_ok"] = [d1, d2]

    def products(s):
        t, i = divmod(s, BT)
        pt, vs = of[s]["pt"], of[s]["v"]
        for k in range(DC):
            ob = sums[k]
            m = c.mm(ob.t[:, i * 2 * NS:(i + 1) * 2 * NS],
                     [(vs.t[:n, j * D + k * P:j * D + (k + 1) * P],
                       pt.t[:n, j * P + k * 2 * NS:j * P + (k + 1) * 2 * NS]) for j, n in enumerate((P, P, L3))],
                     ob.free, of[s]["pt_ok"], of[s]["v_ok"])
        vs.free = pt.free = [m]
        if i == BT - 1:
            od = []
            for k in range(DC):
                ob = sums[k]
                for odd in range(2):
                    r = slice(odd * DK, odd * DK + DK)
                    od.append(c.copy(c.dve, ot.t[r, k].rearrange("p (s q) -> p s q", s=BT),
                                     ob.t[r, :BT * 2 * NS].rearrange("p (s h q) -> p h s q", s=BT, h=2)[:, odd],
                                     m, ot.free))
                ob.free = od[-2:]
            c.add_output(ot.t, c.wc("wo", DC), DC, od, c.w("bo"), tiles=[t], cols=slice(0, P))
            ot.free = [c.pe.now()]

    for i in range(NB + 3):
        if i < NB:
            context_stats(i)
        if 2 <= i < NB + 2:
            keys_scale(i - 2)
        if i >= 3:
            of[i - 3]["p_ok"] = divide_keys(c, KEYS, of[i - 3]["p"], of[i - 3]["sums"], of[i - 3]["exp"])
        if 1 <= i <= NB:
            keys_values(i - 1)
        if i >= 3:
            weights_to_keys(i - 3)
        if i < NB:
            context_normal(i)
            context_features(i)
        if 2 <= i < NB + 2:
            keys_features(i - 2)
        if i >= 3:
            products(i - 3)
        if 2 <= i < NB + 2:
            scores(i - 2)
        if 1 <= i <= NB:
            keys_normal(i - 1)
    c.banks = every


def l1_xattn(c):
    H, DH, TOP = 4, 32, 32
    TAKEN = -3.0e38
    ready, xt = c.enter()
    ct3 = c.tmp(DC * NT).rearrange("p (k n) -> p k n", k=DC)
    mark = c.used
    mask, mask_ok = mask_rows(c, "keep1", G, 0, G - 1, "keep1_loaded")
    sem = c.new_sem("query_mask_loaded")
    packed = c.tmp(NB // 4).bitcast(U32)
    qraw = packed.bitcast(U8)
    qmask = c.tmp(NB)
    c.sp.silent(lambda e: e.dma_start(packed, c.dram["qmask"]).then_inc(sem, 16))
    qm = c.copy(c.dve, qmask, qraw, (sem, 16))
    q3 = c.tmp(NT)
    qd = []
    for h in range(2):
        b = c.banks.next()
        m = c.mm(b.t, [(c.wc("wq", DC)[:, k], c.XT[:, k, h * HALF:(h + 1) * HALF]) for k in range(DC)], b.free, xt)
        d = c.ts(q3[:, h * HALF:(h + 1) * HALF], b.t, DH ** -0.5, None, ALU.mult, None, m)
        b.free = [d]
        qd.append(d)
    wk = c.w("wk0").rearrange("p (h f) -> p h f", h=H)
    ctx = Context(c, 5)
    qslots = Ring([Slot((c.tmp(BT * P).rearrange("p (s h q) -> p s h q", s=BT, h=H),
                         c.tmp(BT * P).rearrange("p (s h q) -> p s h q", s=BT, h=H))) for _ in range(2)])
    works = Ring([Slot((c.tmp(G), c.tmp(8), c.tmp(1), c.tmp(1))) for _ in range(4)])
    probs = Ring([Slot(c.tmp(G)) for _ in range(4)])
    pts = Ring([Slot(c.tmp(3 * P)) for _ in range(2)])
    pc = Slot((c.tmp(H * P).rearrange("p (h n) -> p h n", h=H), c.tmp(H * P).rearrange("p (h n) -> p h n", h=H)))
    state, turned = {}, {}
    ctd = []

    def turn(t):
        slot = qslots.next()
        turned[t] = slot, head_queries(c, lambda h: wk[:, h], H, DV, lambda h: q3, slice(t * P, (t + 1) * P),
                                       None, qd, slot)

    def scores(s):
        t, i = divmod(s, BT)
        slot, hd = turned[t]
        qa, qb = slot.t
        cx, got = ctx.next()
        b, w, p = c.banks.next(), works.next(), probs.next()
        work, top, nmax, total = w.t
        m = c.mm(b.t[:, :G], [(pick(c, s), mask), (qa[:, i].rearrange("p h q -> p (h q)"), cx.t[:, CT0:CT0 + G]),
                              (qb[:V1, i].rearrange("p h q -> p (h q)"), cx.t[:V1, CT1:CT1 + G])],
                 b.free, hd, got, mask_ok)
        slot.free = [m]
        a = c.copy(c.act, work, b.t[:, :G], m, w.free)
        for r in range(TOP // 8):
            x = c.dve(lambda e: e.max(top, work), a)
            if r == 0:
                n = c.ts(nmax, top[:, 0:1], -1.0, None, ALU.mult, None, x)
            a = c.dve(lambda e: e.match_replace(work, top, work, TAKEN), x, n)
        x = c.af(p.t, b.t[:, :G], ACT.Exp, n, p.free, bias=nmax)
        b.free = [x]
        a = c.dve(lambda e: e.scalar_tensor_tensor(out=p.t, in0=work, scalar=TAKEN, in1=p.t, op0=ALU.is_equal,
                                                   op1=ALU.mult, accum_out=total), a, x)
        a = c.recip(total, a)
        a = c.tt(total, total, qmask[:, s:s + 1], ALU.mult, a, qm)
        a = c.ts(p.t, p.t, total, None, ALU.mult, None, a, q=c.pool)
        w.free = [a]
        return cx, p, a

    of = [None] * NB

    def weights_to_keys(s):
        cx, p, pd = of[s]
        pt = pts.next()
        b = c.banks.next()
        for k, n in enumerate((P, P, 1)):
            m = c.transpose(b.t[:n, k * P:(k + 1) * P], p.t[:, k * P:k * P + n], b.free, pd)
        p.free = [m]
        d1 = c.copy(c.act, pt.t[:, :2 * P], b.t[:, :2 * P], m, pt.free)
        d2 = c.copy(c.act, pt.t[:1, 2 * P:], b.t[:1, 2 * P:3 * P], m, pt.free)
        b.free = [d1, d2]
        of[s] = cx, pt, d1, d2

    def products(s):
        t, i = divmod(s, BT)
        cx, pt, d1, d2 = of[s]
        b = c.banks.next()
        for j, rows, f0 in ((0, P, 0), (1, V1, P)):
            m = c.mm(b.t[:rows, j * P:(j + 1) * P],
                     [(cx.t[:n, CK + k * (DV + 1) + f0:CK + k * (DV + 1) + f0 + rows], pt.t[:n, k * P:(k + 1) * P])
                      for k, n in enumerate((P, P, 1))], b.free, d1, d2)
        for j, rows in ((0, P), (1, V1)):
            d = c.copy(c.act, pc.t[j][:rows, :, i * NS:(i + 1) * NS],
                       b.t[:rows, j * P:(j + 1) * P].rearrange("p (h q) -> p h q", h=H), m, pc.free)
            state.setdefault("pc", []).append(d)
        b.free = [d]
        pt.free = cx.free = [m]
        ctx.ask()
        if i == BT - 1:
            pr = state.pop("pc")
            b = c.banks.next()
            for o in range(DC):
                oc = slice(o * P, (o + 1) * P)
                m = c.mm(b.t[:, oc], [x for h in range(H) for x in ((c.w("wv0")[:, oc], pc.t[0][:, h]),
                                                                  (c.w("wv1")[:, oc], pc.t[1][:V1, h]))], b.free, pr)
            pc.free = [m]
            d = c.af(ct3[:, :, t * P:(t + 1) * P], b.t[:, :D].rearrange("p (k n) -> p k n", k=DC), ACT.Copy, m,
                     scale=1.0 / H)
            b.free = [d]
            ctd.append(d)

    turn(0)
    for s in range(NB + 3):
        if s < NB:
            of[s] = scores(s)
        if s % BT == 2 and s // BT + 1 < TILES:
            turn(s // BT + 1)
        if 2 <= s < NB + 2:
            weights_to_keys(s - 2)
        if s >= 3:
            products(s - 3)

    c.fence()
    c.used = mark
    if c.kern_ok is None:
        s4d_kernel(c, c.w, c.tmp, None)
        c.fence()
        c.used = mark
    kern, kern_ok = c.kern, c.kern_ok
    mg = c.w("mg")
    flat = lambda a: a.rearrange("p k n -> p (k n)")
    film = c.tmp(2 * DC * NT).rearrange("p (k n) -> p k n", k=2 * DC)
    x3, y3 = (c.tmp(DC * NT).rearrange("p (k n) -> p k n", k=DC) for _ in range(2))
    tok = c.tmp(TILES * D).rearrange("p (t d) -> p t d", t=TILES)

    def modulate(v, w, bias, ready, free):
        f = c.project(film, c.wc(w, DC), DC, ct3, 2 * DC, [ctd, free], bias=c.w(bias))
        a = c.ts(flat(film[:, :DC]), flat(film[:, :DC]), mg, 1.0, ALU.mult, ALU.add, f)
        b = c.ts(flat(film[:, DC:]), flat(film[:, DC:]), mg, None, ALU.mult, None, f, q=c.pool)
        a = c.tt(flat(v), flat(v), flat(film[:, :DC]), ALU.mult, a, ready)
        return c.tt(flat(v), flat(v), flat(film[:, DC:]), ALU.add, a, b)

    n = c.normalise(c.XN, tok, ready)
    f = c.to_features(tok, x3, n, c.w("gi"), c.w("bi"))
    a = modulate(x3, "fi", "bfi", f, None)
    first = c.tmp(DC)
    k0 = c.tt(first, kern[:, :, 0], c.w("dskip"), ALU.add, kern_ok)
    yd = []
    for k in range(DC):
        d = c.ts(y3[:, k], x3[:, k], first[:, k:k + 1], None, ALU.mult, None, k0, a)
        for j in range(1, NS):
            src = x3[:, k].rearrange("p (b s) -> p b s", s=NS)[:, :, :NS - j]
            dst = y3[:, k].rearrange("p (b s) -> p b s", s=NS)[:, :, j:]
            d = c.stt(dst, src, kern[:, k, j:j + 1], dst, ALU.mult, ALU.add, d)
        yd.append(d)
    a = modulate(y3, "fo", "bfo", yd, yd)
    back = to_tokens(c, y3, tok, [a] * DC)
    r = [c.tt(tok[:, t], tok[:, t], c.XN[:, t], ALU.add, back) for t in range(TILES)]
    hn = c.normalise(tok, c.XN, [r, n])
    h3 = c.XT
    f = c.to_features(c.XN, h3, hn, c.w("gf"), c.w("bf"))
    c.fence()
    c.used = mark
    tok2 = tok
    HC = 8
    hid = c.tmp(HC * NT).rearrange("p (k n) -> p k n", k=HC)
    hd = c.project(hid, c.wc("w1", DC), DC, h3, HC, f, bias=c.w("b1"), func=ACT.Gelu)
    od = []
    for t in range(TILES):
        b = c.banks.next()
        m = c.mm(b.t[:, :D], [(hid[:, k, t * P:(t + 1) * P], c.wc("w2", HC)[:, k]) for k in range(HC)]
                 + [(c.const("ones")[0:1, :P], c.w("b2"))], b.free, hd)
        d = c.tt(tok2[:, t], b.t[:, :D], tok2[:, t], ALU.add, m)
        b.free = [d]
        od.append(d)
    n = c.normalise(tok2, c.XN, od)
    for t in range(TILES):
        a = c.tt(c.XN[:, t], c.XN[:, t], c.w("go"), ALU.mult, n[t])
        a = c.tt(c.XN[:, t], c.XN[:, t], c.w("bo"), ALU.add, a)
        c.tt(c.X[:, t], c.X[:, t], c.XN[:, t], ALU.add, a)


def s4d_kernel(c, w_of, tmp, ready):
    N = 64
    kern = c.kern
    n2 = lambda: tmp(DC * N)
    dt = tmp(DC)
    a0 = c.af(dt, w_of("logdt"), ACT.Exp, ready)
    a, w = n2(), n2()
    k3 = lambda x: x.rearrange("p (k n) -> p k n", k=DC)
    r1 = c.tt(k3(a), k3(w_of("are")), each(dt, N), ALU.mult, a0)
    r2 = c.tt(k3(w), k3(w_of("aim")), each(dt, N), ALU.mult, a0)
    th, em1, ea, sw, cw, sh, t1 = (n2() for _ in range(7))
    r = c.af(th, a, ACT.Tanh, r1, scale=0.5)
    x = c.ts(t1, th, -1.0, 1.0, ALU.mult, ALU.add, r)
    x = c.recip(t1, x)
    x = c.stt(em1, th, 2.0, t1, ALU.mult, ALU.mult, x)
    e = c.ts(ea, em1, 1.0, None, ALU.add, None, x)
    s = phase_sin(c, sw, w, t1, 0.0, [x, e, r2])
    s = phase_sin(c, cw, w, t1, np.pi / 2, s)
    h = c.ts(th, w, 0.5, None, ALU.mult, None, s)
    s = phase_sin(c, sh, th, t1, 0.0, h)
    x = c.tt(em1, em1, cw, ALU.mult, s)
    y = c.tt(sh, sh, sh, ALU.mult, x)
    x = c.stt(em1, sh, -2.0, em1, ALU.mult, ALU.add, y)
    y = c.tt(sw, sw, ea, ALU.mult, x)
    cr, ci, ar, ai = w_of("cre"), w_of("cim"), w_of("are"), w_of("aim")
    nr, ni, dr, di, den = th, ea, cw, sh, n2()
    x = c.tt(nr, em1, cr, ALU.mult, y)
    y = c.tt(t1, sw, ci, ALU.mult, y)
    x = c.tt(nr, nr, t1, ALU.subtract, x, y)
    y = c.tt(ni, em1, ci, ALU.mult, x)
    z = c.tt(t1, sw, cr, ALU.mult, x)
    y = c.tt(ni, ni, t1, ALU.add, y, z)
    x = c.tt(den, ar, ar, ALU.mult, y)
    z = c.tt(t1, ai, ai, ALU.mult, y)
    x = c.tt(den, den, t1, ALU.add, x, z)
    x = c.recip(den, x)
    x = c.ts(den, den, 2.0, None, ALU.mult, None, x)
    x = c.tt(dr, nr, ar, ALU.mult, x)
    z = c.tt(t1, ni, ai, ALU.mult, x)
    x = c.tt(dr, dr, t1, ALU.add, z)
    x = c.tt(di, ni, ar, ALU.mult, x)
    z = c.tt(t1, nr, ai, ALU.mult, x)
    x = c.tt(di, di, t1, ALU.subtract, z)
    x = c.tt(dr, dr, den, ALU.mult, x)
    x = c.tt(di, di, den, ALU.mult, x)
    NQ = 16
    mag, s_, t_, u_, wl = (tmp(NQ * NS) for _ in range(5))
    part = tmp(NS)
    v = lambda q: q.rearrange("p (n l) -> p n l", n=NQ)
    for k in range(DC):
        for n0 in range(0, N, NQ):
            ak, wk, drk, dik = (q[:, k * N + n0:k * N + n0 + NQ] for q in (a, w, dr, di))
            y = c.tt(v(mag), each(ak, NS), rows_of(c.const("pos"), NQ), ALU.mult, x)
            y = c.af(mag, mag, ACT.Exp, y)
            z = c.tt(v(wl), each(wk, NS), rows_of(c.const("pos"), NQ), ALU.mult, x)
            z = phase_sin(c, s_, wl, t_, np.pi / 2, z)
            z = c.tt(v(s_), v(s_), each(drk, NS), ALU.mult, z)
            z2 = phase_sin(c, t_, wl, u_, 0.0, z)
            z2 = c.tt(v(t_), v(t_), each(dik, NS), ALU.mult, z2)
            z = c.tt(s_, s_, t_, ALU.subtract, z2)
            z = c.tt(s_, s_, mag, ALU.mult, z, y)
            dst = part if n0 else kern[:, k]
            x = c.reduce(dst, s_.rearrange("p (n l) -> p l n", n=NQ), ALU.add, z)
            if n0:
                x = c.tt(kern[:, k], kern[:, k], part, ALU.add, x)
    c.kern_ok = x



BLOCKS = [("L0_xattn", l0_xattn), ("L0_attn", l0_attn), ("L0_ffn", l0_ffn), ("L1_xattn", l1_xattn),
          ("L1_attn", l1_attn), ("L1_ffn", l1_ffn), ("L2_xattn", l2_xattn), ("L2_attn", l2_attn),
          ("L2_ffn", l2_ffn), ("L3_xattn", l3_xattn), ("L3_attn", l3_attn), ("L3_ffn", l3_ffn)]


def build(nc, dram, out, at, only=None):
    todo = [BLOCKS[i] for i in only] if only is not None else BLOCKS
    with ExitStack() as ctx:
        c = Core(nc, ctx, dram, at)
        x_in, x_out = c.new_sem("x_and_consts_loaded"), c.new_sem("x_stored")
        c.sp.silent(lambda e: e.dma_start(c.X, dram["x"]).then_inc(x_in, 16))
        c.sp.silent(lambda e: e.dma_start(c.consts, dram["w_const"]).then_inc(x_in, 16))
        for q in (c.pe, c.dve, c.act, c.pool):
            q.wait((x_in, 32))
        for i, (name, body) in enumerate(todo):
            c.begin(name, todo[i + 1][0] if i + 1 < len(todo) else None)
            body(c)
            c.end()
        c.sp.wait(c.ends[-1])
        c.sp.silent(lambda e: e.dma_start(out, c.X).then_inc(x_out, 16))
        c.sp.wait((x_out, 16))

        block = ctx.enter_context(nc.Block())

        @block.sync
        def _(e):
            for op in c.sp.ops:
                op(e)

        @block.tensor
        def _(e):
            for op in c.pe.ops:
                op(e)

        @block.vector
        def _(e):
            for op in c.dve.ops:
                op(e)

        @block.scalar
        def _(e):
            for op in c.act.ops:
                op(e)

        @block.gpsimd
        def _(e):
            for op in c.pool.ops:
                op(e)


def kernel(**inputs):
    import concourse.bacc as _bacc
    from concourse.bass_utils import run_bass_kernel_spmd as _run

    at, arrays = host_layout(inputs)
    nc = _bacc.Bacc("TRN2", target_bir_lowering=False, num_devices=1)
    dram = {}
    for name, a in arrays.items():
        dram[name] = nc.dram_tensor(f"in_{name}", a.shape, mybir.dt.from_np(a.dtype), kind="ExternalInput").ap()
    out = nc.dram_tensor("out_x", (P, TILES, D), F32, kind="ExternalOutput").ap()
    build(nc, dram, out, at)
    r = _run(nc, [{f"in_{n}": a for n, a in arrays.items()}], core_ids=[0])
    x = r.results[0]["out_x"]
    return x.reshape(P, TILES, D).transpose(1, 0, 2).reshape(NB, NS, D)
```

```python
from contextlib import ExitStack

import numpy as np

import concourse.bass as bass
from concourse import mybir

F32 = mybir.dt.float32
F32R = mybir.dt.float32r
BF16 = mybir.dt.bfloat16
U8 = mybir.dt.uint8
U32 = mybir.dt.uint32
I32 = mybir.dt.int32
ALU = mybir.AluOpType
ACT = mybir.ActivationFunctionType
AX = mybir.AxisListType.X

P = 128
NB, NS, D = 32, 32, 256
NT = NB * NS
TILES = NT // P
BT = P // NS
DC = D // P
G, DV = 257, 192
V1 = DV - P
GE = G + G % 2
CT0, CT1, CK = 0, GE, 2 * GE
NEG = -1.0e30
HALF = 512
LN_EPS = 1e-5
ROUND = 12582912.0
TWO_PI_HI, TWO_PI_LO = 6.28125, 0.0019353071795864769
PI_CLAMP = 3.1415925


class Queue:

    def __init__(self, name):
        self.name, self.ops, self.sem, self.n, self.seen = name, [], None, 0, {}

    def wait(self, *tickets):
        for t in tickets:
            if t is None:
                continue
            if isinstance(t, list):
                self.wait(*t)
                continue
            s, v = t
            if self.seen.get(id(s), 0) < v:
                self.seen[id(s)] = v
                self.ops.append(lambda e, s=s, v=v: e.wait_ge(s, v))

    def __call__(self, fn, *tickets):
        self.wait(*tickets)
        self.n += 1
        self.ops.append(lambda e, s=self.sem: fn(e).then_inc(s, 1))
        return (self.sem, self.n)

    def silent(self, fn, *tickets):
        self.wait(*tickets)
        self.ops.append(fn)

    def now(self):
        return (self.sem, self.n) if self.n else None


class Pair:

    def __init__(self, high, low):
        self.high, self.low = high, low

    def __getitem__(self, i):
        return Pair(self.high[i], self.low[i])

    def rearrange(self, form, **sizes):
        return Pair(self.high.rearrange(form, **sizes), self.low.rearrange(form, **sizes))


class Slot:

    def __init__(self, t, sem=None):
        self.t, self.free, self.sem, self.n = t, [], sem, 0


class Ring:
    def __init__(self, slots):
        self.slots, self.i = slots, 0

    def next(self):
        self.i += 1
        return self.slots[(self.i - 1) % len(self.slots)]



def chunks(w, rows=P):
    k = -(-w.shape[0] // rows)
    out = np.zeros((k * rows, w.shape[1]), w.dtype)
    out[:w.shape[0]] = w
    return out.reshape(k, rows, w.shape[1]).transpose(1, 0, 2).reshape(rows, -1)


def col(b):
    return chunks(b.reshape(-1, 1))


def row(b):
    return b.reshape(1, -1)


def wide(b):
    return np.broadcast_to(b.reshape(1, -1), (P, b.size))


def layout(pieces):
    at, n = {}, 0
    for name, a in pieces.items():
        at[name] = (a.shape[0], n, n + a.shape[1])
        n += a.shape[1]
    out = np.zeros((P, n), np.float32)
    for name, a in pieces.items():
        r, c0, c1 = at[name]
        out[:r, c0:c1] = a
    return at, out


def words(mask):
    pad = -mask.shape[1] % 4
    return np.ascontiguousarray(np.pad(mask, ((0, 0), (0, pad)))).view(np.uint32)


def head_pad_k(wk, dh, aug):
    h = wk.shape[1] // dh
    out = np.zeros((P, h, aug), np.float32)
    for i in range(h):
        f = i * dh % P
        out[f:f + dh, i, :] = wk[:, i * dh:(i + 1) * dh].T
    return out.reshape(P, -1)


def head_pad_v(wv, dh):
    h = wv.shape[1] // dh
    out = np.zeros((wv.shape[0], h, P), np.float32)
    for i in range(h):
        f = i * dh % P
        out[:, i, f:f + dh] = wv[:, i * dh:(i + 1) * dh]
    return out.reshape(wv.shape[0], -1)


def host_layout(a):
    p, s = {}, {}
    eye = np.eye(P, dtype=np.float32)
    tok = np.arange(P)
    same = (tok[:, None] // NS == tok[None, :] // NS)
    causal = same & (tok[:, None] % NS <= tok[None, :] % NS)
    head16 = (np.arange(P)[:, None] // 16 == np.arange(8)[None, :]).astype(np.float32)
    p["const"] = {
        "eye": eye, "ones": np.ones((P, HALF), np.float32), "causal": causal.astype(np.float32),
        "mhalf": np.full((P, P), -0.5, np.float32), "half": np.full((P, P), 0.5, np.float32),
        "head16": head16, "iota8": wide(np.arange(8, dtype=np.float32)),
        "causal_neg": np.tile(np.where(np.arange(NS)[None, :] <= np.arange(NS)[:, None], 0.0, NEG)
                              .astype(np.float32), (BT, 1)),
        "diag32": np.tile(np.eye(NS, dtype=np.float32), (BT, 1)),
        "pos": wide(np.arange(NS, dtype=np.float32)),
        "not_first": wide((np.arange(NT) % NS != 0).astype(np.float32)),
    }
    L = lambda b, n: np.asarray(a[f"{b}_{n}"])
    b = "L0_xattn"
    p[b] = {"wq": chunks(L(b, "Wq").T), "wkv0": L(b, "Wkv").T[:P], "wkv1": L(b, "Wkv").T[P:],
            "wlkv": chunks(L(b, "Wlkv").T), "wo": chunks(L(b, "Wo").T), "bo": row(L(b, "bo")),
            "gx0": col(L(b, "ln_x_g")[:P]), "gx1": L(b, "ln_x_g")[P:, None],
            "bx0": col(L(b, "ln_x_b")[:P]), "bx1": L(b, "ln_x_b")[P:, None],
            "gl": col(L(b, "ln_l_g")), "bl": col(L(b, "ln_l_b")),
            "qn": wide(L(b, "qn_g")), "kn": wide(L(b, "kn_g"))}
    b = "L0_attn"
    flat = lambda w: w.transpose(1, 0, 2).reshape(D, -1)
    p[b] = {"wq": chunks(flat(L(b, "P_q"))), "wk": chunks(flat(L(b, "P_k"))),
            "wv": chunks(flat(L(b, "P_v")))}
    p[b] |= {"wo": chunks(L(b, "P_o").transpose(0, 2, 1).reshape(-1, D))}
    b = "L0_ffn"
    p[b] = {"gw1": chunks(L(b, "gW1").T), "gb1": col(L(b, "gb1")), "gw2": chunks(L(b, "gW2").T),
            "gw2b": chunks(np.repeat(L(b, "gW2").T[:, :, None], P, 2).reshape(D, -1)),
            "gb2w": wide(L(b, "gb2")), "gb2": L(b, "gb2")[:, None],
            "eb1": L(b, "eb1"), "eb2": L(b, "eb2")}
    s["eW1"] = np.ascontiguousarray(L(b, "eW1").reshape(8, 8, P, DC, P).transpose(1, 4, 0, 3, 2)
                                    .reshape(8, P, 8 * DC * P))
    s["eW2"] = np.ascontiguousarray(L(b, "eW2").reshape(4, 2, D, 8, P).transpose(0, 4, 3, 1, 2)
                                    .reshape(4, P, 8 * 2 * D))
    b = "L1_xattn"
    wk = L(b, "Wk")
    p[b] = {"wq": chunks(L(b, "Wq")), "wk0": head_pad_k(wk, 32, DV),
            "wv0": L(b, "Wv")[:P], "wv1": L(b, "Wv")[P:],
            "fi": chunks(L(b, "W_film_in")), "bfi": col(L(b, "b_film_in")),
            "fo": chunks(L(b, "W_film_out")), "bfo": col(L(b, "b_film_out")),
            "gi": col(L(b, "g_norm_in")), "bi": col(L(b, "b_norm_in")),
            "gf": col(L(b, "g_ffn")), "bf": col(L(b, "b_ffn")),
            "go": wide(L(b, "g_norm_out")), "bo": wide(L(b, "b_norm_out")),
            "b1": col(L(b, "b1")), "b2": row(L(b, "b2")), "logdt": col(L(b, "log_dt")),
            "are": chunks(L(b, "A_re")), "aim": chunks(L(b, "A_im")),
            "cre": chunks(L(b, "C_re")), "cim": chunks(L(b, "C_im")),
            "dskip": col(L(b, "D_skip")), "mg": wide(L(b, "mod_gate"))}
    p[b] |= {"w1": chunks(L(b, "W1")), "w2": chunks(L(b, "W2"))}
    b = "L1_attn"
    p[b] = {"wq": chunks(L(b, "W_q").T), "wk": chunks(L(b, "W_k").T), "wv": chunks(L(b, "W_v").T),
            "wo": chunks(L(b, "W_o").T), "logc": wide(L(b, "log_c")), "beta": wide(L(b, "beta")),
            "ab": wide(L(b, "attention_bias"))}
    b = "L1_ffn"
    p[b] = {"ws": chunks(L(b, "Ws")), "bs": row(L(b, "bs"))}
    s["Wgu"] = np.stack([np.concatenate([chunks(L(b, "Wg")[e]), chunks(L(b, "Wu")[e]),
                                         chunks(L(b, "Wd")[e])], 1) for e in range(8)])
    b = "L2_xattn"
    p[b] = {"wq": chunks(L(b, "Wq")),
            "wk": L(b, "Wk").T.reshape(8, P, DV).transpose(1, 0, 2).reshape(P, -1),
            "bo": row(L(b, "bo"))}
    p[b] |= {"wv0": L(b, "Wv")[:P], "wv1": L(b, "Wv")[P:], "wo": chunks(L(b, "Wo"))}
    b = "L2_attn"
    p[b] = {n.lower(): chunks(L(b, n)) for n in ("Wk", "Wv", "Wq", "Wkp", "Wqp", "Wo")}
    p[b] |= {n: col(L(b, n)) for n in ("bk", "bv", "bq", "bkp", "bqp", "phase_scale", "ln_g", "ln_b")}
    p[b] |= {"bo": row(L(b, "bo"))}
    b = "L2_ffn"
    p[b] = {"w": chunks(L(b, "weight").T), "bias": wide(L(b, "bias"))}
    b = "L3_xattn"
    wka = np.concatenate([L(b, "Wk"), L(b, "bk")[None]], 0)
    wva = np.concatenate([L(b, "Wv"), L(b, "bv")[None]], 0)
    p[b] = {"wq": chunks(L(b, "Wq")), "bq": col(L(b, "bq")), "wk": head_pad_k(wka, 16, DV + 1),
            "wv0": head_pad_v(wva[:P], 16), "wv1": head_pad_v(wva[P:], 16),
            "wo": chunks(L(b, "Wo")), "bo": row(L(b, "bo"))}
    b = "L3_attn"
    qc = np.zeros((DC, P, 4, 2, 64), np.float32)
    for h in range(16):
        qc[h // 8, h % 8 * 16:h % 8 * 16 + 16, h % 8 // 2, h % 2] = L(b, "q_c")[:, h * 16:h * 16 + 16].T
    p[b] = {n.lower(): chunks(L(b, n).T) for n in ("Wq", "Wk", "Wv", "Wo")}
    p[b] |= {"bq": col(L(b, "bq")), "bk": col(L(b, "bk")), "bv": row(L(b, "bv")), "bo": row(L(b, "bo")),
             "qc": qc.transpose(1, 0, 2, 3, 4).reshape(P, -1), "beta": col(np.repeat(L(b, "beta"), 16))}
    b = "L3_ffn"
    p[b] = {"gate": chunks(L(b, "w_gate")), "up": chunks(L(b, "w_up")), "down": chunks(L(b, "w_down"))}
    at, arrays = {}, {}
    for name, pieces in p.items():
        at[name], arrays[f"w_{name}"] = layout(pieces)
    for name, x in s.items():
        arrays[f"s_{name}"] = x
    arrays["x"] = np.ascontiguousarray(np.asarray(a["x"]).reshape(TILES, P, D).transpose(1, 0, 2))
    ctx = np.asarray(a["ctx_768"])
    aug = np.concatenate([ctx, np.ones((NB, G, 1), np.float32)], 2)
    pack = np.zeros((NB, P, 2 * GE + 3 * (DV + 1)), np.float32)
    tr = aug.transpose(0, 2, 1)
    pack[:, :, CT0:CT0 + G], pack[:, :V1 + 1, CT1:CT1 + G] = tr[:, :P], tr[:, P:]
    for i in range(3):
        part = aug[:, i * P:(i + 1) * P]
        pack[:, :part.shape[1], CK + i * (DV + 1):CK + (i + 1) * (DV + 1)] = part
    arrays["ctx"] = pack
    arrays["ctx_last"] = np.ascontiguousarray(ctx[:, G - 1])
    arrays["keep0"] = words(np.asarray(a["mask_BxS2_bk0"]))
    arrays["keep1"] = words(np.asarray(a["mask_BxS2_bf1"]))
    arrays["qmask"] = words(np.tile(np.asarray(a["mask_BxS_bf1"]).T, (4, 1)))
    return at, arrays


class Core:

    WEIGHTS = 9500
    SCRATCH = 25400
    PARTS = {"L0_ffn": 16384, "L1_ffn": 25000, "L2_xattn": 17700, "L3_xattn": 17700}

    def __init__(self, nc, ctx, dram, at):
        self.nc, self.ctx, self.dram, self.at = nc, ctx, dram, at
        self.pe, self.dve, self.act, self.pool, self.sp = (Queue(n) for n in ("pe", "dve", "act", "pool", "sp"))
        self.X = self.sb("X", TILES * D).rearrange("p (t d) -> p t d", t=TILES)
        self.XN = self.sb("XN", TILES * D).rearrange("p (t d) -> p t d", t=TILES)
        self.XT = self.sb("XT", DC * NT).rearrange("p (c n) -> p c n", c=DC)
        self.consts = self.sb("consts", max(c1 for _, _, c1 in at["const"].values()))
        self.stats = self.sb("stats", TILES * 6).rearrange("p (t k) -> p t k", t=TILES)
        self.meanvar = self.sb("meanvar", TILES * 2).rearrange("p (t k) -> p t k", t=TILES)
        self.rstd = self.sb("rstd", TILES)
        self.kern = self.sb("kern", DC * NS).rearrange("p (k l) -> p k l", k=DC)
        self.kern_ok = None
        self.areas = [self.sb(f"weights{i}", self.WEIGHTS) for i in range(2)]
        self.lower_memory = ctx.enter_context(ExitStack())
        self.upper_memory = ctx.enter_context(ExitStack())
        self.banks = Ring([Slot(ctx.enter_context(nc.psum_tensor(f"bank{i}", [P, HALF], F32))[:, :])
                           for i in range(8)])
        self.weight_sem = [self.new_sem(f"weights{i}_loaded") for i in range(2)]
        self.block_no = 0
        self.prefetched = None
        self.ends = []

    def sb(self, name, cols):
        return self.ctx.enter_context(self.nc.sbuf_tensor(name, [P, cols], F32))[:, :]

    def new_sem(self, name):
        return self.ctx.enter_context(self.nc.semaphore(name))

    def const(self, name):
        r, c0, c1 = self.at["const"][name]
        return self.consts[:r, c0:c1]

    def load_weights(self, name, area):
        cols = self.dram[f"w_{name}"].shape[1]
        assert cols <= self.WEIGHTS, (name, cols)
        sem, n = self.weight_sem[area], 16 * (self.loads.get(area, 0) + 1)
        self.loads[area] = self.loads.get(area, 0) + 1
        if len(self.ends) >= 1:
            self.sp.wait(self.ends[-1])
        self.sp.silent(lambda e: e.dma_start(self.areas[area][:, :cols], self.dram[f"w_{name}"]).then_inc(sem, 16))
        return (sem, n)

    loads = {}

    def begin(self, name, nxt):
        for q in (self.pe, self.dve, self.act, self.pool):
            q.sem, q.n = self.new_sem(f"{name}_{q.name}"), 0
            if self.ends:
                q.wait(self.ends[-1])
        area = self.block_no % 2
        self.w_ready = self.prefetched or self.load_weights(name, area)
        self.prefetched = self.load_weights(nxt, 1 - area) if nxt else None
        for q in (self.pe, self.dve, self.act, self.pool):
            q.wait(self.w_ready)
        self.area, self.name = self.areas[area], name
        self.tail = self.WEIGHTS
        self.upper_memory.close()
        self.lower_memory.close()
        n = self.PARTS.get(name, 0)
        if n:
            self.take_parts(self.lower_memory, "parts", n)
        self.take_scratch("scratch", self.SCRATCH - n)
        self.next = (nxt, self.areas[1 - area])
        self.block_no += 1
        for b in self.banks.slots:
            b.free = []

    def fence(self):
        now = [q.now() for q in (self.pe, self.dve, self.act, self.pool)]
        for q in (self.pe, self.dve, self.act, self.pool, self.sp):
            q.wait(now)

    def end(self):
        self.ends.append([q.now() for q in (self.pe, self.dve, self.act, self.pool)])

    def w(self, piece):
        r, c0, c1 = self.at[self.name][piece]
        return self.area[:r, c0:c1]

    def w_next(self, piece):
        name, area = self.next
        r, c0, c1 = self.at[name][piece]
        return area[:r, c0:c1]

    def wc(self, piece, k):
        return self.w(piece).rearrange("p (k n) -> p k n", k=k)

    def tmp(self, cols, rows=P):
        a = self.scratch[:rows, self.used:self.used + cols]
        self.used += cols
        assert self.used <= self.scratch_cols, (self.name, self.used)
        return a

    def spare(self, cols, rows=P):
        self.tail -= cols
        assert self.tail >= self.dram[f"w_{self.name}"].shape[1], self.name
        return self.area[:rows, self.tail:self.tail + cols]

    def mm(self, out, terms, *tickets):
        self.pe.wait(*tickets)
        for i, (l, r) in enumerate(terms):
            last = i == len(terms) - 1
            f = lambda e, l=l, r=r, i=i, last=last: e.matmul(out, lhsT=l, rhs=r, start=i == 0, stop=last)
            t = self.pe(f) if last else self.pe.silent(f)
        return t

    def halves_of_xn(self):
        a = self.XN.rearrange("p t d -> p (t d)")
        return a[:, :TILES * D // 2], a[:, TILES * D // 2:]

    def take_parts(self, memory, what, cols):
        a = memory.enter_context(self.nc.sbuf_tensor(f"{self.name}_{what}", [P, cols], F32R))
        self.parts, self.parts_cols, self.parts_used = a[:, :], cols, 0

    def take_scratch(self, what, cols):
        a = self.upper_memory.enter_context(self.nc.sbuf_tensor(f"{self.name}_{what}", [P, cols], F32))
        self.scratch, self.scratch_cols, self.used = a[:, :], cols, 0

    def scratch_to_parts(self):
        self.fence()
        self.upper_memory.close()
        self.take_parts(self.upper_memory, "more_parts", self.scratch_cols)

    def part(self, cols):
        u = self.parts_used
        self.parts_used += 2 * cols
        assert self.parts_used <= self.parts_cols, (self.name, self.parts_used)
        return Pair(self.parts[:, u:u + cols], self.parts[:, u + cols:u + 2 * cols])

    def split(self, x, pair, *tickets, q=None):
        d = self.copy(self.act, pair.high, x, *tickets)
        return self.tt(pair.low, x, pair.high.bitcast(F32), ALU.subtract, d, q=q)

    def mm_split(self, out, terms, *tickets):
        return self.mm(out, [lr for l, r in terms
                             for lr in ((l.high, r.high), (l.low, r.high), (l.high, r.low))], *tickets)

    def transpose(self, out, in_, *tickets):
        k = in_.shape[0]
        return self.pe(lambda e: e.transpose(out, in_, self.const("eye")[:k, :k]), *tickets)

    def copy(self, q, out, in_, *tickets):
        if q is self.act:
            return q(lambda e: e.activation(out, in_, ACT.Copy), *tickets)
        return q(lambda e: e.tensor_copy(out, in_), *tickets)

    def tt(self, out, a, b, op, *tickets, q=None):
        return (q or self.dve)(lambda e: e.tensor_tensor(out, a, b, op), *tickets)

    def ts(self, out, a, s1, s2, op0, op1, *tickets, q=None):
        if op1 is None:
            return (q or self.dve)(lambda e: e.tensor_scalar(out, a, s1, None, op0), *tickets)
        return (q or self.dve)(lambda e: e.tensor_scalar(out, a, s1, s2, op0, op1), *tickets)

    def stt(self, out, a, s, b, op0, op1, *tickets):
        return self.dve(lambda e: e.scalar_tensor_tensor(out=out, in0=a, scalar=s, in1=b, op0=op0, op1=op1),
                        *tickets)

    def recip(self, x, *tickets, out=None):
        out = x if out is None else out
        return self.dve(lambda e: e.reciprocal(out, x), *tickets)

    def power(self, x, which, *tickets, out=None):
        out = x if out is None else out
        return self.tt(out, x, self.const(which)[:x.shape[0], :x.shape[1]], ALU.pow, *tickets, q=self.pool)

    def reduce(self, out, in_, op, *tickets):
        return self.dve(lambda e: e.tensor_reduce(out, in_, AX.X, op), *tickets)

    def af(self, out, in_, func, *tickets, bias=0.0, scale=1.0, accum=None):
        if accum is None:
            return self.act(lambda e: e.activation(out, in_, func, bias=bias, scale=scale), *tickets)
        return self.act(lambda e: e.activation(out, in_, func, bias=bias, scale=scale, accum_out=accum), *tickets)


    def normalise(self, src, dst, *tickets):
        done = []
        for h in (slice(0, TILES // 2), slice(TILES // 2, TILES)):
            tiles = range(h.start, h.stop)
            for t in tiles:
                st = self.dve(lambda e, t=t: e.bn_stats(self.stats[:, t, :], src[:, t, :]), *tickets)
            for t in tiles:
                st = self.dve(lambda e, t=t: e.bn_aggr(self.meanvar[:, t, :], self.stats[:, t, :]), st)
            r = self.ts(self.rstd[:, h], self.meanvar[:, h, 1], LN_EPS, None, ALU.add, None, st)
            done.append((tiles, self.power(self.rstd[:, h], "mhalf", r)))
        return [self.ts(dst[:, t, :], src[:, t, :], self.meanvar[:, t, 0:1], self.rstd[:, t:t + 1],
                        ALU.subtract, ALU.mult, r) for tiles, r in done for t in tiles]

    def to_features(self, src, dst, src_ready, gain=None, shift=None, *tickets):
        done = []
        for h in range(2):
            for c in range(DC):
                b = self.banks.next()
                for j in range(4):
                    t = 4 * h + j
                    tr = self.transpose(b.t[:, j * P:(j + 1) * P], src[:, t, c * P:(c + 1) * P],
                                        b.free, src_ready[t], *tickets)
                o = dst[:, c, h * HALF:(h + 1) * HALF]
                if gain is not None:
                    d = self.ts(o, b.t, gain[:, c:c + 1], shift[:, c:c + 1], ALU.mult, ALU.add, tr)
                else:
                    d = self.copy(self.act, o, b.t, tr)
                b.free = [d]
                done.append(d)
        return done

    def enter(self):
        ready = self.normalise(self.X, self.XN)
        return ready, self.to_features(self.XN, self.XT, ready)

    def project(self, dst, w, k, src, outs, ready, bias=None, scale=None, func=None):
        done = []
        for o in range(outs):
            for h in range(2):
                b = self.banks.next()
                cols = slice(h * HALF, (h + 1) * HALF)
                m = self.mm(b.t, [(w[:, c, o * P:(o + 1) * P], src[:, c, cols]) for c in range(k)],
                            b.free, ready, self.w_ready)
                bb = 0.0 if bias is None else bias[:, o:o + 1]
                if func is not None:
                    d = self.af(dst[:, o, cols], b.t, func, m, bias=bb)
                elif bias is None:
                    d = self.copy(self.act if (o + h) % 2 else self.dve, dst[:, o, cols], b.t, m)
                else:
                    d = self.ts(dst[:, o, cols], b.t, bb, None, ALU.add, None, m)
                b.free = [d]
                done.append(d)
        return done

    def add_output(self, src, w, k, ready, bias=None, tiles=range(TILES), cols=None):
        done = []
        for t in tiles:
            b = self.banks.next()
            o = b.t[:, :D]
            sel = cols if cols is not None else slice(t * P, (t + 1) * P)
            terms = [(src[:, c, sel], w[:, c, :]) for c in range(k)]
            if bias is not None:
                terms.append((self.const("ones")[0:1, :P], bias))
            m = self.mm(o, terms, b.free, ready, self.w_ready)
            d = self.tt(self.X[:, t, :], o, self.X[:, t, :], ALU.add, m)
            b.free = [d]
            done.append(d)
        return done


def l1_ffn(c):
    E, F = 8, 688
    FC = -(-F // P)
    sizes = [min(P, F - P * f) for f in range(FC)]
    widths = DC * F, DC * F, FC * D
    starts = 0, DC * F, 2 * DC * F
    raw = [Slot(c.spare(n), c.new_sem(f"expert_weights{i}")) for i, n in enumerate(widths)]
    split = [Slot(c.part(n)) for n in widths]

    def load(e, i):
        s = raw[i]
        c.sp.wait(s.free)
        c.sp.silent(lambda q: q.dma_start(s.t, c.dram["s_Wgu"][e, :, starts[i]:starts[i] + widths[i]]).then_inc(s.sem, 16))
        s.n += 16

    def split_weights(e, i):
        d = c.split(raw[i].t, split[i].t, (raw[i].sem, raw[i].n), split[i].free, q=(c.dve, c.pool, c.pool)[i])
        raw[i].free = [d]
        if e + 1 < E:
            load(e + 1, i)
        return d

    c.sp.wait(c.ends[-1] if c.ends else None)
    for i in range(3):
        load(0, i)
    ready, xt = c.enter()
    w_ok = [split_weights(0, i) for i in range(3)]
    logit = c.spare(TILES * E).rearrange("p (t e) -> p t e", t=TILES)
    top = c.spare(TILES * 8).rearrange("p (t e) -> p t e", t=TILES)
    idx = c.spare(TILES * 8).bitcast(U32).rearrange("p (t e) -> p t e", t=TILES)
    idf = c.spare(TILES * 8).rearrange("p (t e) -> p t e", t=TILES)
    comb = c.spare(TILES * E).rearrange("p (t e) -> p t e", t=TILES)
    hot = c.spare(TILES * E).rearrange("p (t e) -> p t e", t=TILES)
    wt = c.spare(TILES * 2).rearrange("p (t k) -> p t k", t=TILES)
    b = c.banks.next()
    for t in range(TILES):
        m = c.mm(b.t[:, t * E:(t + 1) * E],
                 [(c.XT[:, k, t * P:(t + 1) * P], c.wc("ws", DC)[:, k, :]) for k in range(DC)]
                 + [(c.const("ones")[0:1, :P], c.w("bs"))], b.free, xt, c.w_ready)
    cp = c.copy(c.dve, logit, b.t[:, :TILES * E], m)
    b.free = [cp]
    for t in range(TILES):
        mx = c.dve(lambda e, t=t: e.max(top[:, t, :], logit[:, t, :]), cp)
        mi = c.dve(lambda e, t=t: e.max_index(idx[:, t, :], top[:, t, :], logit[:, t, :]), mx)
    ix = c.copy(c.dve, idf, idx, mi)
    d1 = c.tt(wt[:, :, 1], top[:, :, 1], top[:, :, 0], ALU.subtract, mx)
    ex = c.af(wt[:, :, 1], wt[:, :, 1], ACT.Exp, d1)
    s1 = c.ts(wt[:, :, 0], wt[:, :, 1], 1.0, None, ALU.add, None, ex)
    s2 = c.dve(lambda e: e.reciprocal(wt[:, :, 0], wt[:, :, 0]), s1)
    s3 = c.tt(wt[:, :, 1], wt[:, :, 1], wt[:, :, 0], ALU.mult, s2)
    for t in range(TILES):
        h1 = c.ts(comb[:, t, :], c.const("iota8"), idf[:, t, 0:1], wt[:, t, 0:1], ALU.is_equal, ALU.mult, ix, s3)
        h2 = c.ts(hot[:, t, :], c.const("iota8"), idf[:, t, 1:2], wt[:, t, 1:2], ALU.is_equal, ALU.mult, ix, s3)
    comb_ready = c.tt(comb, comb, hot, ALU.add, h1, h2)
    x = c.part(DC * NT).rearrange("p (k n) -> p k n", k=DC)
    xs = [c.split(c.XT[:, k], x[:, k], xt, q=(c.pool, c.dve)[k]) for k in range(DC)]
    hid = c.part(FC * NT).rearrange("p (f n) -> p f n", f=FC)
    gact = Ring([Slot(c.spare(HALF)) for _ in range(4)])
    hid_free = [[], []]
    wg, wu = (split[i].t.rearrange("p (k f) -> p k f", k=DC) for i in (0, 1))
    wd = split[2].t.rearrange("p (k d) -> p k d", k=FC)
    last_x = [None] * TILES
    for e_ in range(E):
        hid_done = [[], []]
        for h in range(2):
            cols = slice(h * HALF, (h + 1) * HALF)
            for f in range(FC):
                n = sizes[f]
                fs = slice(f * P, f * P + n)
                bg, bu = c.banks.next(), c.banks.next()
                mg = c.mm_split(bg.t[:n], [(wg[:, k, fs], x[:, k, cols]) for k in range(DC)], bg.free, xs, w_ok[0])
                mu = c.mm_split(bu.t[:n], [(wu[:, k, fs], x[:, k, cols]) for k in range(DC)], bu.free, w_ok[1])
                g = gact.next()
                a = c.af(g.t[:n], bg.t[:n], ACT.Silu, mg, g.free)
                bg.free = [a]
                v = c.tt(g.t[:n], g.t[:n], bu.t[:n], ALU.mult, a, mu)
                bu.free = [v]
                v = c.split(g.t[:n], hid[:n, f, cols], v, hid_free[h], q=c.pool if f % 2 else c.dve)
                g.free = [v]
                hid_done[h].append(v)
            if h == 0 and e_:
                w_ok[2] = split_weights(e_, 2)
        split[0].free = split[1].free = [mu]
        down_ok = w_ok[2]
        if e_ + 1 < E:
            w_ok[:2] = [split_weights(e_ + 1, i) for i in range(2)]
        for h in range(2):
            for t in range(4 * h, 4 * h + 4):
                b = c.banks.next()
                m = c.mm_split(b.t[:, :D], [(hid[:sizes[f], f, t * P:(t + 1) * P], wd[:sizes[f], f])
                                            for f in range(FC)], b.free, hid_done[h], down_ok)
                last_x[t] = c.stt(c.X[:, t, :], b.t[:, :D], comb[:, t, e_:e_ + 1], c.X[:, t, :],
                                  ALU.mult, ALU.add, m, comb_ready, ready, last_x[t])
                b.free = [last_x[t]]
            hid_free[h] = [m]
        split[2].free = [m]


def phase_sin(c, out, y, tmp, shift, ready):
    a = c.ts(out, y, 1.0, shift, ALU.mult, ALU.add, ready)
    n = c.ts(tmp, out, 1.0 / (2.0 * np.pi), ROUND, ALU.mult, ALU.add, a)
    n = c.ts(tmp, tmp, ROUND, None, ALU.subtract, None, n)
    r = c.stt(out, tmp, -TWO_PI_HI, out, ALU.mult, ALU.add, n)
    r = c.stt(out, tmp, -TWO_PI_LO, out, ALU.mult, ALU.add, r)
    r = c.ts(out, out, PI_CLAMP, -PI_CLAMP, ALU.min, ALU.max, r)
    return c.af(out, out, ACT.Sin, r)


def phase_sin_cos(c, sin, cos, y, ready, free):
    n = c.ts(cos, y, 1.0 / (2.0 * np.pi), ROUND, ALU.mult, ALU.add, ready, free)
    n = c.ts(cos, cos, ROUND, None, ALU.subtract, None, n)
    r = c.stt(y, cos, -TWO_PI_HI, y, ALU.mult, ALU.add, n)
    r = c.stt(y, cos, -TWO_PI_LO, y, ALU.mult, ALU.add, r)
    r = c.ts(y, y, PI_CLAMP, -PI_CLAMP, ALU.min, ALU.max, r)
    h = c.af(cos, y, ACT.Sin, r, scale=0.5)
    s = c.af(sin, y, ACT.Sin, r, free)
    h = c.tt(cos, cos, cos, ALU.mult, h)
    return s, c.ts(cos, cos, -2.0, 1.0, ALU.mult, ALU.add, h)


def l2_attn(c):
    big = lambda: c.tmp(DC * NT).rearrange("p (k n) -> p k n", k=DC)
    flat = lambda a: a.rearrange("p k n -> p (k n)")
    ready, xt = c.enter()
    key, val, qry, kp, qp, cs, tmp = (big() for _ in range(7))
    k = c.project(key, c.wc("wk", DC), DC, c.XT, DC, xt, bias=c.w("bk"))
    v = c.project(val, c.wc("wv", DC), DC, c.XT, DC, xt, bias=c.w("bv"))
    q = c.project(qry, c.wc("wq", DC), DC, c.XT, DC, xt, bias=c.w("bq"))
    kt = c.project(kp, c.wc("wkp", DC), DC, key, DC, k, bias=c.w("bkp"), func=ACT.Tanh)
    qt = c.project(qp, c.wc("wqp", DC), DC, qry, DC, q, bias=c.w("bqp"), func=ACT.Tanh)
    sn = tmp
    r = []
    for i in range(DC):
        a = c.ts(kp[:, i], kp[:, i], c.w("phase_scale")[:, i:i + 1], None, ALU.mult, None, kt[2 * i:2 * i + 2])
        s, co = phase_sin_cos(c, sn[:, i], cs[:, i], kp[:, i], a, None)
        mem = []
        for trig, ok, to in ((cs, co, key), (sn, s, qry)):
            m = c.tt(trig[:, i], trig[:, i], val[:, i], ALU.mult, ok, v)
            mem.append(c.dve(lambda e, i=i, trig=trig, to=to: e.tensor_tensor_scan(
                to[:, i], c.const("not_first"), trig[:, i], 0.0, ALU.mult, ALU.add), m, kt, qt))
        a = c.ts(qp[:, i], qp[:, i], c.w("phase_scale")[:, i:i + 1], None, ALU.mult, None, qt[2 * i:2 * i + 2])
        s, co = phase_sin_cos(c, sn[:, i], cs[:, i], qp[:, i], a, mem)
        m1 = c.tt(key[:, i], key[:, i], cs[:, i], ALU.mult, co, mem)
        m2 = c.tt(qry[:, i], qry[:, i], sn[:, i], ALU.mult, s, mem, q=c.pool)
        m = c.tt(key[:, i], key[:, i], qry[:, i], ALU.add, m1, m2)
        r.append(c.ts(key[:, i], key[:, i], 1.0 / np.sqrt(D), None, ALU.mult, None, m))
    tm = val.rearrange("p k n -> p (k n)").rearrange("p (t d) -> p t d", t=TILES)
    back = to_tokens(c, key, tm, r)
    tm2 = kp.rearrange("p k n -> p (k n)").rearrange("p (t d) -> p t d", t=TILES)
    n = c.normalise(tm, tm2, back)
    f = c.to_features(tm2, qp, n, c.w("ln_g"), c.w("ln_b"))
    c.add_output(qp, c.wc("wo", DC), DC, [f, ready], c.w("bo"))
    for t in range(TILES):
        c.tt(c.X[:, t, :], c.X[:, t, :], c.XN[:, t, :], ALU.add, c.dve.now())


def to_tokens(c, src, dst, ready):
    done = []
    for t in range(0, TILES, 2):
        b = c.banks.next()
        for j in range(2):
            for k in range(DC):
                tr = c.transpose(b.t[:, j * D + k * P:j * D + (k + 1) * P],
                                 src[:, k, (t + j) * P:(t + j + 1) * P], b.free, ready[k])
        d = c.copy(c.act if t % 4 else c.dve, dst[:, t:t + 2, :], b.t, tr)
        b.free = [d]
        done.append(d)
    return done


def global_max(c, parts, ready):
    one, allp = c.tmp(1), c.tmp(1)
    line = c.tmp(P, 1)
    m = c.reduce(one, parts, ALU.max, ready)
    b = c.banks.next()
    t = c.transpose(b.t[0:1, :P], one, b.free, m)
    m = c.reduce(line[:, 0:1], b.t[0:1, :P], ALU.max, t)
    t = c.mm(b.t[:, 256:257], [(c.const("ones")[0:1, :P], line[:, 0:1])], m)
    m = c.copy(c.dve, allp, b.t[:, 256:257], t)
    b.free = [m]
    return allp, m


def absmax(c, out, in_, ready):
    return c.dve(lambda e: e.tensor_reduce(out, in_, AX.X, ALU.max, apply_absolute_value=True), ready)


def l2_ffn(c):
    FP8_MAX = 448.0
    ready, xt = c.enter()

    def quantise(x, n, ready):
        q, step = c.tmp(n), c.tmp(n)
        out = c.tmp(n // 2).bitcast(BF16)
        part, sc, inv = c.tmp(1), c.tmp(1), c.tmp(1)
        a = absmax(c, part, x, ready)
        big, a = global_max(c, part, a)
        a = c.ts(sc, big, 1e-12, None, ALU.max, None, a)
        a = c.recip(sc, a)
        a = c.ts(sc, sc, FP8_MAX, FP8_MAX, ALU.mult, ALU.min, a)
        i = c.recip(sc, a, out=inv)
        a = c.ts(q, x, sc, FP8_MAX, ALU.mult, ALU.min, a)
        a = c.ts(q, q, -FP8_MAX, None, ALU.max, None, a)
        b = c.dve(lambda e: e.tensor_scalar(step.bitcast(U32), q.bitcast(U32), 0x7F800000, None,
                                            ALU.bitwise_and), a)
        b = c.ts(step, step, 2.0 ** -6, 1.5 * 2.0 ** 20, ALU.max, ALU.mult, b)
        b = c.tt(q, q, step, ALU.add, b)
        b = c.tt(out, q, step, ALU.subtract, b)
        return out, inv, [b, i]

    wq, w_inv, wr = quantise(c.w("w"), DC * D, c.w_ready)
    xq, x_inv, xr = quantise(c.XT.rearrange("p c n -> p (c n)"), DC * NT, xt)
    wq = wq.rearrange("p (c n) -> p c n", c=DC)
    xq = xq.rearrange("p (c n) -> p c n", c=DC)
    sc = c.tmp(1)
    s = c.tt(sc, w_inv, x_inv, ALU.mult, wr, xr)
    res = Ring([Slot((c.tmp(D), c.tmp(D // 2).bitcast(BF16))) for _ in range(2)])
    for t in range(TILES):
        b = c.banks.next()
        m = c.mm(b.t[:, :D], [(xq[:, k, t * P:(t + 1) * P], wq[:, k, :]) for k in range(DC)], b.free, wr, xr)
        r = res.next()
        y, yb = r.t
        d = c.stt(y, b.t[:, :D], sc, c.w("bias"), ALU.mult, ALU.add, m, s, r.free)
        b.free = [d]
        d = c.copy(c.dve, yb, y, d)
        r.free = [c.tt(c.X[:, t, :], yb, c.X[:, t, :], ALU.add, d)]


def l3_ffn(c):
    H, HC, BLK = 768, 6, 32
    QMAX = 32767.0
    ready, xt = c.enter()
    one = c.const("ones")[:, 0:1]

    def dequant(w, cols, ready):
        nb = cols // BLK
        s, inv = c.tmp(nb), c.tmp(nb)
        sb, ib = (v.rearrange("p (b o) -> p b o", o=1).to_broadcast([P, nb, BLK]) for v in (s, inv))
        wv = w.rearrange("p (b k) -> p b k", k=BLK)
        a = absmax(c, s, wv, ready)
        a = c.ts(s, s, 1.0 / 7.0, 1e-12, ALU.mult, ALU.max, a)
        a = c.recip(s, a, out=inv)
        a = c.tt(wv, wv, ib, ALU.mult, a)
        a = c.ts(w, w, ROUND, None, ALU.add, None, a)
        a = c.ts(w, w, ROUND, None, ALU.subtract, None, a)
        a = c.ts(w, w, 7.0, -8.0, ALU.min, ALU.max, a)
        return c.tt(wv, wv, sb, ALU.mult, a)

    def flip(w, rows, cols, ready):
        rc, cc = rows // P, cols // P
        src = w.rearrange("p (r n) -> p r n", r=rc)
        dst = c.tmp(rows * cc).rearrange("p (k r) -> p k r", k=cc)
        done = []
        for k in range(cc):
            for r0 in range(0, rc, 4):
                b = c.banks.next()
                n = min(4, rc - r0)
                for r in range(n):
                    tr = c.transpose(b.t[:, r * P:(r + 1) * P], src[:, r0 + r, k * P:(k + 1) * P], b.free, ready)
                d = c.copy(c.act, dst[:, k, r0 * P:(r0 + n) * P], b.t[:, :n * P], tr)
                b.free = [d]
                done.append(d)
        return dst, done

    def act_scale(parts, ready):
        big, a = global_max(c, parts, ready)
        sc = c.tmp(1)
        a = c.ts(sc, big, 1.0 / QMAX, 1e-12, ALU.mult, ALU.max, a)
        inv = c.tmp(1)
        return (sc, inv), c.recip(sc, a, out=inv)

    def qdq(x, sc, ready, q=None):
        scale, inv = sc
        a = c.ts(x, x, inv, ROUND, ALU.mult, ALU.add, ready, q=q)
        a = c.ts(x, x, ROUND, QMAX, ALU.subtract, ALU.min, a, q=q)
        return c.ts(x, x, -QMAX - 1.0, scale, ALU.max, ALU.mult, a, q=q)

    queue_of = lambda f: c.pool if f == 0 else c.dve

    wg, gr = flip(c.w("gate"), H, D, dequant(c.w("gate"), HC * D, c.w_ready))
    wu, ur = flip(c.w("up"), H, D, dequant(c.w("up"), HC * D, c.w_ready))
    wd, dr = flip(c.w("down"), D, H, dequant(c.w("down"), DC * H, c.w_ready))
    part = c.tmp(1)
    x = c.XT.rearrange("p c n -> p (c n)")
    sc, a = act_scale(part, absmax(c, part, x, xt))
    xq = qdq(x, sc, a)
    up = c.tmp(HC * NT).rearrange("p (f n) -> p f n", f=HC)
    gate = c.tmp(HC * NT).rearrange("p (f n) -> p f n", f=HC)
    parts = c.tmp(HC), c.tmp(HC)

    def branch(y, w, part, wr):
        d = c.project(y, w, DC, c.XT, HC, [xq, wr])
        m = [absmax(c, part[:, f:f + 1], y[:, f], d) for f in range(HC)]
        sc, a = act_scale(part, m)
        return [qdq(y[:, f], sc, a, queue_of(f)) for f in range(HC)]

    g = branch(gate, wg, parts[0], gr)
    u = branch(up, wu, parts[1], ur)
    sig = Ring([Slot(c.tmp(NT)) for _ in range(3)])
    m = []
    for f in range(HC):
        s = sig.next()
        a = c.af(s.t, gate[:, f], ACT.Sigmoid, g[f], s.free)
        a = c.ts(s.t, s.t, 65536.0, ROUND, ALU.mult, ALU.add, a, q=queue_of(f))
        a = c.ts(s.t, s.t, ROUND, 65535.0, ALU.subtract, ALU.min, a, q=queue_of(f))
        a = c.ts(s.t, s.t, 0.0, 1.0 / 65536.0, ALU.max, ALU.mult, a, q=queue_of(f))
        a = c.tt(gate[:, f], gate[:, f], s.t, ALU.mult, a, q=queue_of(f))
        s.free = [a]
        m.append(a)
    m = [absmax(c, parts[0][:, f:f + 1], gate[:, f], m[f]) for f in (1, 2, 3, 4, 5, 0)]
    sc, a = act_scale(parts[0], m)
    m = []
    for f in range(HC):
        b = qdq(gate[:, f], sc, a, queue_of(f))
        m.append(c.tt(gate[:, f], gate[:, f], up[:, f], ALU.mult, b, u, q=queue_of(f)))
    m = [absmax(c, parts[1][:, f:f + 1], gate[:, f], m[f]) for f in (1, 2, 3, 4, 5, 0)]
    sc, a = act_scale(parts[1], m)
    o = [qdq(gate[:, f], sc, a, queue_of(f)) for f in range(HC)]
    c.add_output(gate, wd, HC, [o, dr])



def each(a, n):
    m = a.shape[1]
    return a.rearrange("p (m o) -> p m o", o=1).to_broadcast([P, m, n])


def rows_of(a, m):
    n = a.shape[1]
    return a.rearrange("p (o n) -> p o n", o=1).to_broadcast([P, m, n])


def softmax_rows(c, s3, n, ready, normalise=True):
    m = s3.shape[1]
    mx, sm = c.tmp(m), c.tmp(m)
    a = c.reduce(mx, s3, ALU.max, ready)
    a = c.tt(s3, s3, each(mx, n), ALU.subtract, a)
    a = c.af(s3, s3, ACT.Exp, a)
    a = c.reduce(sm, s3, ALU.add, a)
    a = c.recip(sm, a)
    if normalise:
        a = c.tt(s3, s3, each(sm, n), ALU.mult, a)
    return a, sm


def l0_attn(c):
    H, DK = 16, 64
    HC = H * DK // P
    ready, xt = c.enter()
    q3 = c.tmp(HC * NT).rearrange("p (k n) -> p k n", k=HC)
    k3 = c.tmp(HC * NT).rearrange("p (k n) -> p k n", k=HC)
    q = c.project(q3, c.wc("wq", DC), DC, c.XT, HC, xt)
    k = c.project(k3, c.wc("wk", DC), DC, c.XT, HC, xt)
    wv = c.wc("wv", DC)
    slots = Ring([Slot((c.tmp(H * NS), c.tmp(H), c.tmp(H), c.tmp(H))) for _ in range(3)])
    vals = Ring([Slot(c.tmp(H * DK)) for _ in range(2)])
    outs = Ring([Slot(c.tmp(HC * P)) for _ in range(2)])
    own_buf = Slot(c.tmp(H * NS))
    of = [None] * TILES

    def weights(t):
        sl = slots.next()
        sc, mx, sm, own = sl.t
        s3 = sc.rearrange("p (h n) -> p h n", h=H)
        a = []
        for odd in range(2):
            b = c.banks.next()
            r = slice(odd * DK, odd * DK + DK)
            for s in range(BT):
                cols = slice(t * P + s * NS, t * P + (s + 1) * NS)
                for i in range(H // 2):
                    m = c.mm(b.t[s * NS:(s + 1) * NS, i * NS:(i + 1) * NS],
                             [(q3[r, i, cols], k3[r, i, cols])], b.free, q, k)
            d = c.stt(s3[:, odd::2], b.t[:, :H // 2 * NS].rearrange("p (h n) -> p h n", n=NS), float(np.sqrt(DK)),
                      rows_of(c.const("causal_neg"), H // 2), ALU.mult, ALU.add, m, sl.free)
            b.free = [d]
            a.append(d)
        a = c.reduce(mx, s3, ALU.max, a)
        a = c.tt(s3, s3, each(mx, NS), ALU.subtract, a)
        a = c.af(s3, s3, ACT.Exp, a)
        a1 = c.reduce(sm, s3, ALU.add, a)
        a1 = c.recip(sm, a1)
        o3 = own_buf.t.rearrange("p (h n) -> p h n", h=H)
        a2 = c.tt(o3, s3, rows_of(c.const("diag32"), H), ALU.mult, a, own_buf.free)
        a2 = c.reduce(own, o3, ALU.add, a2)
        own_buf.free = [a2]
        of[t] = sl, own, c.tt(own, own, sm, ALU.mult, a1, a2)

    def values(t):
        sl, own, a = of[t]
        v = vals.next()
        vd = []
        for half in range(2):
            b = c.banks.next()
            m = c.mm(b.t, [(c.XT[:, i, t * P:(t + 1) * P], wv[:, i, half * HALF:(half + 1) * HALF])
                           for i in range(DC)], b.free, xt)
            n = HALF // DK
            d = c.tt(v.t[:, half * HALF:(half + 1) * HALF].rearrange("p (h d) -> p h d", h=n),
                     b.t.rearrange("p (h d) -> p h d", h=n), each(own[:, half * n:(half + 1) * n], DK),
                     ALU.mult, m, a, v.free)
            b.free = [d]
            vd.append(d)
        sl.free = [d]
        of[t] = v, vd

    def output(t):
        v, vd = of[t]
        o = outs.next()
        od = []
        for half in range(2):
            b = c.banks.next()
            for i in range(4):
                m = c.transpose(b.t[:, i * P:(i + 1) * P], v.t[:, half * HALF + i * P:half * HALF + (i + 1) * P],
                                b.free, vd[half])
            d = c.copy(c.act, o.t[:, half * HALF:(half + 1) * HALF], b.t, m, o.free)
            b.free = [d]
            od.append(d)
        v.free = [m]
        c.add_output(o.t.rearrange("p (k n) -> p k n", k=HC), c.wc("wo", HC), HC, od, tiles=[t], cols=slice(0, P))
        o.free = [c.pe.now()]

    for t in range(TILES + 2):
        if t < TILES:
            weights(t)
        if t >= 2:
            output(t - 2)
        if 1 <= t <= TILES:
            values(t - 1)


def l0_ffn(c):
    E, HC = 8, 8
    EH = E // 2
    w1_ring = Ring([Slot(c.spare(EH * DC * P), c.new_sem(f"hidden_weights{i}")) for i in range(3)])
    xn = c.XN.rearrange("p t d -> p (t d)")
    c.sp.wait(c.ends[-1] if c.ends else None)

    def load(ring, src):
        s = ring.next()
        c.sp.wait(s.free)
        c.sp.silent(lambda q: q.dma_start(s.t, src).then_inc(s.sem, 16))
        s.n += 16
        return s, (s.sem, s.n)

    w1 = lambda i: c.dram["s_eW1"][i // 2 % HC, :, i % 2 * EH * DC * P:(i % 2 + 1) * EH * DC * P]
    first = [load(w1_ring, w1(i)) for i in range(3)]
    asked = 3
    ready, xt = c.enter()
    hid = c.part(HC * NT).rearrange("p (k n) -> p k n", k=HC)
    xs = c.tmp(E * DC * HALF)
    h = xs[:, :DC * NT].rearrange("p (k n) -> p k n", k=DC)
    d = c.project(h, c.wc("gw1", DC), DC, c.XT, DC, xt, bias=c.w("gb1"), func=ACT.Relu)
    mean = c.tmp(DC * NB).rearrange("p (k b) -> p k b", k=DC)
    for k in range(DC):
        a = c.reduce(mean[:, k], h[:, k].rearrange("p (s b) -> p b s", b=NB), ALU.add, d)
    a = c.ts(mean, mean, 1.0 / NS, None, ALU.mult, None, a)
    rep = c.tmp(DC * P).rearrange("p (k s b) -> p k s b", k=DC, s=BT)
    for k in range(DC):
        r = c.copy(c.dve, rep[:, k], rows_of(mean[:, k], BT), a)
    gate_tok, gate_row = c.spare(E), c.tmp(E * NB)
    gate_col = c.spare(HALF, E)
    b = c.banks.next()
    rep2 = rep.rearrange("p k s b -> p k (s b)")
    c.mm(b.t[:, 0:E], [(rep2[:, k], c.wc("gw2", DC)[:, k]) for k in range(DC)], b.free, r)
    c.mm(b.t[0:E, 32:32 + NB], [(c.wc("gw2", DC)[:, k], mean[:, k]) for k in range(DC)])
    gw = c.w("gw2b").rearrange("p (k e m) -> p k e m", k=DC, e=E)
    for e in range(E):
        m3 = c.mm(b.t[:, 64 + e * NB:64 + (e + 1) * NB], [(gw[:, k, e], mean[:, k]) for k in range(DC)])
    g1 = c.tt(gate_tok, b.t[:, 0:E], c.w("gb2w"), ALU.add, m3)
    g2 = c.ts(gate_col.rearrange("p (s b) -> p s b", b=NB),
              b.t[0:E, 32:32 + NB].rearrange("p (o b) -> p o b", o=1).to_broadcast([E, HALF // NB, NB]),
              c.w("gb2"), None, ALU.add, None, m3)
    gr3 = gate_row.rearrange("p (e b) -> p e b", e=E)
    g3 = c.tt(gr3, b.t[:, 64:64 + E * NB].rearrange("p (e b) -> p e b", e=E), each(c.w("gb2w"), NB), ALU.add, m3)
    b.free = [g1, g2, g3]
    xs4 = xs.rearrange("p (e k n) -> p e k n", e=E, k=DC)
    xs_free, hid_done = [], []
    for half in range(2):
        cols = slice(half * HALF, (half + 1) * HALF)
        sd = []
        for e in range(E):
            for k in range(DC):
                sd.append(c.tt(xs4[:, e, k].rearrange("p (s b) -> p s b", b=NB),
                               c.XT[:, k, cols].rearrange("p (s b) -> p s b", b=NB),
                               rows_of(gr3[:, e], HALF // NB), ALU.mult, g3, xt, a, xs_free,
                               q=c.pool if k else c.dve))
        if half == 0 and c.next[0] == "L1_xattn":
            taken = [0]

            def in_xn(n):
                taken[0] += n
                return xn[:, taken[0] - n:taken[0]] if taken[0] <= TILES * D else c.spare(n)

            s4d_kernel(c, c.w_next, in_xn, [c.prefetched, xt])
        for f in range(HC):
            b = c.banks.next()
            for part in range(2):
                s, got = first.pop(0)
                w = s.t.rearrange("p (e k n) -> p e k n", e=EH, k=DC)
                terms = [(w[:, e, k], xs4[:, part * EH + e, k]) for e in range(EH) for k in range(DC)]
                if part:
                    terms.append((c.w("eb1")[:, f * P:(f + 1) * P], gate_col))
                c.pe.wait(b.free, sd, got, g2)
                for n, (l, r) in enumerate(terms):
                    q = c.pe if n == len(terms) - 1 else c.pe.silent
                    m = q(lambda e, l=l, r=r, b=b, start=part == 0 and n == 0, stop=part == 1 and n == len(terms) - 1:
                          e.matmul(b.t, lhsT=l, rhs=r, start=start, stop=stop))
                s.free = [m]
                if asked < 2 * 2 * HC:
                    first.append(load(w1_ring, w1(asked)))
                    asked += 1
            u = hid[:, f, cols]
            d = c.af(u.high, b.t, ACT.Relu, m)
            d = c.stt(u.low, b.t, 0.0, u.high.bitcast(F32), ALU.max, ALU.subtract, d)
            b.free = [d]
            hid_done.append(d)
        xs_free = [m]
    c.scratch_to_parts()
    PC = 2 * D
    raws = Ring([Slot(xn[:, i * PC:(i + 1) * PC], c.new_sem(f"output_weights{i}")) for i in range(4)])
    pieces = Ring([Slot(c.part(PC)) for _ in range(8)])
    w2 = lambda i: c.dram["s_eW2"][i // HC, :, i % HC * PC:(i % HC + 1) * PC]
    PIECES = E // 2 * HC
    coming = [load(raws, w2(i)) for i in range(4)]
    split = []

    def split_piece():
        s, got = coming.pop(0)
        p = pieces.next()
        d = c.split(s.t, p.t, got, p.free, q=c.pool)
        s.free = [d]
        split.append((p, d))
        if len(split) + 3 < PIECES:
            coming.append(load(raws, w2(len(split) + 3)))

    for _ in range(4):
        split_piece()
    x_done = [[] for _ in range(TILES)]
    for t in range(TILES):
        b = c.banks.next()
        m = c.mm(b.t[:, :D], [(gate_col[:, :P], c.w("eb2"))], b.free, g2)
        x_done[t] = b.free = [c.tt(c.X[:, t], b.t[:, :D], c.X[:, t], ALU.add, m, ready)]
    every = [c.banks.next() for _ in range(TILES)]
    for p_ in range(E // 2):
        for k in range(HC):
            s, ok = split[p_ * HC + k]
            for t, b in enumerate(every):
                c.pe.wait(ok, b.free if k == 0 else None, hid_done)
                u = hid[:, k, t * P:(t + 1) * P]
                for n, (l, r) in enumerate(((u.high, s.t.high), (u.low, s.t.high), (u.high, s.t.low))):
                    f = lambda e, l=l, r=r, b=b, start=k == 0 and n == 0, stop=k == HC - 1 and n == 2: \
                        e.matmul(b.t, lhsT=l, rhs=r, start=start, stop=stop)
                    m = c.pe(f) if n == 2 else c.pe.silent(f)
                if k == HC - 1:
                    for i in range(2):
                        e = 2 * p_ + i
                        x_done[t] = c.stt(c.X[:, t], b.t[:, i * D:(i + 1) * D], gate_tok[:, e:e + 1], c.X[:, t],
                                          ALU.mult, ALU.add, m, g1, x_done[t])
                    b.free = [x_done[t]]
            s.free = [m]
            if len(split) < PIECES:
                split_piece()


def l1_attn(c):
    H, DH, EPS = 16, 16, 1e-5
    NH = TILES * H
    ready, xt = c.enter()

    def softplus(x):
        y, z = c.tmp(1), c.tmp(1)
        a = c.ts(y, x, -1.0, None, ALU.mult, None, c.w_ready)
        a = c.tt(y, y, x, ALU.min, a)
        a = c.af(y, y, ACT.Exp, a)
        a = c.af(y, y, ACT.Ln, a, bias=1.0)
        a2 = c.ts(z, x, 0.0, None, ALU.max, None, c.w_ready)
        return z, c.tt(z, z, y, ALU.add, a, a2)

    cc, a0 = softplus(c.w("logc"))
    bp, a1 = softplus(c.w("beta"))
    rc, irc, edge, negc, twoc, slope, negab = (c.tmp(1) for _ in range(7))
    a = c.af(rc, cc, ACT.Sqrt, a0)
    a = c.recip(rc, a, out=irc)
    consts = [c.ts(edge, irc, EPS, None, ALU.subtract, None, a),
              c.ts(negc, cc, -1.0, None, ALU.mult, None, a0),
              c.ts(twoc, cc, 2.0, None, ALU.mult, None, a0),
              c.ts(slope, bp, irc, -1.0, ALU.mult, ALU.mult, a, a1),
              c.ts(negab, c.w("ab"), -1.0, None, ALU.mult, None, c.w_ready)]

    tok = lambda a: a.rearrange("p (t d) -> p t d", t=TILES)
    heads = lambda a: a.rearrange("p t (h d) -> p (t h) d", h=H)
    qkv, done = [], []
    for n in ("wq", "wk", "wv"):
        dst = tok(c.tmp(TILES * D))
        dd = []
        for t in range(0, TILES, 2):
            b = c.banks.next()
            for j in range(2):
                m = c.mm(b.t[:, j * D:(j + 1) * D],
                         [(c.XT[:, k, (t + j) * P:(t + j + 1) * P], c.wc(n, DC)[:, k]) for k in range(DC)],
                         b.free, xt)
            d = c.copy(c.act if t % 4 else c.dve, dst[:, t:t + 2], b.t, m)
            b.free = [d]
            dd.append(d)
        qkv.append(dst)
        done.append(dd)
    sq = tok(c.tmp(TILES * D))

    def norm2(v, ready):
        n2 = c.tmp(NH)
        a = c.tt(sq, v, v, ALU.mult, ready, c.dve.now())
        return n2, c.reduce(n2, heads(sq), ALU.add, a)

    def exp_factor(n2, ready):
        vn, f = c.tmp(NH), c.tmp(NH)
        a = c.af(vn, n2, ACT.Sqrt, ready)
        a = c.ts(vn, vn, EPS, rc, ALU.max, ALU.mult, a, consts)
        a = c.af(f, vn, ACT.Tanh, a)
        a = c.recip(vn, a)
        return f, c.tt(f, f, vn, ALU.mult, a)

    def log_factor(n2, ready):
        y, z, g = c.tmp(NH), c.tmp(NH), c.tmp(NH)
        a = c.af(y, n2, ACT.Sqrt, ready)
        a = c.ts(y, y, EPS, None, ALU.max, None, a)
        b = c.ts(z, y, edge, rc, ALU.min, ALU.mult, a, consts)
        a = c.ts(y, y, rc, 2.0, ALU.mult, ALU.mult, b)
        a = c.recip(y, a)
        b = c.ts(g, z, -1.0, 1.0, ALU.mult, ALU.add, b)
        b = c.recip(g, b)
        b = c.stt(g, z, 1.0, g, ALU.add, ALU.mult, b)
        b = c.af(g, g, ACT.Ln, b)
        return g, c.tt(g, g, y, ALU.mult, a, b)

    def times(v, f, ready):
        return c.tt(heads(v), heads(v), each(f, DH), ALU.mult, ready)

    def to_ball_and_back(v, ready):
        n2, a = norm2(v, ready)
        f, b = exp_factor(n2, a)
        a = times(v, f, b)
        n2, a = norm2(v, a)
        f, b = log_factor(n2, a)
        return times(v, f, b)

    q, k, v = qkv
    sides = []
    for x, d in ((q, done[0]), (k, done[1])):
        n2, a = norm2(x, d)
        f, a = exp_factor(n2, a)
        a = times(x, f, a)
        n2, b = norm2(x, a)
        sides.append((n2, b, a))
    vdone = to_ball_and_back(v, done[2])
    (xns, xns_ok, q_ok), (_, kb, k_ok) = sides
    onemc = c.tmp(NH)
    om = c.ts(onemc, xns, negc, 1.0, ALU.mult, ALU.add, xns_ok, consts)
    qT = c.XT
    kT = c.XN.rearrange("p t d -> p (t d)").rearrange("p (k n) -> p k n", k=DC)
    qd = c.to_features(q, qT, [[q_ok, m]] * TILES)
    kd = c.to_features(k, kT, [[k_ok, xt]] * TILES)
    work = q.rearrange("p t d -> p (t d)"), k.rearrange("p t d -> p (t d)")
    kbds = Ring([Slot(w.rearrange("p (k h n) -> p k h n", k=DC, h=8)) for w in (work[0], c.tmp(TILES * D))])
    kbds.slots[0].free = [qd]
    k2s = Ring([Slot(w.rearrange("p (k h n) -> p k h n", k=DC, h=8)) for w in (work[1], c.tmp(TILES * D))])
    k2s.slots[0].free = [kd]
    dist = c.tmp(TILES * H * NS).rearrange("p (t n) -> p t n", t=TILES)
    ynss = Ring([Slot(c.tmp(H * NS)) for _ in range(2)])
    dd = []

    def spread_keys(t):
        kbd, k2, e1 = kbds.next(), k2s.next(), [None] * DC
        for i in range(DC):
            e1[i] = c.tt(kbd.t[:, i], rows_of(kT[:, i, t * P:(t + 1) * P], 8), each(c.const("head16"), P),
                      ALU.mult, kd, kbd.free, q=c.pool if i else c.dve)
        return kbd, k2, e1, c.af(k2.t, kbd.t, ACT.Square, e1, k2.free)

    def distances(t, kbd, k2, e1, e2):
        yns = ynss.next()
        bxy, by = c.banks.next(), c.banks.next()
        for s in range(BT):
            r = slice(s * NS, (s + 1) * NS)
            for i in range(DC):
                m1 = c.mm(bxy.t[r, i * D:(i + 1) * D],
                          [(qT[:, i, t * P + s * NS:t * P + (s + 1) * NS], kbd.t[:, i, :, r])], bxy.free, qd, e1)
                m2 = c.mm(by.t[r, i * D:(i + 1) * D], [(c.const("ones")[:, :NS], k2.t[:, i, :, r])], by.free, e2)
        kbd.free, k2.free = [m1, e2], [m2]
        hs = slice(t * H, (t + 1) * H)
        y3 = yns.t.rearrange("p (h n) -> p h n", h=H)
        d3 = dist[:, t].rearrange("p (h n) -> p h n", h=H)
        a = c.copy(c.act, yns.t, by.t, m2, yns.free)
        by.free = [a]
        b = c.stt(dist[:, t], bxy.t, -2.0, yns.t, ALU.mult, ALU.add, m1, a)
        bxy.free = [b]
        b = c.tt(d3, d3, each(xns[:, hs], NS), ALU.add, b)
        a = c.ts(yns.t, yns.t, negc, 1.0, ALU.mult, ALU.add, b)
        a = c.tt(y3, y3, each(onemc[:, hs], NS), ALU.mult, a, om)
        a = c.ts(yns.t, yns.t, EPS, None, ALU.max, None, a)
        a = c.recip(yns.t, a)
        b = c.tt(dist[:, t], dist[:, t], yns.t, ALU.mult, a)
        yns.free = [b]
        return b

    nxt = spread_keys(0)
    for t in range(TILES):
        now, nxt = nxt, spread_keys(t + 1) if t + 1 < TILES else None
        dd.append(distances(t, *now))
    u = dist.rearrange("p t n -> p (t n)")
    r2 = c.tmp(TILES * H * NS)
    a = c.ts(u, u, twoc, EPS, ALU.mult, ALU.max, dd)
    a = c.stt(r2, u, 2.0, u, ALU.add, ALU.mult, a)
    a = c.af(r2, r2, ACT.Sqrt, a)
    a = c.tt(u, u, r2, ALU.add, a)
    a = c.af(u, u, ACT.Ln, a, bias=1.0)
    a = c.ts(u, u, slope, negab, ALU.mult, ALU.add, a)
    u3 = u.rearrange("p (m n) -> p m n", n=NS)
    a, _ = softmax_rows(c, u3, NS, a)
    wt = r2
    bds = Ring([Slot(s.t.rearrange("p k h n -> p (k h n)").rearrange("p (h m) -> p h m", h=H)) for s in kbds.slots])
    for old, s in zip(kbds.slots, bds.slots):
        s.free = [c.pool(lambda e, s=s: e.memset(s.t, 0.0), old.free)]
    out = sq
    od = []

    def lay_out(t):
        w = wt[:, t * H * NS:(t + 1) * H * NS]
        x = c.dve(lambda e: e.transpose(w, dist[:, t]), a)
        w3 = w.rearrange("p (h m) -> p h m", h=H)
        bd = bds.next()
        return bd, [c.copy((c.dve, c.act, c.dve, c.pool)[s], bd.t[r, :, r], w3[r], x, bd.free,
                           c.pool.now() if s == 3 else None)
                    for s, r in ((s, slice(s * NS, (s + 1) * NS)) for s in range(BT))]

    nxt = lay_out(0)
    for t in range(TILES):
        (bd, x2), nxt = nxt, lay_out(t + 1) if t + 1 < TILES else None
        b = c.banks.next()
        for h in range(H):
            m = c.mm(b.t[:, h * DH:(h + 1) * DH], [(bd.t[:, h], v[:, t, h * DH:(h + 1) * DH])], b.free, x2, vdone)
        bd.free = [m]
        d = c.copy(c.act, out[:, t], b.t[:, :D], m)
        b.free = [d]
        od.append(d)
    sq = tok(r2[:, :TILES * D])
    a = to_ball_and_back(out, [od, c.dve.now(), m])
    oT = c.XT
    f = c.to_features(out, oT, [a] * TILES)
    c.add_output(oT, c.wc("wo", DC), DC, f)


def l3_attn(c):
    H, DH, C = 16, 16, 64
    HP = H // 2
    ready, xt = c.enter()
    big = lambda: c.tmp(DC * NT).rearrange("p (k n) -> p k n", k=DC)
    xs = c.XN.rearrange("p t d -> p (t d)").rearrange("p (k n) -> p k n", k=DC)
    perm = [c.copy(q, xs[:, k].rearrange("p (b s) -> p b s", b=NB), c.XT[:, k].rearrange("p (s b) -> p b s", b=NB), xt)
            for k, q in ((0, c.dve), (1, c.pool))]
    q3, k3 = big(), big()
    kd = c.project(k3, c.wc("wk", DC), DC, xs, DC, perm, bias=c.w("bk"))
    qd = c.project(q3, c.wc("wq", DC), DC, xs, DC, perm, bias=c.w("bq"))
    temp = c.tmp(DC)
    a = c.af(temp, c.w("beta"), ACT.Exp, c.w_ready, scale=-1.0)
    qd = [c.ts(q3[:, k], q3[:, k], temp[:, k:k + 1], 1.0 / np.sqrt(DH), ALU.mult, ALU.mult, a, qd) for k in range(DC)]
    v3 = c.tmp(TILES * D).rearrange("p (t d) -> p t d", t=TILES)
    vd = []
    for t in range(TILES):
        b = c.banks.next()
        m = c.mm(b.t[:, :D], [(xs[:, k, t * P:(t + 1) * P], c.wc("wv", DC)[:, k]) for k in range(DC)]
                 + [(c.const("ones")[0:1, :P], c.w("bv"))], b.free, perm)
        d = c.copy(c.act, v3[:, t], b.t[:, :D], m)
        b.free = [d]
        vd.append(d)
    cw = c.tmp(HP * NT).rearrange("p (g n) -> p g n", g=HP)
    mx = Ring([Slot(c.tmp(NB // 2)) for _ in range(4)])
    qc = c.w("qc").rearrange("p (k g m) -> p k g m", k=DC, g=HP // DC)
    cd = [[], []]
    for half in range(2):
        for g in range(HP):
            cols = slice(half * HALF, (half + 1) * HALF)
            b = c.banks.next()
            k = g * DC // HP
            m = c.mm(b.t, [(qc[:, k, g % (HP // DC)], k3[:, k, cols])], b.free, kd)
            x = mx.next()
            b3 = b.t.rearrange("p (b s) -> p b s", s=NS)
            a = c.reduce(x.t, b3, ALU.max, m, x.free)
            a = c.tt(cw[:, g, cols].rearrange("p (b s) -> p b s", s=NS), b3, each(x.t, NS), ALU.subtract, a)
            b.free = x.free = [a]
            cd[half].append(c.af(cw[:, g, cols], cw[:, g, cols], ACT.Exp, a))
    HU = H // DC
    ring = lambda n, cols: Ring([Slot(c.tmp(cols)) for _ in range(n)])
    cwTs, rns, scs, wTs = ring(2, HU * C), ring(2, HU * C), ring(3, HU * C), ring(1, HU * C)
    qbds, ams, bms = ring(1, HU * P), ring(2, HU * P), ring(1, HU * P)
    o_ = Slot(c.tmp(D))
    maxima, totals = ring(2, HU), ring(3, HU)
    oT = c.XT
    outd = []
    UNITS = TILES * DC
    of = [{} for _ in range(UNITS)]

    def turn_keys(u):
        t, k = divmod(u, DC)
        cols = slice(t * P, (t + 1) * P)
        of[u]["cwT"] = cwT = cwTs.next()
        b = c.banks.next()
        for g in range(4):
            m = c.transpose(b.t[:, g * P:(g + 1) * P], cw[:, 4 * k + g, cols], b.free, cd[t // 4])
        of[u]["cwT_ok"] = d = c.copy(c.act, cwT.t, b.t, m, cwT.free)
        b.free = [d]
        of[u]["qbd"] = qbd = qbds.next()
        of[u]["qbd_ok"] = c.tt(qbd.t.rearrange("p (h n) -> p h n", h=HU), rows_of(q3[:, k, cols], HU),
                               each(c.const("head16"), P), ALU.mult, qd, qbd.free, q=c.pool)

    def norms(u):
        t, k = divmod(u, DC)
        cols = slice(t * P, (t + 1) * P)
        of[u]["rn"], of[u]["am"] = rn, am = rns.next(), ams.next()
        b = c.banks.next()
        m = c.mm(b.t, [(c.const("causal"), of[u]["cwT"].t)], b.free, of[u]["cwT_ok"])
        of[u]["rn_ok"] = d = c.recip(b.t, m, rn.free, out=rn.t)
        b.free = [d]
        ad = []
        for g in range(2):
            b = c.banks.next()
            m = c.mm(b.t, [(k3[:, k, cols], of[u]["qbd"].t[:, g * HALF:(g + 1) * HALF])], b.free, kd, of[u]["qbd_ok"])
            d = c.tt(am.t[:, g * HALF:(g + 1) * HALF].rearrange("p (h n) -> p h n", h=4),
                     b.t.rearrange("p (h n) -> p h n", h=4), rows_of(c.const("causal"), 4), ALU.mult, m, am.free)
            b.free = [d]
            ad.append(d)
        of[u]["qbd"].free = [m]
        of[u]["am_ok"] = ad

    def scores(u):
        cwT, rn, am = of[u]["cwT"], of[u]["rn"], of[u]["am"]
        of[u]["s"], mx = scs.next(), maxima.next()
        s_ = of[u]["s"]
        b = c.banks.next()
        for h in range(HU):
            m = c.mm(b.t[:, h * C:(h + 1) * C], [(am.t[:, h * P:(h + 1) * P], cwT.t[:, h * C:(h + 1) * C])], b.free,
                     of[u]["am_ok"])
        cwT.free = am.free = [m]
        a = c.tt(s_.t, b.t, rn.t, ALU.mult, m, of[u]["rn_ok"], s_.free)
        b.free = [a]
        s3 = s_.t.rearrange("p (h n) -> p h n", h=HU)
        a = c.reduce(mx.t, s3, ALU.max, a, mx.free)
        a = c.tt(s3, s3, each(mx.t, C), ALU.subtract, a)
        mx.free = [a]
        of[u]["exp"] = c.af(s3, s3, ACT.Exp, a)

    def weights(u):
        s_, rn, sm = of[u]["s"], of[u]["rn"], totals.next()
        s3 = s_.t.rearrange("p (h n) -> p h n", h=HU)
        a1 = c.reduce(sm.t, s3, ALU.add, of[u]["exp"], sm.free)
        a1 = c.recip(sm.t, a1)
        a2 = c.tt(s_.t, s_.t, rn.t, ALU.mult, of[u]["exp"], a1)
        rn.free = [a2]
        of[u]["w_ok"] = c.tt(s3, s3, each(sm.t, C), ALU.mult, a1, a2)
        sm.free = [of[u]["w_ok"]]

    def turn_weights(u):
        s_ = of[u]["s"]
        of[u]["wT"] = wT = wTs.next()
        b = c.banks.next()
        for g in range(4):
            m = c.transpose(b.t[:, g * P:(g + 1) * P], s_.t[:, g * P:(g + 1) * P], b.free, of[u]["w_ok"])
        of[u]["wT_ok"] = d = c.copy(c.act, wT.t, b.t, m, wT.free)
        b.free = s_.free = [d]

    def pairs(u):
        t, k = divmod(u, DC)
        cols = slice(t * P, (t + 1) * P)
        of[u]["bm"] = bm = bms.next()
        b3 = bm.t.rearrange("p (h n) -> p h n", h=HU)
        bd = []
        for odd in range(2):
            b = c.banks.next()
            r = slice(odd * C, odd * C + C)
            for g in range(4):
                m = c.mm(b.t[:, g * P:(g + 1) * P], [(cw[r, 4 * k + g, cols], of[u]["wT"].t[r, g * P:(g + 1) * P])],
                         b.free, of[u]["wT_ok"])
            d = c.tt(b3[:, odd::2], b.t.rearrange("p (h n) -> p h n", h=4), rows_of(c.const("causal"), 4),
                     ALU.mult, m, bm.free)
            b.free = [d]
            bd.append(d)
        of[u]["wT"].free = [m]
        of[u]["bm_ok"] = bd

    def outputs(u):
        t, k = divmod(u, DC)
        bm = of[u]["bm"]
        b = c.banks.next()
        for h in range(HU):
            f = k * P + h * DH
            m = c.mm(b.t[:, h * DH:(h + 1) * DH], [(bm.t[:, h * P:(h + 1) * P], v3[:, t, f:f + DH])], b.free,
                     of[u]["bm_ok"], vd)
        bm.free = [m]
        of[u]["o_ok"] = d = c.copy(c.act, o_.t[:, k * P:(k + 1) * P], b.t[:, :P], m, o_.free)
        b.free = [d]

    def turn_outputs(t):
        b = c.banks.next()
        for k in range(DC):
            m = c.transpose(b.t[:, k * P:(k + 1) * P], o_.t[:, k * P:(k + 1) * P], b.free, of[DC * t + k]["o_ok"])
        o_.free = [m]
        for k in range(DC):
            d = c.copy(c.dve, oT[:, k].rearrange("p (s b) -> p b s", b=NB)[:, t * BT:(t + 1) * BT],
                       b.t[:, k * P:(k + 1) * P].rearrange("p (b s) -> p b s", b=BT), m, perm)
            outd.append(d)
        b.free = [d]

    for i in range(UNITS + 3):
        if 1 <= i <= UNITS:
            weights(i - 1)
        if i >= 3 and (i - 3) % DC == DC - 1:
            turn_outputs((i - 3) // DC)
        if i < UNITS:
            turn_keys(i)
        if 2 <= i < UNITS + 2:
            turn_weights(i - 2)
        if i < UNITS:
            norms(i)
        if 2 <= i < UNITS + 2:
            pairs(i - 2)
        if i < UNITS:
            scores(i)
        if 2 <= i < UNITS + 2:
            outputs(i - 2)
    c.add_output(oT, c.wc("wo", DC), DC, [outd, ready], c.w("bo"))



class Context:

    def __init__(self, c, slots):
        self.c = c
        self.cols = CK + 3 * (DV + 1)
        self.ring = Ring([Slot(c.tmp(self.cols), c.new_sem(f"{c.name}_context{i}")) for i in range(slots)])
        c.sp.wait(c.ends[-1] if c.ends else None)
        self.queue, self.asked = [], 0
        for _ in range(slots):
            self.ask()

    def ask(self):
        if self.asked < NB:
            s, b = self.ring.next(), self.asked
            self.c.sp.wait(s.free)
            self.c.sp.silent(lambda q: q.dma_start(s.t, self.c.dram["ctx"][b]).then_inc(s.sem, 16))
            s.n += 16
            self.queue.append((s, (s.sem, s.n)))
            self.asked += 1

    def next(self):
        return self.queue.pop(0)


def head_queries(c, wk, heads, aug, src, q_tile, scale, ready, slot):
    qa, qb = slot.t
    done = []
    for part, rows, c0 in ((qa, P, 0), (qb, aug - P, P)):
        for g in range(0, heads, 4):
            b = c.banks.next()
            for j in range(4):
                m = c.mm(b.t[:rows, j * P:(j + 1) * P], [(wk(g + j)[:, c0:c0 + rows], src(g + j)[:, q_tile])],
                         b.free, ready, slot.free)
            to = part[:rows, :, g:g + 4, :].rearrange("p s h q -> p h s q")
            got = b.t[:rows].rearrange("p (h s q) -> p h s q", h=4, s=BT)
            if isinstance(to, Pair):
                done.append(c.split(got, to, m, slot.free))
            else:
                done.append(c.copy(c.act if c0 else c.dve, to, got, m, slot.free))
            b.free = done[-1:]
    return done


def exp_keys(c, bank, n, p_slot, stat, m):
    nmax, total = stat.t
    a = c.dve(lambda e: e.tensor_reduce(nmax, bank.t[:, :n], AX.X, ALU.max, negate=True), m, stat.free)
    a = c.af(p_slot.t[:, :n], bank.t[:, :n], ACT.Exp, a, p_slot.free, bias=nmax, accum=total)
    bank.free = [a]
    return a


def divide_keys(c, n, p_slot, stat, ready, q=None):
    _, total = stat.t
    a = c.recip(total, ready)
    a = c.ts(p_slot.t[:, :n], p_slot.t[:, :n], total, None, ALU.mult, None, a, q=q or c.pool)
    stat.free = [a]
    return a


def raw_attention(c, heads, aug_k, aug_v, queries, finish):
    R = heads // 4
    ctx = Context(c, 2)
    qslot = Slot(tuple(c.part(BT * heads * NS).rearrange("p (s h q) -> p s h q", s=BT, h=heads) for _ in range(2)))
    keys = Slot(c.part(CK))
    values = Ring([Slot(c.part(ctx.cols - CK)) for _ in range(2)])
    probs = Ring([Slot(c.spare(G) if i < 3 else c.tmp(G)) for i in range(2 * R)])
    stats = Ring([Slot((c.tmp(1), c.tmp(1))) for _ in range(2 * R)])
    pts = Ring([Slot([c.part(R * P) for _ in range(3)]) for _ in range(2)])
    pc = Slot(tuple(
        c.tmp(heads * P).rearrange("p (h n) -> p h n", h=heads) for _ in range(2)))
    of = [{} for _ in range(NB)]
    turned, sums = {}, {}

    def turn(t):
        turned[t] = queries(t, qslot)

    def split_keys(s):
        of[s]["cx"], of[s]["got"] = cx, got = ctx.next()
        of[s]["k_ok"] = c.split(cx.t[:, :CK], keys.t, got, keys.free)

    def split_values(s):
        of[s]["v"], cx = values.next(), of[s]["cx"]
        of[s]["v_ok"] = c.split(cx.t[:, CK:], of[s]["v"].t, of[s]["got"], of[s]["v"].free)
        cx.free = [of[s]["k_ok"], of[s]["v_ok"]]
        ctx.ask()

    def scores(s):
        t, i = divmod(s, BT)
        out = []
        for r in range(R):
            b, p, st = c.banks.next(), probs.next(), stats.next()
            m = c.mm_split(b.t[:, :GE], [
                (q[:rows, i, 4 * r:4 * r + 4].rearrange("p h q -> p (h q)"), keys.t[:rows, c0:c0 + GE])
                for q, rows, c0 in zip(qslot.t, (P, aug_k - P), (CT0, CT1))], b.free, turned[t], of[s]["k_ok"])
            out.append((p, st, exp_keys(c, b, G, p, st, m)))
        qslot.free = keys.free = [m]
        of[s]["p"] = [(p, divide_keys(c, G, p, st, a)) for p, st, a in out]

    def weights_to_keys(s):
        of[s]["pt"] = pt = pts.next()
        done = []
        for k, (k0, n) in enumerate(((0, P), (P, P), (2 * P, 1))):
            b = c.banks.next()
            for r, (p, ready) in enumerate(of[s]["p"]):
                m = c.transpose(b.t[:n, r * P:(r + 1) * P], p.t[:, k0:k0 + n], b.free, ready)
            d = c.split(b.t[:n, :R * P], pt.t[k][:n], m, pt.free)
            b.free = [d]
            done.append(d)
        for p, _ in of[s]["p"]:
            p.free = [m]
        of[s]["pt_ok"] = done

    def products(s):
        t, i = divmod(s, BT)
        pt, v = of[s]["pt"], of[s]["v"]
        for part, rows, f0 in ((pc.t[0], P, 0), (pc.t[1], aug_v - P, P)):
            b = c.banks.next()
            terms = [(v.t[:n, k * (DV + 1) + f0:k * (DV + 1) + f0 + rows], pt.t[k][:n])
                     for k, n in enumerate((P, P, 1))]
            m = c.mm_split(b.t[:rows, :R * P], terms, b.free, of[s]["pt_ok"], of[s]["v_ok"])
            d = c.copy(c.dve if f0 else c.act, part[:rows, :, i * NS:(i + 1) * NS],
                       b.t[:rows, :R * P].rearrange("p (h q) -> p h q", h=heads), m, pc.free)
            b.free = [d]
            sums.setdefault(t, []).append(d)
        pt.free = v.free = [m]

    turn(0)
    split_keys(0)
    for s in range(NB + 3):
        if s < NB:
            scores(s)
        if s % BT == BT - 1 and s // BT + 1 < TILES:
            turn(s // BT + 1)
        if s + 1 < NB:
            split_keys(s + 1)
        if 1 <= s <= NB:
            weights_to_keys(s - 1)
        if s >= 3 and (s - 3) % BT == BT - 1:
            t = (s - 3) // BT
            finish(t, pc.t[0], pc.t[1], sums[t])
            pc.free = [c.pe.now()]
        if 2 <= s < NB + 2:
            products(s - 2)
        if s < NB:
            split_values(s)


def l2_xattn(c):
    H, DK = 16, 64
    ready, xt = c.enter()
    HC = H * DK // P
    qt, ot = (Slot(a.rearrange("p (k n) -> p k n", k=HC)) for a in c.halves_of_xn())
    wk = c.w("wk").rearrange("p (k f) -> p k f", k=HC)

    def queries(t, slot):
        d = []
        for g in range(0, HC, 4):
            b = c.banks.next()
            for j in range(4):
                m = c.mm(b.t[:, j * P:(j + 1) * P],
                         [(c.wc("wq", DC)[:, k, (g + j) * P:(g + j + 1) * P], c.XT[:, k, t * P:(t + 1) * P])
                          for k in range(DC)], b.free, xt)
            d.append(c.dve(lambda e, b=b, g=g: e.tensor_scalar(qt.t[:, g:g + 4].rearrange("p k n -> p (k n)"), b.t,
                                                              DK ** -0.5, None, ALU.mult), m, qt.free))
            b.free = [d[-1]]
        qa, qb = slot.t
        done = []
        for odd in range(2):
            r = slice(odd * DK, odd * DK + DK)
            for part, rows, c0 in ((qa, P, 0), (qb, V1, P)):
                for g in range(0, HC, 4):
                    b = c.banks.next()
                    for j in range(4):
                        m = c.mm(b.t[:rows, j * P:(j + 1) * P], [(wk[r, g + j, c0:c0 + rows], qt.t[r, g + j])],
                                 b.free, d)
                    done.append(c.split(b.t[:rows].rearrange("p (h s q) -> p h s q", h=4, s=BT),
                                        part[:rows, :, 2 * g + odd:2 * g + odd + 7:2, :].rearrange("p s h q -> p h s q"),
                                        m, slot.free))
                    b.free = done[-1:]
        qt.free = [m]
        return done

    def finish(t, pa, pb, pr):
        d = []
        for g in range(0, HC, 4):
            b = c.banks.next()
            for j in range(4):
                for odd in range(2):
                    h = 2 * (g + j) + odd
                    hc = slice(h * DK, (h + 1) * DK)
                    m = c.mm(b.t[odd * DK:(odd + 1) * DK, j * P:(j + 1) * P],
                             [(c.w("wv0")[:, hc], pa[:, h]), (c.w("wv1")[:, hc], pb[:V1, h])], b.free, pr)
            d.append(c.copy(c.act, ot.t[:, g:g + 4].rearrange("p k n -> p (k n)"), b.t, m, ot.free))
            b.free = [d[-1]]
        c.add_output(ot.t, c.wc("wo", HC), HC, [d, ready], c.w("bo"), tiles=[t], cols=slice(0, P))
        ot.free = [c.pe.now()]

    raw_attention(c, H, DV, DV, queries, finish)


def l3_xattn(c):
    H, DK = 16, 16
    ready, xt = c.enter()
    q3 = c.XN.rearrange("p t d -> p (t d)").rearrange("p (k n) -> p k n", k=DC)
    ot = Slot(c.spare(DC * P).rearrange("p (k n) -> p k n", k=DC))
    qd = c.project(q3, c.wc("wq", DC), DC, c.XT, DC, xt, bias=c.w("bq"))
    qd = [c.ts(q3[:, k], q3[:, k], DK ** -0.5, None, ALU.mult, None, qd) for k in range(DC)]
    wk = c.w("wk").rearrange("p (h f) -> p h f", h=H)
    wv = [c.w(n).rearrange("p (h f) -> p h f", h=H) for n in ("wv0", "wv1")]

    def queries(t, slot):
        return head_queries(c, lambda h: wk[:, h], H, DV + 1, lambda h: q3[:, h // 8], slice(t * P, (t + 1) * P),
                            None, qd, slot)

    def finish(t, pa, pb, pr):
        b = c.banks.next()
        for k in range(DC):
            m = c.mm(b.t[:, k * P:(k + 1) * P],
                     [x for h in range(8 * k, 8 * k + 8)
                      for x in ((wv[0][:, h], pa[:, h]), (wv[1][:, h], pb[:V1 + 1, h]))], b.free, pr)
        d = c.copy(c.act, ot.t.rearrange("p k n -> p (k n)"), b.t[:, :DC * P], m, ot.free)
        b.free = [d]
        c.add_output(ot.t, c.wc("wo", DC), DC, [d, ready], c.w("bo"), tiles=[t], cols=slice(0, P))
        ot.free = [c.pe.now()]

    raw_attention(c, H, DV + 1, DV + 1, queries, finish)


def mask_rows(c, src, cols, first, last, name):
    sem = c.new_sem(name)
    packed = c.tmp(-(-G // 4), NB).bitcast(U32)
    raw = packed.bitcast(U8)[:, :G]
    out = c.tmp(cols, NB)
    c.sp.wait(c.ends[-1] if c.ends else None)
    c.sp.silent(lambda q: q.dma_start(packed, c.dram[src]).then_inc(sem, 16))
    z = c.dve(lambda e: e.memset(out, 0.0))
    a = c.copy(c.dve, out[:, first:first + G - 1], raw[:, :G - 1], z, (sem, 16))
    a = c.copy(c.dve, out[:, last:last + 1], raw[:, G - 1:G], a)
    for x in (out[:, first:first + G - 1], out[:, last:last + 1]):
        a = c.ts(x, x, -NEG, NEG, ALU.mult, ALU.add, a)
    return out, a


def pick(c, b):
    return c.const("eye")[:NB, b:b + 1].to_broadcast([NB, P])


def l0_xattn(c):
    H, DK, RMS_EPS = 4, 64, 1e-8
    KEYS = G + NS
    L3 = NS + 1
    ctx = Context(c, 3)
    mask, mask_ok = mask_rows(c, "keep0", KEYS, 0, KEYS - 1, "keep0_loaded")
    ready = c.normalise(c.X, c.XN)
    tmp = c.tmp(TILES * D).rearrange("p (t d) -> p t d", t=TILES)
    n2 = c.normalise(c.XN, tmp, ready)
    lt = c.to_features(tmp, c.XT, n2, c.w("gl"), c.w("bl"))
    lnT = c.XT
    gq = c.tmp(DK)
    g = c.stt(gq, c.w("qn"), DK ** -0.5, c.w("kn"), ALU.mult, ALU.mult)
    q = tmp
    qd = []
    for t in range(0, TILES, 2):
        b = c.banks.next()
        for j in range(2):
            m = c.mm(b.t[:, j * D:(j + 1) * D],
                     [(lnT[:, k, (t + j) * P:(t + j + 1) * P], c.wc("wq", DC)[:, k]) for k in range(DC)], b.free, lt)
        d = c.copy(c.act if t % 4 else c.dve, q[:, t:t + 2], b.t, m)
        b.free = [d]
        qd.append(d)
    NH = TILES * H
    heads = lambda a: a.rearrange("p t (h d) -> p (t h) d", h=H)
    nrm = c.tmp(NH)
    qbd = c.tmp(DC * NB * P)

    def rms(n2, ready):
        a = c.ts(n2, n2, 1.0 / DK, RMS_EPS ** 2, ALU.mult, ALU.max, ready)
        return c.power(n2, "mhalf", a)

    a = c.tt(c.XN, q, q, ALU.mult, qd)
    a = c.reduce(nrm, heads(c.XN), ALU.add, a)
    a = rms(nrm, a)
    a = c.tt(heads(q), heads(q), each(nrm, DK), ALU.mult, a)
    a = c.tt(heads(q), heads(q), rows_of(gq, NH), ALU.mult, a, g)
    qT = c.XN.rearrange("p t d -> p (t d)").rearrange("p (k n) -> p k n", k=DC)
    qd = c.to_features(q, qT, [a] * TILES)
    z = c.pool(lambda e: e.memset(qbd, 0.0))
    q5 = qbd.rearrange("p (k b h q) -> p k b h q", k=DC, b=NB, h=H)
    bd = []
    for k in range(DC):
        for odd in range(2):
            r = slice(odd * DK, odd * DK + DK)
            bd.append(c.copy(c.dve if odd else c.act, q5[r, k, :, 2 * k + odd],
                             qT[r, k].rearrange("p (b q) -> p b q", b=NB), qd, z))
    sem = c.new_sem("last_rows_loaded")
    last = c.tmp(DV, NB)
    lT = [c.tmp(NB), c.tmp(NB, V1)]
    st = c.tmp(12)
    c.sp.silent(lambda e: e.dma_start(last, c.dram["ctx_last"]).then_inc(sem, 16))
    a = c.dve(lambda e: e.bn_stats(st[:NB, 0:6], last), (sem, 16))
    a = c.dve(lambda e: e.bn_aggr(st[:NB, 6:8], st[:NB, 0:6]), a)
    a = c.ts(st[:NB, 8:9], st[:NB, 7:8], LN_EPS, None, ALU.add, None, a)
    a = c.power(st[:NB, 8:9], "mhalf", a)
    a = c.ts(last, last, st[:NB, 6:7], st[:NB, 8:9], ALU.subtract, ALU.mult, a)
    b = c.banks.next()
    c.transpose(b.t[:, 0:NB], last[:, 0:P], b.free, a)
    m = c.transpose(b.t[:V1, 64:64 + NB], last[:, P:DV])
    l1 = c.ts(lT[0], b.t[:, 0:NB], c.w("gx0"), c.w("bx0"), ALU.mult, ALU.add, m)
    l2 = c.ts(lT[1], b.t[:V1, 64:64 + NB], c.w("gx1"), c.w("bx1"), ALU.mult, ALU.add, m)
    b.free = [l1, l2]
    xn = Ring([Slot((c.tmp(2 * DV).rearrange("p (k d) -> p k d", k=2), c.tmp(24))) for _ in range(2)])
    xnT = Ring([Slot((c.tmp(2 * P), c.tmp(2 * P))) for _ in range(2)])
    k3 = Ring([Slot(c.tmp(3 * D)) for _ in range(2)])
    v3 = Ring([Slot(c.tmp(3 * D)) for _ in range(3)])
    sq = Slot((c.tmp(3 * D), c.tmp(3 * H)))
    kT = Ring([Slot(c.tmp(DC * KEYS).rearrange("p (k n) -> p k n", k=DC)) for _ in range(2)])
    probs = Ring([Slot(c.tmp(KEYS)) for _ in range(2)])
    stats = Ring([Slot((c.tmp(1), c.tmp(1))) for _ in range(2)])
    pts = Ring([Slot(c.tmp(3 * P)) for _ in range(2)])
    ot = Slot(c.tmp(DC * P).rearrange("p (k n) -> p k n", k=DC))
    for s in k3.slots:
        s.free = [c.pool(lambda e, s=s: e.memset(s.t, 0.0))]
    every, sums = c.banks, c.banks.slots[6:]
    c.banks = Ring(every.slots[:6])
    of = [{} for _ in range(NB)]

    def context_stats(s):
        of[s]["cx"], of[s]["got"] = cx, got = ctx.next()
        of[s]["xn"] = xs = xn.next()
        x, st = xs.t
        for i in range(2):
            src = cx.t[:, CK + i * (DV + 1):CK + i * (DV + 1) + DV]
            a = c.dve(lambda e, src=src, i=i: e.bn_stats(st[:, 6 * i:6 * i + 6], src), got, xs.free)
        for i in range(2):
            a = c.dve(lambda e, i=i: e.bn_aggr(st[:, 12 + 2 * i:14 + 2 * i], st[:, 6 * i:6 * i + 6]), a)
        rs = st[:, 16:18]
        a = c.ts(rs, st[:, 12:16].rearrange("p (k v) -> p k v", k=2)[:, :, 1], LN_EPS, None, ALU.add, None, a)
        of[s]["rstd"] = c.power(rs, "mhalf", a)

    def context_normal(s):
        cx, xs = of[s]["cx"], of[s]["xn"]
        x, st = xs.t
        for i in range(2):
            src = cx.t[:, CK + i * (DV + 1):CK + i * (DV + 1) + DV]
            nd = c.ts(x[:, i], src, st[:, 12 + 2 * i:13 + 2 * i], st[:, 16 + i:17 + i], ALU.subtract, ALU.mult,
                      of[s]["rstd"])
        cx.free = [nd]
        ctx.ask()
        of[s]["normal"] = nd

    def context_features(s):
        xs = of[s]["xn"]
        x, _ = xs.t
        b = c.banks.next()
        for i in range(2):
            c.transpose(b.t[:, i * P:(i + 1) * P], x[:, i, 0:P], b.free, of[s]["normal"])
            m = c.transpose(b.t[:V1, 256 + i * P:256 + (i + 1) * P], x[:, i, P:DV])
        xs.free = [m]
        of[s]["xt"] = xt = xnT.next()
        d1 = c.ts(xt.t[0], b.t[:, :256], c.w("gx0"), c.w("bx0"), ALU.mult, ALU.add, m, xt.free)
        d2 = c.ts(xt.t[1][:V1], b.t[:V1, 256:], c.w("gx1"), c.w("bx1"), ALU.mult, ALU.add, m, xt.free)
        b.free = [d1, d2]
        of[s]["xt_ok"] = [d1, d2]

    def keys_values(s):
        xt = of[s]["xt"]
        of[s]["k"], of[s]["v"] = ks, vs = k3.next(), v3.next()
        kd, vd = [], []
        for i in range(3):
            b = c.banks.next()
            if i < 2:
                n = P
                m = c.mm(b.t, [(xt.t[0][:, i * P:(i + 1) * P], c.w("wkv0")),
                               (xt.t[1][:V1, i * P:(i + 1) * P], c.w("wkv1"))], b.free, of[s]["xt_ok"])
            else:
                n = L3
                c.mm(b.t[:NS], [(lnT[:, k, s * NS:(s + 1) * NS], c.wc("wlkv", DC)[:, k]) for k in range(DC)],
                     b.free, lt)
                m = c.mm(b.t[NS:L3], [(lT[0][:, s:s + 1], c.w("wkv0")), (lT[1][:, s:s + 1], c.w("wkv1"))], l1, l2)
            e = c.act
            kd.append(c.copy(e, ks.t[:n, i * D:(i + 1) * D], b.t[:n, :D], m, ks.free))
            vd.append(c.copy(e, vs.t[:n, i * D:(i + 1) * D], b.t[:n, D:], m, vs.free))
            b.free = [kd[-1], vd[-1]]
        xt.free = [m]
        of[s]["squares"] = c.af(sq.t[0], ks.t, ACT.Square, kd, sq.free)
        of[s]["v_ok"] = vd

    def keys_normal(s):
        s2, nr = sq.t
        ks = of[s]["k"]
        a = c.reduce(nr, s2.rearrange("p (m d) -> p m d", d=DK), ALU.add, of[s]["squares"])
        of[s]["k_norm"] = rms(nr, a)

    def keys_scale(s):
        ks, a = of[s]["k"], of[s]["k_norm"]
        nr = sq.t[1]
        k4 = ks.t.rearrange("p (m d) -> p m d", d=DK)
        a = c.tt(k4, k4, each(nr, DK), ALU.mult, a)
        sq.free = [a]
        of[s]["k_ok"] = a

    def keys_features(s):
        ks = of[s]["k"]
        of[s]["kt"] = kt = kT.next()
        td = []
        for k in range(DC):
            b = c.banks.next()
            for i, n in enumerate((P, P, L3)):
                m = c.transpose(b.t[:, i * P:i * P + n], ks.t[:n, i * D + k * P:i * D + (k + 1) * P], b.free,
                                of[s]["k_ok"])
            d = c.copy((c.act, c.dve)[k], kt.t[:, k], b.t[:, :KEYS], m, kt.free)
            b.free = [d]
            td.append(d)
        ks.free = [m]
        of[s]["kt_ok"] = td

    def scores(s):
        kt = of[s]["kt"]
        b, st = c.banks.next(), stats.next()
        of[s]["p"] = p = probs.next()
        q4 = qbd.rearrange("p (k b m) -> p k b m", k=DC, b=NB)
        m = c.mm(b.t[:, :KEYS], [(pick(c, s), mask)] + [(q4[:, k, s], kt.t[:, k]) for k in range(DC)],
                 b.free, bd, of[s]["kt_ok"], mask_ok)
        kt.free = [m]
        of[s]["sums"], of[s]["exp"] = st, exp_keys(c, b, KEYS, p, st, m)

    def weights_to_keys(s):
        p = of[s]["p"]
        of[s]["pt"] = pt = pts.next()
        b = c.banks.next()
        for k, n in enumerate((P, P, L3)):
            m = c.transpose(b.t[:n, k * P:(k + 1) * P], p.t[:, k * P:k * P + n], b.free, of[s]["p_ok"])
        p.free = [m]
        d1 = c.copy(c.act, pt.t[:, :2 * P], b.t[:, :2 * P], m, pt.free)
        d2 = c.copy(c.act, pt.t[:L3, 2 * P:], b.t[:L3, 2 * P:3 * P], m, pt.free)
        b.free = [d1, d2]
        of[s]["pt_ok"] = [d1, d2]

    def products(s):
        t, i = divmod(s, BT)
        pt, vs = of[s]["pt"], of[s]["v"]
        for k in range(DC):
            ob = sums[k]
            m = c.mm(ob.t[:, i * 2 * NS:(i + 1) * 2 * NS],
                     [(vs.t[:n, j * D + k * P:j * D + (k + 1) * P],
                       pt.t[:n, j * P + k * 2 * NS:j * P + (k + 1) * 2 * NS]) for j, n in enumerate((P, P, L3))],
                     ob.free, of[s]["pt_ok"], of[s]["v_ok"])
        vs.free = pt.free = [m]
        if i == BT - 1:
            od = []
            for k in range(DC):
                ob = sums[k]
                for odd in range(2):
                    r = slice(odd * DK, odd * DK + DK)
                    od.append(c.copy(c.dve, ot.t[r, k].rearrange("p (s q) -> p s q", s=BT),
                                     ob.t[r, :BT * 2 * NS].rearrange("p (s h q) -> p h s q", s=BT, h=2)[:, odd],
                                     m, ot.free))
                ob.free = od[-2:]
            c.add_output(ot.t, c.wc("wo", DC), DC, od, c.w("bo"), tiles=[t], cols=slice(0, P))
            ot.free = [c.pe.now()]

    for i in range(NB + 3):
        if i < NB:
            context_stats(i)
        if 2 <= i < NB + 2:
            keys_scale(i - 2)
        if i >= 3:
            of[i - 3]["p_ok"] = divide_keys(c, KEYS, of[i - 3]["p"], of[i - 3]["sums"], of[i - 3]["exp"], c.dve)
        if 1 <= i <= NB:
            keys_values(i - 1)
        if i >= 3:
            weights_to_keys(i - 3)
        if i < NB:
            context_normal(i)
            context_features(i)
        if 2 <= i < NB + 2:
            keys_features(i - 2)
        if i >= 3:
            products(i - 3)
        if 1 <= i <= NB:
            keys_normal(i - 1)
        if 2 <= i < NB + 2:
            scores(i - 2)
    c.banks = every


def l1_xattn(c):
    H, DH, TOP = 4, 32, 32
    TAPS = 11
    TAKEN = -3.0e38
    ready, xt = c.enter()
    ct3 = c.tmp(DC * NT).rearrange("p (k n) -> p k n", k=DC)
    mark = c.used
    mask, mask_ok = mask_rows(c, "keep1", G, 0, G - 1, "keep1_loaded")
    sem = c.new_sem("query_mask_loaded")
    packed = c.tmp(NB // 4).bitcast(U32)
    qraw = packed.bitcast(U8)
    qmask = c.tmp(NB)
    c.sp.silent(lambda e: e.dma_start(packed, c.dram["qmask"]).then_inc(sem, 16))
    qm = c.copy(c.dve, qmask, qraw, (sem, 16))
    q3 = c.tmp(NT)
    qd = []
    for h in range(2):
        b = c.banks.next()
        m = c.mm(b.t, [(c.wc("wq", DC)[:, k], c.XT[:, k, h * HALF:(h + 1) * HALF]) for k in range(DC)], b.free, xt)
        d = c.ts(q3[:, h * HALF:(h + 1) * HALF], b.t, DH ** -0.5, None, ALU.mult, None, m)
        b.free = [d]
        qd.append(d)
    wk = c.w("wk0").rearrange("p (h f) -> p h f", h=H)
    ctx = Context(c, 5)
    qslots = Ring([Slot((c.tmp(BT * P).rearrange("p (s h q) -> p s h q", s=BT, h=H),
                         c.tmp(BT * P).rearrange("p (s h q) -> p s h q", s=BT, h=H))) for _ in range(2)])
    works = Ring([Slot((c.tmp(G), c.tmp(8), c.tmp(1), c.tmp(1))) for _ in range(4)])
    probs = Ring([Slot(c.tmp(G)) for _ in range(4)])
    pts = Ring([Slot(c.tmp(3 * P)) for _ in range(2)])
    pc = Slot((c.tmp(H * P).rearrange("p (h n) -> p h n", h=H), c.tmp(H * P).rearrange("p (h n) -> p h n", h=H)))
    state, turned = {}, {}
    ctd = []

    def turn(t):
        slot = qslots.next()
        turned[t] = slot, head_queries(c, lambda h: wk[:, h], H, DV, lambda h: q3, slice(t * P, (t + 1) * P),
                                       None, qd, slot)

    def scores(s):
        t, i = divmod(s, BT)
        slot, hd = turned[t]
        qa, qb = slot.t
        cx, got = ctx.next()
        b, w, p = c.banks.next(), works.next(), probs.next()
        work, top, nmax, total = w.t
        m = c.mm(b.t[:, :G], [(pick(c, s), mask), (qa[:, i].rearrange("p h q -> p (h q)"), cx.t[:, CT0:CT0 + G]),
                              (qb[:V1, i].rearrange("p h q -> p (h q)"), cx.t[:V1, CT1:CT1 + G])],
                 b.free, hd, got, mask_ok)
        slot.free = [m]
        a = c.copy(c.act, work, b.t[:, :G], m, w.free)
        for r in range(TOP // 8):
            x = c.dve(lambda e: e.max(top, work), a)
            if r == 0:
                n = c.ts(nmax, top[:, 0:1], -1.0, None, ALU.mult, None, x)
            a = c.dve(lambda e: e.match_replace(work, top, work, TAKEN), x, n)
        x = c.af(p.t, b.t[:, :G], ACT.Exp, n, p.free, bias=nmax)
        b.free = [x]
        a = c.dve(lambda e: e.scalar_tensor_tensor(out=p.t, in0=work, scalar=TAKEN, in1=p.t, op0=ALU.is_equal,
                                                   op1=ALU.mult, accum_out=total), a, x)
        a = c.recip(total, a)
        a = c.tt(total, total, qmask[:, s:s + 1], ALU.mult, a, qm)
        a = c.ts(p.t, p.t, total, None, ALU.mult, None, a, q=c.pool)
        w.free = [a]
        return cx, p, a

    of = [None] * NB

    def weights_to_keys(s):
        cx, p, pd = of[s]
        pt = pts.next()
        b = c.banks.next()
        for k, n in enumerate((P, P, 1)):
            m = c.transpose(b.t[:n, k * P:(k + 1) * P], p.t[:, k * P:k * P + n], b.free, pd)
        p.free = [m]
        d1 = c.copy(c.act, pt.t[:, :2 * P], b.t[:, :2 * P], m, pt.free)
        d2 = c.copy(c.act, pt.t[:1, 2 * P:], b.t[:1, 2 * P:3 * P], m, pt.free)
        b.free = [d1, d2]
        of[s] = cx, pt, d1, d2

    def products(s):
        t, i = divmod(s, BT)
        cx, pt, d1, d2 = of[s]
        b = c.banks.next()
        for j, rows, f0 in ((0, P, 0), (1, V1, P)):
            m = c.mm(b.t[:rows, j * P:(j + 1) * P],
                     [(cx.t[:n, CK + k * (DV + 1) + f0:CK + k * (DV + 1) + f0 + rows], pt.t[:n, k * P:(k + 1) * P])
                      for k, n in enumerate((P, P, 1))], b.free, d1, d2)
        for j, rows in ((0, P), (1, V1)):
            d = c.copy(c.act, pc.t[j][:rows, :, i * NS:(i + 1) * NS],
                       b.t[:rows, j * P:(j + 1) * P].rearrange("p (h q) -> p h q", h=H), m, pc.free)
            state.setdefault("pc", []).append(d)
        b.free = [d]
        pt.free = cx.free = [m]
        ctx.ask()
        if i == BT - 1:
            pr = state.pop("pc")
            b = c.banks.next()
            for o in range(DC):
                oc = slice(o * P, (o + 1) * P)
                m = c.mm(b.t[:, oc], [x for h in range(H) for x in ((c.w("wv0")[:, oc], pc.t[0][:, h]),
                                                                  (c.w("wv1")[:, oc], pc.t[1][:V1, h]))], b.free, pr)
            pc.free = [m]
            d = c.af(ct3[:, :, t * P:(t + 1) * P], b.t[:, :D].rearrange("p (k n) -> p k n", k=DC), ACT.Copy, m,
                     scale=1.0 / H)
            b.free = [d]
            ctd.append(d)

    turn(0)
    for s in range(NB + 3):
        if s < NB:
            of[s] = scores(s)
        if s % BT == 2 and s // BT + 1 < TILES:
            turn(s // BT + 1)
        if 2 <= s < NB + 2:
            weights_to_keys(s - 2)
        if s >= 3:
            products(s - 3)

    c.fence()
    c.used = mark
    if c.kern_ok is None:
        s4d_kernel(c, c.w, c.tmp, None)
        c.fence()
        c.used = mark
    kern, kern_ok = c.kern, c.kern_ok
    mg = c.w("mg")
    flat = lambda a: a.rearrange("p k n -> p (k n)")
    film = c.tmp(2 * DC * NT).rearrange("p (k n) -> p k n", k=2 * DC)
    x3, y3 = (c.tmp(DC * NT).rearrange("p (k n) -> p k n", k=DC) for _ in range(2))
    tok = c.tmp(TILES * D).rearrange("p (t d) -> p t d", t=TILES)

    def modulate(v, w, bias, ready, free):
        f = c.project(film, c.wc(w, DC), DC, ct3, 2 * DC, [ctd, free], bias=c.w(bias))
        a = c.ts(flat(film[:, :DC]), flat(film[:, :DC]), mg, 1.0, ALU.mult, ALU.add, f)
        b = c.ts(flat(film[:, DC:]), flat(film[:, DC:]), mg, None, ALU.mult, None, f, q=c.pool)
        a = c.tt(flat(v), flat(v), flat(film[:, :DC]), ALU.mult, a, ready)
        return c.tt(flat(v), flat(v), flat(film[:, DC:]), ALU.add, a, b)

    diag = c.tmp(DC * (NS - TAPS) * P).rearrange("p (k j m) -> p k j m", k=DC, j=NS - TAPS)
    diag_ok = [[], []]
    for k in range(DC):
        for j in range(TAPS, NS):
            o, tap = diag[:, k, j - TAPS], kern[:, k, j:j + 1]
            diag_ok[k] = [c.af(o, c.const("eye"), ACT.Copy, kern_ok, scale=tap)]
    n = c.normalise(c.XN, tok, ready)
    f = c.to_features(tok, x3, n, c.w("gi"), c.w("bi"))
    a = modulate(x3, "fi", "bfi", f, None)
    first = c.tmp(DC)
    k0 = c.tt(first, kern[:, :, 0], c.w("dskip"), ALU.add, kern_ok)
    yd, late = [], []
    seqs = lambda v: v.rearrange("p (b s) -> p b s", s=NS)
    for k in range(DC):
        for h in range(2):
            b = c.banks.next()
            c.pe.wait(b.free, diag_ok[k], a)
            for j in range(TAPS, NS):
                f = lambda e, k=k, h=h, j=j, b=b: e.matmul(
                    seqs(b.t)[:, :, j:], lhsT=diag[:, k, j - TAPS],
                    rhs=seqs(x3[:, k, h * HALF:(h + 1) * HALF])[:, :, :NS - j], start=j == TAPS, stop=j == NS - 1)
                m = c.pe(f) if j == NS - 1 else c.pe.silent(f)
            late.append((k, h, b, m))
    for k in range(DC):
        d = c.ts(y3[:, k], x3[:, k], first[:, k:k + 1], None, ALU.mult, None, k0, a)
        for j in range(1, TAPS):
            src = x3[:, k].rearrange("p (b s) -> p b s", s=NS)[:, :, :NS - j]
            dst = y3[:, k].rearrange("p (b s) -> p b s", s=NS)[:, :, j:]
            d = c.stt(dst, src, kern[:, k, j:j + 1], dst, ALU.mult, ALU.add, d)
    for k, h, b, m in late:
        dst = seqs(y3[:, k, h * HALF:(h + 1) * HALF])[:, :, TAPS:]
        b.free = [c.tt(dst, dst, seqs(b.t)[:, :, TAPS:], ALU.add, m, d)]
        yd.append(b.free[0])
    a = modulate(y3, "fo", "bfo", yd, yd)
    back = to_tokens(c, y3, tok, [a] * DC)
    r = [c.tt(tok[:, t], tok[:, t], c.XN[:, t], ALU.add, back) for t in range(TILES)]
    hn = c.normalise(tok, c.XN, [r, n])
    h3 = c.XT
    f = c.to_features(c.XN, h3, hn, c.w("gf"), c.w("bf"))
    c.fence()
    c.used = mark
    tok2 = tok
    HC = 8
    hid = c.tmp(HC * NT).rearrange("p (k n) -> p k n", k=HC)
    hd = c.project(hid, c.wc("w1", DC), DC, h3, HC, f, bias=c.w("b1"), func=ACT.Gelu)
    od = []
    for t in range(TILES):
        b = c.banks.next()
        m = c.mm(b.t[:, :D], [(hid[:, k, t * P:(t + 1) * P], c.wc("w2", HC)[:, k]) for k in range(HC)]
                 + [(c.const("ones")[0:1, :P], c.w("b2"))], b.free, hd)
        d = c.tt(tok2[:, t], b.t[:, :D], tok2[:, t], ALU.add, m)
        b.free = [d]
        od.append(d)
    n = c.normalise(tok2, c.XN, od)
    for t in range(TILES):
        a = c.tt(c.XN[:, t], c.XN[:, t], c.w("go"), ALU.mult, n[t])
        a = c.tt(c.XN[:, t], c.XN[:, t], c.w("bo"), ALU.add, a)
        c.tt(c.X[:, t], c.X[:, t], c.XN[:, t], ALU.add, a)


def s4d_kernel(c, w_of, tmp, ready):
    N = 64
    kern = c.kern
    n2 = lambda: tmp(DC * N)
    dt = tmp(DC)
    a0 = c.af(dt, w_of("logdt"), ACT.Exp, ready)
    a, w = n2(), n2()
    k3 = lambda x: x.rearrange("p (k n) -> p k n", k=DC)
    r1 = c.tt(k3(a), k3(w_of("are")), each(dt, N), ALU.mult, a0)
    r2 = c.tt(k3(w), k3(w_of("aim")), each(dt, N), ALU.mult, a0)
    th, em1, ea, sw, cw, sh, t1 = (n2() for _ in range(7))
    r = c.af(th, a, ACT.Tanh, r1, scale=0.5)
    x = c.ts(t1, th, -1.0, 1.0, ALU.mult, ALU.add, r)
    x = c.recip(t1, x)
    x = c.stt(em1, th, 2.0, t1, ALU.mult, ALU.mult, x)
    e = c.ts(ea, em1, 1.0, None, ALU.add, None, x)
    s = phase_sin(c, sw, w, t1, 0.0, [x, e, r2])
    s = phase_sin(c, cw, w, t1, np.pi / 2, s)
    h = c.ts(th, w, 0.5, None, ALU.mult, None, s)
    s = phase_sin(c, sh, th, t1, 0.0, h)
    x = c.tt(em1, em1, cw, ALU.mult, s)
    y = c.tt(sh, sh, sh, ALU.mult, x)
    x = c.stt(em1, sh, -2.0, em1, ALU.mult, ALU.add, y)
    y = c.tt(sw, sw, ea, ALU.mult, x)
    cr, ci, ar, ai = w_of("cre"), w_of("cim"), w_of("are"), w_of("aim")
    nr, ni, dr, di, den = th, ea, cw, sh, n2()
    x = c.tt(nr, em1, cr, ALU.mult, y)
    y = c.tt(t1, sw, ci, ALU.mult, y)
    x = c.tt(nr, nr, t1, ALU.subtract, x, y)
    y = c.tt(ni, em1, ci, ALU.mult, x)
    z = c.tt(t1, sw, cr, ALU.mult, x)
    y = c.tt(ni, ni, t1, ALU.add, y, z)
    x = c.tt(den, ar, ar, ALU.mult, y)
    z = c.tt(t1, ai, ai, ALU.mult, y)
    x = c.tt(den, den, t1, ALU.add, x, z)
    x = c.recip(den, x)
    x = c.ts(den, den, 2.0, None, ALU.mult, None, x)
    x = c.tt(dr, nr, ar, ALU.mult, x)
    z = c.tt(t1, ni, ai, ALU.mult, x)
    x = c.tt(dr, dr, t1, ALU.add, z)
    x = c.tt(di, ni, ar, ALU.mult, x)
    z = c.tt(t1, nr, ai, ALU.mult, x)
    x = c.tt(di, di, t1, ALU.subtract, z)
    x = c.tt(dr, dr, den, ALU.mult, x)
    x = c.tt(di, di, den, ALU.mult, x)
    NQ = 8
    mag, s_, t_, u_, wl = (tmp(NQ * NS) for _ in range(5))
    part = tmp(NS)
    v = lambda q: q.rearrange("p (n l) -> p n l", n=NQ)
    for k in range(DC):
        for n0 in range(0, N, NQ):
            ak, wk, drk, dik = (q[:, k * N + n0:k * N + n0 + NQ] for q in (a, w, dr, di))
            y = c.tt(v(mag), each(ak, NS), rows_of(c.const("pos"), NQ), ALU.mult, x)
            y = c.af(mag, mag, ACT.Exp, y)
            z = c.tt(v(wl), each(wk, NS), rows_of(c.const("pos"), NQ), ALU.mult, x)
            z = phase_sin(c, s_, wl, t_, np.pi / 2, z)
            z = c.tt(v(s_), v(s_), each(drk, NS), ALU.mult, z)
            z2 = phase_sin(c, t_, wl, u_, 0.0, z)
            z2 = c.tt(v(t_), v(t_), each(dik, NS), ALU.mult, z2)
            z = c.tt(s_, s_, t_, ALU.subtract, z2)
            z = c.tt(s_, s_, mag, ALU.mult, z, y)
            dst = part if n0 else kern[:, k]
            x = c.reduce(dst, s_.rearrange("p (n l) -> p l n", n=NQ), ALU.add, z)
            if n0:
                x = c.tt(kern[:, k], kern[:, k], part, ALU.add, x)
    c.kern_ok = x



BLOCKS = [("L0_xattn", l0_xattn), ("L0_attn", l0_attn), ("L0_ffn", l0_ffn), ("L1_xattn", l1_xattn),
          ("L1_attn", l1_attn), ("L1_ffn", l1_ffn), ("L2_xattn", l2_xattn), ("L2_attn", l2_attn),
          ("L2_ffn", l2_ffn), ("L3_xattn", l3_xattn), ("L3_attn", l3_attn), ("L3_ffn", l3_ffn)]


def build(nc, dram, out, at, only=None):
    todo = [BLOCKS[i] for i in only] if only is not None else BLOCKS
    with ExitStack() as ctx:
        c = Core(nc, ctx, dram, at)
        x_in, x_out = c.new_sem("x_and_consts_loaded"), c.new_sem("x_stored")
        c.sp.silent(lambda e: e.dma_start(c.X, dram["x"]).then_inc(x_in, 16))
        c.sp.silent(lambda e: e.dma_start(c.consts, dram["w_const"]).then_inc(x_in, 16))
        for q in (c.pe, c.dve, c.act, c.pool):
            q.wait((x_in, 32))
        for i, (name, body) in enumerate(todo):
            c.begin(name, todo[i + 1][0] if i + 1 < len(todo) else None)
            body(c)
            c.end()
        c.sp.wait(c.ends[-1])
        c.sp.silent(lambda e: e.dma_start(out, c.X).then_inc(x_out, 16))
        c.sp.wait((x_out, 16))

        block = ctx.enter_context(nc.Block())

        @block.sync
        def _(e):
            for op in c.sp.ops:
                op(e)

        @block.tensor
        def _(e):
            for op in c.pe.ops:
                op(e)

        @block.vector
        def _(e):
            for op in c.dve.ops:
                op(e)

        @block.scalar
        def _(e):
            for op in c.act.ops:
                op(e)

        @block.gpsimd
        def _(e):
            for op in c.pool.ops:
                op(e)


def kernel(**inputs):
    import concourse.bacc as _bacc
    from concourse.bass_utils import run_bass_kernel_spmd as _run

    at, arrays = host_layout(inputs)
    nc = _bacc.Bacc("TRN2", target_bir_lowering=False, num_devices=1)
    dram = {}
    for name, a in arrays.items():
        dram[name] = nc.dram_tensor(f"in_{name}", a.shape, mybir.dt.from_np(a.dtype), kind="ExternalInput").ap()
    out = nc.dram_tensor("out_x", (P, TILES, D), F32, kind="ExternalOutput").ap()
    build(nc, dram, out, at)
    r = _run(nc, [{f"in_{n}": a for n, a in arrays.items()}], core_ids=[0])
    x = r.results[0]["out_x"]
    return x.reshape(P, TILES, D).transpose(1, 0, 2).reshape(NB, NS, D)
```
